# Optimizing a Trainium2 kernel written in Bass

```python
import numpy as np
import jax
import jax.numpy as jnp

def _softmax(x, axis=-1):
    return jax.nn.softmax(x, axis=axis)

def _gelu(x):
    return jax.nn.gelu(x, approximate=True)

def _silu(x):
    return jax.nn.silu(x)

def _sigmoid(x):
    return jax.nn.sigmoid(x)

def _layernorm(x, axis=-1, eps=1e-05):
    m = jnp.mean(x, axis=axis, keepdims=True)
    v = jnp.var(x, axis=axis, keepdims=True)
    return (x - m) / jnp.sqrt(v + eps)

def _scatter_add(tgt, idx, src, axis=0):
    return tgt.at[idx].add(src)

def _segment_sum(src, seg, n):
    return jax.ops.segment_sum(src, seg, n)
kernel_name = 'mk_seq_preln_d4_jaxref_r8_e3f565'

def setup_inputs(seed: int=0):
    np.random.seed(seed)
    _w = jnp.asarray

    def _L0_attn_setup():
        import jax, jax.numpy as jnp
        import numpy as np
        D_MODEL = 128
        B, T = (4, 512)
        LN_EPS = 1e-05
        DEN_EPS = 1e-06
        key = jax.random.key(seed)
        ks = jax.random.split(key, 10)
        s = 1.0 / np.sqrt(D_MODEL)
        return {'x': jax.random.normal(ks[0], (B, T, D_MODEL), dtype=jnp.float32), 'w_qkv': jax.random.normal(ks[1], (D_MODEL, 3 * D_MODEL), dtype=jnp.float32) * s, 'b_qkv': jnp.zeros((3 * D_MODEL,), dtype=jnp.float32), 'w_gate': jax.random.normal(ks[2], (D_MODEL, D_MODEL), dtype=jnp.float32) * s, 'b_gate': jnp.zeros((D_MODEL,), dtype=jnp.float32), 'w_proj': jax.random.normal(ks[3], (D_MODEL, D_MODEL), dtype=jnp.float32) * s, 'b_proj': jnp.zeros((D_MODEL,), dtype=jnp.float32), 'ln_g': jnp.ones((D_MODEL,), dtype=jnp.float32), 'ln_b': jnp.zeros((D_MODEL,), dtype=jnp.float32)}
    _L0_attn_in = _L0_attn_setup()

    def _L0_ffn_setup():
        import jax, jax.numpy as jnp
        import numpy as np
        BLOCK = 16
        _GRID = jnp.array([0.0, 0.5, 1.0, 1.5, 2.0, 3.0, 4.0, 6.0], dtype=jnp.float32)
        _MID = jnp.array([0.25, 0.75, 1.25, 1.75, 2.5, 3.5, 5.0], dtype=jnp.float32)

        def fp4_quant_dequant(x):
            shape = x.shape
            xb = x.reshape(shape[:-1] + (shape[-1] // BLOCK, BLOCK))
            scale = jnp.max(jnp.abs(xb), axis=-1, keepdims=True) / 6.0
            scale = jnp.maximum(scale, jnp.float32(1e-12))
            xn = xb / scale
            idx = jnp.searchsorted(_MID, jnp.abs(xn))
            q = _GRID[idx] * jnp.sign(xn) * scale
            return q.reshape(shape)

        def fp4_linear(x, w):
            xq = fp4_quant_dequant(x)
            wq = fp4_quant_dequant(w)
            return jnp.einsum('bsk,nk->bsn', xq, wq)
        key = jax.random.key(seed)
        k1, k2, k3, k4 = jax.random.split(key, 4)
        H, I = (128, 352)
        x = jax.random.normal(k1, (4, 512, H), dtype=jnp.float32)
        w_gate = jax.random.normal(k2, (I, H), dtype=jnp.float32) * 0.02
        w_up = jax.random.normal(k3, (I, H), dtype=jnp.float32) * 0.02
        w_down = jax.random.normal(k4, (H, I), dtype=jnp.float32) * 0.02
        return {'x': x, 'w_gate': w_gate, 'w_up': w_up, 'w_down': w_down}
    _L0_ffn_in = _L0_ffn_setup()

    def _L1_attn_setup():
        import jax, jax.numpy as jnp
        import numpy as np
        RSQRT2 = 2 ** (-0.5)
        B, S, D_IN = (2, 512, 128)
        H, D_HEAD = (8, 64)
        QK_DIM = H * D_HEAD
        V_DIM = H * D_HEAD
        OUT_DIM = D_IN
        LN_EPS = 1e-05

        def _layernorm(y, gamma, beta):
            mu = jnp.mean(y, axis=-1, keepdims=True)
            var = jnp.mean(jnp.square(y - mu), axis=-1, keepdims=True)
            return (y - mu) * jax.lax.rsqrt(var + LN_EPS) * gamma + beta
        key = jax.random.key(seed)
        ks = jax.random.split(key, 8)

        def lecun(k, fan_in, shape):
            return jax.random.normal(k, shape, dtype=jnp.float32) * (1.0 / np.sqrt(fan_in))
        return {'x': jax.random.normal(ks[0], (B, S, D_IN), dtype=jnp.float32), 'W_qk': lecun(ks[1], D_IN, (D_IN, 2 * QK_DIM)), 'b_qk': jnp.zeros((2 * QK_DIM,), jnp.float32), 'W_v': lecun(ks[2], D_IN, (D_IN, V_DIM)), 'b_v': jnp.zeros((V_DIM,), jnp.float32), 'W_out': lecun(ks[3], V_DIM, (V_DIM, OUT_DIM)), 'b_out': jnp.zeros((OUT_DIM,), jnp.float32), 'ln_gamma': jnp.ones((OUT_DIM,), jnp.float32), 'ln_beta': jnp.zeros((OUT_DIM,), jnp.float32)}
    _L1_attn_in = _L1_attn_setup()

    def _L1_ffn_setup():
        import jax, jax.numpy as jnp
        import numpy as np
        S, B, D = (128, 2, 128)
        E, TOPK = (15, 3)
        F = 128
        FS = 256

        def _uinit(k, shape, out_dim):
            std = out_dim ** (-0.5)
            return jax.random.uniform(k, shape, jnp.float32, -std, std)
        key = jax.random.key(seed)
        ks = jax.random.split(key, 10)
        return {'x': jax.random.normal(ks[0], (S, B, D), jnp.float32), 'gate_w': jax.random.normal(ks[1], (E, D), jnp.float32) * D ** (-0.5), 'fc1_w': _uinit(ks[2], (E, 2 * F, D), 2 * F), 'fc1_b': _uinit(ks[3], (E, 2 * F), 2 * F), 'geglu_mult': jnp.ones((E, F), jnp.float32), 'fc2_w': _uinit(ks[4], (E, D, F), D), 'fc2_b': _uinit(ks[5], (E, D), D), 's_fc1_w': _uinit(ks[6], (2 * FS, D), 2 * FS), 's_fc1_b': _uinit(ks[7], (2 * FS,), 2 * FS), 's_geglu_mult': jnp.ones((FS,), jnp.float32), 's_fc2_w': _uinit(ks[8], (D, FS), D), 's_fc2_b': _uinit(ks[9], (D,), D)}
    _L1_ffn_in = _L1_ffn_setup()

    def _L2_attn_setup():
        import jax, jax.numpy as jnp
        import numpy as np
        B, S, HID, NH, BS = (1, 256, 128, 16, 64)
        D = HID // NH
        THRESH = 0.01
        SCALE = D ** (-0.5)
        key = jax.random.key(seed)
        ks = jax.random.split(key, 5)
        wscale = 1.0 / np.sqrt(HID)
        x = jax.random.normal(ks[0], (B, S, HID), dtype=jnp.float32)
        wq = jax.random.normal(ks[1], (HID, HID), dtype=jnp.float32) * wscale
        wk = jax.random.normal(ks[2], (HID, HID), dtype=jnp.float32) * wscale
        wv = jax.random.normal(ks[3], (HID, HID), dtype=jnp.float32) * wscale
        wo = jax.random.normal(ks[4], (HID, HID), dtype=jnp.float32) * wscale
        return {'x': x, 'wq': wq, 'wk': wk, 'wv': wv, 'wo': wo}
    _L2_attn_in = _L2_attn_setup()

    def _L2_ffn_setup():
        import jax, jax.numpy as jnp
        import numpy as np
        EPS = 1e-05

        def _quantize(W):
            gamma = jnp.mean(jnp.abs(W))
            return jnp.clip(jnp.round(W / (gamma + EPS)), -1.0, 1.0)
        key = jax.random.key(seed)
        k_x, k_w1, k_b1, k_w2, k_b2 = jax.random.split(key, 5)
        n_embd = 128
        d_ff = 4 * n_embd
        B, S = (4, 512)
        bound1 = 1.0 / np.sqrt(n_embd)
        bound2 = 1.0 / np.sqrt(d_ff)
        x = jax.random.normal(k_x, (B, S, n_embd), dtype=jnp.float32)
        W1 = jax.random.uniform(k_w1, (d_ff, n_embd), jnp.float32, -bound1, bound1)
        b1 = jax.random.uniform(k_b1, (d_ff,), jnp.float32, -bound1, bound1)
        W2 = jax.random.uniform(k_w2, (n_embd, d_ff), jnp.float32, -bound2, bound2)
        b2 = jax.random.uniform(k_b2, (n_embd,), jnp.float32, -bound2, bound2)
        return {'x': x, 'W1': W1, 'b1': b1, 'W2': W2, 'b2': b2}
    _L2_ffn_in = _L2_ffn_setup()

    def _L3_attn_setup():
        import jax, jax.numpy as jnp
        import numpy as np
        N_HEAD = 16
        NEG_BIG = -10000000000.0

        def _rope_cos_sin(T, head_dim):
            t = jnp.arange(T, dtype=jnp.float32)[:, None]
            i = jnp.arange(head_dim // 2, dtype=jnp.float32)
            theta = jnp.power(10000.0, 2.0 * i / head_dim)
            ang = t * theta[None, :]
            return (jnp.cos(ang), jnp.sin(ang))

        def _apply_rope(x, cos, sin):
            B, H, T, D = x.shape
            xr = x.reshape(B, H, T, D // 2, 2)
            x0, x1 = (xr[..., 0], xr[..., 1])
            c = cos[None, None, :, :]
            s = sin[None, None, :, :]
            o0 = x0 * c - x1 * s
            o1 = x0 * s + x1 * c
            return jnp.stack([o0, o1], axis=-1).reshape(B, H, T, D)
        key = jax.random.key(seed)
        ks = jax.random.split(key, 9)
        B, T, C = (2, 256, 128)
        sc = 1.0 / np.sqrt(C)
        return {'x': jax.random.normal(ks[0], (B, T, C), jnp.float32), 'Wq': jax.random.normal(ks[1], (C, C), jnp.float32) * sc, 'bq': jax.random.normal(ks[2], (C,), jnp.float32) * 0.01, 'Wk': jax.random.normal(ks[3], (C, C), jnp.float32) * sc, 'bk': jax.random.normal(ks[4], (C,), jnp.float32) * 0.01, 'Wv': jax.random.normal(ks[5], (C, C), jnp.float32) * sc, 'bv': jax.random.normal(ks[6], (C,), jnp.float32) * 0.01, 'Wp': jax.random.normal(ks[7], (C, C), jnp.float32) * sc, 'bp': jax.random.normal(ks[8], (C,), jnp.float32) * 0.01}
    _L3_attn_in = _L3_attn_setup()

    def _L3_ffn_setup():
        import jax, jax.numpy as jnp
        import numpy as np
        NUM_EXPERTS = 8
        TOP_K = 2
        key = jax.random.key(seed)
        ks = jax.random.split(key, 5)
        B, L, E, H, N = (2, 256, 128, 256, NUM_EXPERTS)
        return {'x': jax.random.normal(ks[0], (B, L, E), dtype=jnp.float32), 'gate_kernel': jax.random.normal(ks[1], (E, N), dtype=jnp.float32) / np.sqrt(E), 'w0_kernel': jax.random.normal(ks[2], (N, E, H), dtype=jnp.float32) / np.sqrt(E), 'w1_kernel': jax.random.normal(ks[3], (N, E, H), dtype=jnp.float32) / np.sqrt(E), 'wo_kernel': jax.random.normal(ks[4], (N, H, E), dtype=jnp.float32) / np.sqrt(H)}
    _L3_ffn_in = _L3_ffn_setup()
    _d = {'L0_attn_x': _L0_attn_in['x'], 'L0_attn_w_qkv': _L0_attn_in['w_qkv'], 'L0_attn_b_qkv': _L0_attn_in['b_qkv'], 'L0_attn_w_gate': _L0_attn_in['w_gate'], 'L0_attn_b_gate': _L0_attn_in['b_gate'], 'L0_attn_w_proj': _L0_attn_in['w_proj'], 'L0_attn_b_proj': _L0_attn_in['b_proj'], 'L0_attn_ln_g': _L0_attn_in['ln_g'], 'L0_attn_ln_b': _L0_attn_in['ln_b'], 'L0_ffn_w_gate': _L0_ffn_in['w_gate'], 'L0_ffn_w_up': _L0_ffn_in['w_up'], 'L0_ffn_w_down': _L0_ffn_in['w_down'], 'L1_attn_W_qk': _L1_attn_in['W_qk'], 'L1_attn_b_qk': _L1_attn_in['b_qk'], 'L1_attn_W_v': _L1_attn_in['W_v'], 'L1_attn_b_v': _L1_attn_in['b_v'], 'L1_attn_W_out': _L1_attn_in['W_out'], 'L1_attn_b_out': _L1_attn_in['b_out'], 'L1_attn_ln_gamma': _L1_attn_in['ln_gamma'], 'L1_attn_ln_beta': _L1_attn_in['ln_beta'], 'L1_ffn_gate_w': _L1_ffn_in['gate_w'], 'L1_ffn_fc1_w': _L1_ffn_in['fc1_w'], 'L1_ffn_fc1_b': _L1_ffn_in['fc1_b'], 'L1_ffn_geglu_mult': _L1_ffn_in['geglu_mult'], 'L1_ffn_fc2_w': _L1_ffn_in['fc2_w'], 'L1_ffn_fc2_b': _L1_ffn_in['fc2_b'], 'L1_ffn_s_fc1_w': _L1_ffn_in['s_fc1_w'], 'L1_ffn_s_fc1_b': _L1_ffn_in['s_fc1_b'], 'L1_ffn_s_geglu_mult': _L1_ffn_in['s_geglu_mult'], 'L1_ffn_s_fc2_w': _L1_ffn_in['s_fc2_w'], 'L1_ffn_s_fc2_b': _L1_ffn_in['s_fc2_b'], 'L2_attn_wq': _L2_attn_in['wq'], 'L2_attn_wk': _L2_attn_in['wk'], 'L2_attn_wv': _L2_attn_in['wv'], 'L2_attn_wo': _L2_attn_in['wo'], 'L2_ffn_W1': _L2_ffn_in['W1'], 'L2_ffn_b1': _L2_ffn_in['b1'], 'L2_ffn_W2': _L2_ffn_in['W2'], 'L2_ffn_b2': _L2_ffn_in['b2'], 'L3_attn_Wq': _L3_attn_in['Wq'], 'L3_attn_bq': _L3_attn_in['bq'], 'L3_attn_Wk': _L3_attn_in['Wk'], 'L3_attn_bk': _L3_attn_in['bk'], 'L3_attn_Wv': _L3_attn_in['Wv'], 'L3_attn_bv': _L3_attn_in['bv'], 'L3_attn_Wp': _L3_attn_in['Wp'], 'L3_attn_bp': _L3_attn_in['bp'], 'L3_ffn_gate_kernel': _L3_ffn_in['gate_kernel'], 'L3_ffn_w0_kernel': _L3_ffn_in['w0_kernel'], 'L3_ffn_w1_kernel': _L3_ffn_in['w1_kernel'], 'L3_ffn_wo_kernel': _L3_ffn_in['wo_kernel']}
    _x0 = _d['L0_attn_x']
    _d['L0_attn_x'] = jax.random.normal(jax.random.fold_in(jax.random.key(seed), 1), (2, 1024, 128), dtype=_x0.dtype)
    del _x0
    return _d

def reference(L0_attn_x, L0_attn_w_qkv, L0_attn_b_qkv, L0_attn_w_gate, L0_attn_b_gate, L0_attn_w_proj, L0_attn_b_proj, L0_attn_ln_g, L0_attn_ln_b, L0_ffn_w_gate, L0_ffn_w_up, L0_ffn_w_down, L1_attn_W_qk, L1_attn_b_qk, L1_attn_W_v, L1_attn_b_v, L1_attn_W_out, L1_attn_b_out, L1_attn_ln_gamma, L1_attn_ln_beta, L1_ffn_gate_w, L1_ffn_fc1_w, L1_ffn_fc1_b, L1_ffn_geglu_mult, L1_ffn_fc2_w, L1_ffn_fc2_b, L1_ffn_s_fc1_w, L1_ffn_s_fc1_b, L1_ffn_s_geglu_mult, L1_ffn_s_fc2_w, L1_ffn_s_fc2_b, L2_attn_wq, L2_attn_wk, L2_attn_wv, L2_attn_wo, L2_ffn_W1, L2_ffn_b1, L2_ffn_W2, L2_ffn_b2, L3_attn_Wq, L3_attn_bq, L3_attn_Wk, L3_attn_bk, L3_attn_Wv, L3_attn_bv, L3_attn_Wp, L3_attn_bp, L3_ffn_gate_kernel, L3_ffn_w0_kernel, L3_ffn_w1_kernel, L3_ffn_wo_kernel):

    def _L0_attn_ref(x, w_qkv, b_qkv, w_gate, b_gate, w_proj, b_proj, ln_g, ln_b):
        import jax, jax.numpy as jnp
        import numpy as np
        D_MODEL = 128
        B, T = (4, 512)
        LN_EPS = 1e-05
        DEN_EPS = 1e-06
        mu = jnp.mean(x, axis=-1, keepdims=True)
        var = jnp.mean(jnp.square(x - mu), axis=-1, keepdims=True)
        xn = (x - mu) * jax.lax.rsqrt(var + LN_EPS) * ln_g + ln_b
        qkv = xn @ w_qkv + b_qkv
        q, k, v = jnp.split(qkv, 3, axis=-1)
        gate = jax.nn.sigmoid(xn @ w_gate + b_gate)
        k = k * gate
        q = jax.nn.elu(q) + 1.0
        k = jax.nn.elu(k) + 1.0
        attn = jnp.einsum('btd,bsd->bts', q, k)
        tq = jnp.arange(q.shape[1])
        mask = (tq[:, None] >= tq[None, :]).astype(attn.dtype)
        attn = attn * mask
        out_num = jnp.einsum('bts,bsd->btd', attn, v)
        k_cumsum = jnp.cumsum(k, axis=1)
        out_den = jnp.sum(q * k_cumsum, axis=-1, keepdims=True) + DEN_EPS
        return out_num / out_den @ w_proj + b_proj

    def _L0_ffn_ref(x, w_gate, w_up, w_down):
        import jax, jax.numpy as jnp
        import numpy as np
        BLOCK = 16
        _GRID = jnp.array([0.0, 0.5, 1.0, 1.5, 2.0, 3.0, 4.0, 6.0], dtype=jnp.float32)
        _MID = jnp.array([0.25, 0.75, 1.25, 1.75, 2.5, 3.5, 5.0], dtype=jnp.float32)

        def fp4_quant_dequant(x):
            shape = x.shape
            xb = x.reshape(shape[:-1] + (shape[-1] // BLOCK, BLOCK))
            scale = jnp.max(jnp.abs(xb), axis=-1, keepdims=True) / 6.0
            scale = jnp.maximum(scale, jnp.float32(1e-12))
            xn = xb / scale
            idx = jnp.searchsorted(_MID, jnp.abs(xn))
            q = _GRID[idx] * jnp.sign(xn) * scale
            return q.reshape(shape)

        def fp4_linear(x, w):
            xq = fp4_quant_dequant(x)
            wq = fp4_quant_dequant(w)
            return jnp.einsum('bsk,nk->bsn', xq, wq)
        gate = fp4_linear(x, w_gate)
        y = fp4_linear(x, w_up)
        h = jax.nn.silu(gate) * y
        return fp4_linear(h, w_down)

    def _L1_attn_ref(x, W_qk, b_qk, W_v, b_v, W_out, b_out, ln_gamma, ln_beta):
        import jax, jax.numpy as jnp
        import numpy as np
        RSQRT2 = 2 ** (-0.5)
        B, S, D_IN = (2, 512, 128)
        H, D_HEAD = (8, 64)
        QK_DIM = H * D_HEAD
        V_DIM = H * D_HEAD
        OUT_DIM = D_IN
        LN_EPS = 1e-05

        def _layernorm(y, gamma, beta):
            mu = jnp.mean(y, axis=-1, keepdims=True)
            var = jnp.mean(jnp.square(y - mu), axis=-1, keepdims=True)
            return (y - mu) * jax.lax.rsqrt(var + LN_EPS) * gamma + beta
        b, s, _ = x.shape
        scale = D_HEAD ** (-0.5)
        qk = x @ W_qk + b_qk
        qk = qk.reshape(b, s, H, D_HEAD, 2)
        q, k = (qk[..., 0], qk[..., 1])
        v = (x @ W_v + b_v).reshape(b, s, H, D_HEAD)
        sim = jnp.einsum('bihd,bjhd->bhij', q, k) * scale
        attn = jax.nn.softmax(sim, axis=-1)
        o = jnp.einsum('bhij,bjhd->bihd', attn, v)
        o = o.reshape(b, s, V_DIM)
        y = _layernorm(o @ W_out + b_out, ln_gamma, ln_beta)
        return (y + x) * RSQRT2

    def _L1_ffn_ref(x, gate_w, fc1_w, fc1_b, geglu_mult, fc2_w, fc2_b, s_fc1_w, s_fc1_b, s_geglu_mult, s_fc2_w, s_fc2_b):
        import jax, jax.numpy as jnp
        import numpy as np
        S, B, D = (128, 2, 128)
        E, TOPK = (15, 3)
        F = 128
        FS = 256

        def _uinit(k, shape, out_dim):
            std = out_dim ** (-0.5)
            return jax.random.uniform(k, shape, jnp.float32, -std, std)
        s, b, d = x.shape
        xt = x.reshape(-1, d)
        T = xt.shape[0]
        logits = xt @ gate_w.T
        scores = jax.nn.softmax(logits, axis=-1)
        topk_w, topk_idx = jax.lax.top_k(scores, TOPK)
        topk_w = topk_w / (jnp.sum(topk_w, axis=-1, keepdims=True) + 1e-20)
        comb = jnp.zeros((T, E), xt.dtype).at[jnp.arange(T)[:, None], topk_idx].add(topk_w)
        h = jnp.einsum('td,efd->etf', xt, fc1_w) + fc1_b[:, None, :]
        xh, g = (h[..., :F], h[..., F:])
        a = jax.nn.gelu(g, approximate=False) * xh * geglu_mult[:, None, :]
        yexp = jnp.einsum('etf,edf->etd', a, fc2_w) + fc2_b[:, None, :]
        y = jnp.einsum('etd,te->td', yexp, comb)
        hs = xt @ s_fc1_w.T + s_fc1_b
        xs, gs = (hs[..., :FS], hs[..., FS:])
        as_ = jax.nn.gelu(gs, approximate=False) * xs * s_geglu_mult
        ys = as_ @ s_fc2_w.T + s_fc2_b
        return (y + ys).reshape(s, b, d)

    def _L2_attn_ref(x, wq, wk, wv, wo):
        import jax, jax.numpy as jnp
        import numpy as np
        B, S, HID, NH, BS = (1, 256, 128, 16, 64)
        D = HID // NH
        THRESH = 0.01
        SCALE = D ** (-0.5)
        b, s, _ = x.shape
        nb = s // BS

        def proj(w):
            return (x @ w.T).reshape(b, s, NH, D).transpose(0, 2, 1, 3)
        q, k, v = (proj(wq), proj(wk), proj(wv))
        q_mean = q.reshape(b, NH, nb, BS, D).mean(axis=3)
        k_mean = k.reshape(b, NH, nb, BS, D).mean(axis=3)
        block_scores = jnp.einsum('bhid,bhjd->bhij', q_mean, k_mean) / np.sqrt(D)
        block_mask = block_scores > THRESH
        full_mask = jnp.broadcast_to(block_mask[:, :, :, None, :, None], (b, NH, nb, BS, nb, BS)).reshape(b, NH, s, s)
        eye = jnp.eye(s, dtype=bool)
        full_mask = full_mask | eye
        scores = jnp.einsum('bhid,bhjd->bhij', q, k) * SCALE
        scores = jnp.where(full_mask, scores, -jnp.inf)
        attn = jax.nn.softmax(scores, axis=-1)
        block_max = attn.reshape(b, NH, nb, BS, nb, BS).max(axis=(3, 5))
        smask = block_max > THRESH
        sfull = jnp.broadcast_to(smask[:, :, :, None, :, None], (b, NH, nb, BS, nb, BS)).reshape(b, NH, s, s) | eye
        attn = jnp.where(sfull, attn, 0.0)
        out = jnp.einsum('bhij,bhjd->bhid', attn, v)
        out = out.transpose(0, 2, 1, 3).reshape(b, s, NH * D)
        return out @ wo.T

    def _L2_ffn_ref(x, W1, b1, W2, b2):
        import jax, jax.numpy as jnp
        import numpy as np
        EPS = 1e-05

        def _quantize(W):
            gamma = jnp.mean(jnp.abs(W))
            return jnp.clip(jnp.round(W / (gamma + EPS)), -1.0, 1.0)
        Wq1 = _quantize(W1)
        Wq2 = _quantize(W2)
        h = jax.nn.relu(jnp.einsum('bsd,fd->bsf', x, Wq1) + b1)
        out = jnp.einsum('bsf,df->bsd', h, Wq2) + b2
        return out

    def _L3_attn_ref(x, Wq, bq, Wk, bk, Wv, bv, Wp, bp):
        import jax, jax.numpy as jnp
        import numpy as np
        N_HEAD = 16
        NEG_BIG = -10000000000.0

        def _rope_cos_sin(T, head_dim):
            t = jnp.arange(T, dtype=jnp.float32)[:, None]
            i = jnp.arange(head_dim // 2, dtype=jnp.float32)
            theta = jnp.power(10000.0, 2.0 * i / head_dim)
            ang = t * theta[None, :]
            return (jnp.cos(ang), jnp.sin(ang))

        def _apply_rope(x, cos, sin):
            B, H, T, D = x.shape
            xr = x.reshape(B, H, T, D // 2, 2)
            x0, x1 = (xr[..., 0], xr[..., 1])
            c = cos[None, None, :, :]
            s = sin[None, None, :, :]
            o0 = x0 * c - x1 * s
            o1 = x0 * s + x1 * c
            return jnp.stack([o0, o1], axis=-1).reshape(B, H, T, D)
        B, T, C = x.shape
        H = N_HEAD
        D = C // H

        def heads(W, b):
            y = jnp.einsum('btc,oc->bto', x, W) + b
            return y.reshape(B, T, H, D).transpose(0, 2, 1, 3)
        q, k, v = (heads(Wq, bq), heads(Wk, bk), heads(Wv, bv))
        cos, sin = _rope_cos_sin(T, D)
        q = _apply_rope(q, cos, sin)
        k = _apply_rope(k, cos, sin)
        att = jnp.einsum('bhqd,bhkd->bhqk', q, k) * (1.0 / np.sqrt(D))
        causal = jnp.tril(jnp.ones((T, T), bool))
        att = jnp.where(causal[None, None], att, NEG_BIG)
        att = jax.nn.softmax(att, axis=-1)
        y = jnp.einsum('bhqk,bhkd->bhqd', att, v)
        y = y.transpose(0, 2, 1, 3).reshape(B, T, C)
        return jnp.einsum('btc,oc->bto', y, Wp) + bp

    def _L3_ffn_ref(x, gate_kernel, w0_kernel, w1_kernel, wo_kernel):
        import jax, jax.numpy as jnp
        import numpy as np
        NUM_EXPERTS = 8
        TOP_K = 2
        B, L, E = x.shape
        gate_logits = jnp.einsum('ble,en->bln', x, gate_kernel)
        top_k_weights, top_k_indices = jax.lax.top_k(gate_logits, TOP_K)
        softmax_probs = jax.nn.softmax(top_k_weights.astype(jnp.float32), axis=-1)
        weights = jnp.zeros_like(gate_logits)
        b_idx = jnp.arange(B)[:, None, None]
        l_idx = jnp.arange(L)[:, None]
        weights = weights.at[b_idx, l_idx, top_k_indices].set(softmax_probs)
        layer_w0 = jnp.einsum('ble,neh->blnh', x, w0_kernel)
        layer_w1 = jnp.einsum('ble,neh->blnh', x, w1_kernel)
        layer_mult = jax.nn.silu(layer_w0) * layer_w1
        intermediate = jnp.einsum('blnh,nhe->blne', layer_mult, wo_kernel)
        output = jnp.einsum('blne,bln->ble', intermediate, weights)
        return output
    x = L0_attn_x
    x = x + _L0_attn_ref(_layernorm(x, axis=-1), L0_attn_w_qkv, L0_attn_b_qkv, L0_attn_w_gate, L0_attn_b_gate, L0_attn_w_proj, L0_attn_b_proj, L0_attn_ln_g, L0_attn_ln_b)
    x = x + _L0_ffn_ref(_layernorm(x, axis=-1), L0_ffn_w_gate, L0_ffn_w_up, L0_ffn_w_down)
    x = x + _L1_attn_ref(_layernorm(x, axis=-1), L1_attn_W_qk, L1_attn_b_qk, L1_attn_W_v, L1_attn_b_v, L1_attn_W_out, L1_attn_b_out, L1_attn_ln_gamma, L1_attn_ln_beta)
    x = x + _L1_ffn_ref(_layernorm(x, axis=-1), L1_ffn_gate_w, L1_ffn_fc1_w, L1_ffn_fc1_b, L1_ffn_geglu_mult, L1_ffn_fc2_w, L1_ffn_fc2_b, L1_ffn_s_fc1_w, L1_ffn_s_fc1_b, L1_ffn_s_geglu_mult, L1_ffn_s_fc2_w, L1_ffn_s_fc2_b)
    x = x + _L2_attn_ref(_layernorm(x, axis=-1), L2_attn_wq, L2_attn_wk, L2_attn_wv, L2_attn_wo)
    x = x + _L2_ffn_ref(_layernorm(x, axis=-1), L2_ffn_W1, L2_ffn_b1, L2_ffn_W2, L2_ffn_b2)
    x = x + _L3_attn_ref(_layernorm(x, axis=-1), L3_attn_Wq, L3_attn_bq, L3_attn_Wk, L3_attn_bk, L3_attn_Wv, L3_attn_bv, L3_attn_Wp, L3_attn_bp)
    x = x + _L3_ffn_ref(_layernorm(x, axis=-1), L3_ffn_gate_kernel, L3_ffn_w0_kernel, L3_ffn_w1_kernel, L3_ffn_wo_kernel)
    return x

_drawn_inputs = setup_inputs


def setup_inputs(seed=0):
    import zlib

    import numpy as np

    out = dict(_drawn_inputs(seed))
    spreads = {'L0_attn_b_qkv': (0.0, 0.1),
     'L0_attn_b_gate': (0.0, 0.8),
     'L0_attn_b_proj': (0.0, 0.1),
     'L0_attn_ln_g': (1.0, 0.2),
     'L0_attn_ln_b': (0.0, 0.1),
     'L1_attn_b_qk': (0.0, 0.1),
     'L1_attn_b_v': (0.0, 0.1),
     'L1_attn_b_out': (0.0, 0.1),
     'L1_attn_ln_gamma': (1.0, 0.2),
     'L1_attn_ln_beta': (0.0, 0.1),
     'L1_ffn_geglu_mult': (1.0, 0.6),
     'L1_ffn_s_geglu_mult': (1.0, 0.6)}
    factors = {'L0_attn_w_gate': 2.859,
     'L0_ffn_w_up': 3.095,
     'L1_ffn_fc1_w': 2.918,
     'L1_ffn_fc1_b': 4.185,
     'L1_ffn_s_fc1_b': 8.0,
     'L2_ffn_b1': 8.0,
     'L2_ffn_b2': 25.865,
     'L3_attn_Wq': 8.0,
     'L3_attn_bq': 8.0,
     'L3_attn_Wk': 8.0,
     'L3_attn_bk': 8.0,
     'L3_attn_Wv': 8.0,
     'L3_attn_bv': 22.852,
     'L3_attn_Wp': 8.0,
     'L3_attn_bp': 200.0,
     'L3_ffn_gate_kernel': 8.0,
     'L3_ffn_w0_kernel': 8.0,
     'L3_ffn_w1_kernel': 8.0,
     'L3_ffn_wo_kernel': 8.0}
    for name, (base, spread) in spreads.items():
        noise = np.random.default_rng([zlib.crc32(name.encode()), seed]).standard_normal(out[name].shape)
        drawn = base * np.exp(spread * noise) if base else spread * noise
        out[name] = jnp.asarray(drawn.astype(out[name].dtype))
    for name, factor in factors.items():
        out[name] = (out[name] * factor).astype(out[name].dtype)
    return out
```

```python
from contextlib import ExitStack

import numpy as np

import concourse.bass as bass
from concourse import mybir

F32 = mybir.dt.float32
BF16 = mybir.dt.bfloat16
ALU = mybir.AluOpType
ACT = mybir.ActivationFunctionType
AX = mybir.AxisListType

P = 128
BATCH, SEQ, D = 2, 1024, 128
TOKENS = BATCH * SEQ
TILES = TOKENS // P
TPB = SEQ // P
BANK = 512
CHUNKS = TOKENS // BANK
TPC = BANK // P
LN_EPS = 1e-5


def wait_from(eng, sem, value):
    if not isinstance(value, int) or value > 0:
        eng.wait_ge(sem, value)


class Chip:

    def __init__(self, nc, ctx, ins, out):
        self.nc, self.ctx, self.ins, self.out = nc, ctx, ins, out
        self.x = self.sbuf(ctx, "x_res", [P, TILES, D])
        self.xn = self.sbuf(ctx, "x_norm", [P, TILES, D])
        self.xt = self.sbuf(ctx, "x_norm_t", [P, TOKENS])
        self.ident = self.sbuf(ctx, "identity", [P, P])
        self.ones_row = self.sbuf(ctx, "ones_row", [1, P])
        self.ident_bf = self.sbuf(ctx, "identity_bf", [P, P], BF16)
        self.stats = self.sbuf(ctx, "ln_stats", [P, TILES, 6])
        self.moments = self.sbuf(ctx, "ln_moments", [P, TILES, 2])
        self.std = self.sbuf(ctx, "ln_std", [P, TILES])
        self.rstd = self.sbuf(ctx, "ln_rstd", [P, TILES])
        self.newton = self.sbuf(ctx, "ln_newton", [P, TILES])
        self.eps = self.sbuf(ctx, "ln_eps", [P, 1])
        self.semaphores = []
        self.share_ln_semaphores("first")
        self.ps = ctx.enter_context(nc.psum_tensor("psum", [P, 8, BANK], F32))

    def sbuf(self, ctx, name, shape, dt=F32):
        return ctx.enter_context(self.nc.sbuf_tensor(name, shape, dt))

    def semaphore(self, name):
        self.semaphores.append(self.nc.alloc_semaphore(name=name))
        return self.semaphores[-1]

    def share_ln_semaphores(self, half):
        self.ln = {what: self.semaphore(f"ln_{half}_{what}") for what in
                   ("stats", "moments", "std", "rstd", "normed", "turned", "loaded")}
        self.ln_count = dict.fromkeys(self.ln, 0)

    def clear_semaphores(self):
        self.nc.clear_and_free_semaphores(self.semaphores)
        self.nc.all_engine_barrier()
        self.semaphores = []
        self.share_ln_semaphores("second")

    def bank(self, k):
        return self.ps[:, k, :]


def start(nc, c):
    with ExitStack() as ctx:
        loaded = c.semaphore("start_loaded")
        ident_ready = c.semaphore("ident_ready")
        block = ctx.enter_context(nc.Block())

        @block.sync
        def _(sp):
            sp.dma_start(c.x[:, :, :], c.ins["x"].rearrange("(t p) d -> p t d", p=P)).then_inc(loaded, 16)
            sp.dma_start(c.ident[:, :], c.ins["ident"]).then_inc(ident_ready, 16)
            sp.wait_ge(loaded, 16)

        @block.vector
        def _(dve):
            dve.memset(c.ones_row[:, :], 1.0)
            dve.memset(c.eps[:, :], LN_EPS)
            dve.wait_ge(ident_ready, 16)
            dve.tensor_copy(c.ident_bf[:, :], c.ident[:, :])


def finish(nc, c):
    with ExitStack() as ctx:
        stored = c.semaphore("output_stored")
        block = ctx.enter_context(nc.Block())

        @block.sync
        def _(sp):
            sp.dma_start(c.out.rearrange("(t p) d -> p t d", p=P), c.x[:, :, :]).then_inc(stored, 16)
            sp.wait_ge(stored, 16)


def layer_norm(nc, c, name, src, transpose=True, gain=None, shift=None, loads=(), dst=None):
    dst = c.xn if dst is None else dst
    with ExitStack() as ctx:
        stats_ready, moments_ready, std_ready = c.ln["stats"], c.ln["moments"], c.ln["std"]
        rstd_ready, normed, turned, loaded = c.ln["rstd"], c.ln["normed"], c.ln["turned"], c.ln["loaded"]
        stats0, moments0, std0, rstd0, normed0, turned0, loaded0 = c.ln_count.values()
        for what, more in (("stats", TILES), ("moments", TILES), ("std", 1), ("rstd", 5), ("normed", TILES),
                           ("turned", TILES if transpose else 0), ("loaded", 16 * len(loads))):
            c.ln_count[what] += more
        block = ctx.enter_context(nc.Block())

        @block.sync
        def _(sp):
            for dst, dram in loads:
                sp.dma_start(dst, dram).then_inc(loaded, 16)
            if loads:
                sp.wait_ge(loaded, loaded0 + 16 * len(loads))

        @block.vector
        def _(dve):
            for t in range(TILES):
                dve.bn_stats(c.stats[:, t, :], src[:, t, :]).then_inc(stats_ready, 1)
            for t in range(TILES):
                dve.wait_ge(stats_ready, stats0 + t + 1)
                dve.bn_aggr(c.moments[:, t, :], c.stats[:, t, :]).then_inc(moments_ready, 1)
            dve.wait_ge(std_ready, std0 + 1)
            dve.reciprocal(c.rstd[:, :], c.std[:, :]).then_inc(rstd_ready, 1)
            dve.wait_ge(rstd_ready, rstd0 + 1)
            dve.tensor_tensor(c.newton[:, :], c.rstd[:, :], c.rstd[:, :], ALU.mult).then_inc(rstd_ready, 1)
            dve.wait_ge(rstd_ready, rstd0 + 2)
            dve.scalar_tensor_tensor(c.newton[:, :], c.moments[:, :, 1], LN_EPS, c.newton[:, :],
                                     ALU.add, ALU.mult).then_inc(rstd_ready, 1)
            dve.wait_ge(rstd_ready, rstd0 + 3)
            dve.tensor_scalar(c.newton[:, :], c.newton[:, :], -0.5, 1.5, ALU.mult, ALU.add).then_inc(rstd_ready, 1)
            dve.wait_ge(rstd_ready, rstd0 + 4)
            dve.tensor_tensor(c.rstd[:, :], c.rstd[:, :], c.newton[:, :], ALU.mult).then_inc(rstd_ready, 1)
            dve.wait_ge(rstd_ready, rstd0 + 5)
            for t in range(TILES):
                dve.tensor_scalar(dst[:, t, :], src[:, t, :], c.moments[:, t, 0:1], c.rstd[:, t:t + 1],
                                  ALU.subtract, ALU.mult).then_inc(normed, 1)

        @block.scalar
        def _(act):
            act.wait_ge(moments_ready, moments0 + TILES)
            act.activation(c.std[:, :], c.moments[:, :, 1], ACT.Sqrt, bias=c.eps[:, 0:1]).then_inc(std_ready, 1)
            if transpose:
                for g in range(CHUNKS):
                    act.wait_ge(turned, turned0 + TPC * (g + 1))
                    out = c.xt[:, g * BANK:(g + 1) * BANK]
                    if gain is None:
                        act.activation(out, c.bank(g), ACT.Identity)
                    else:
                        act.activation(out, c.bank(g), ACT.Identity, bias=shift, scale=gain)

        if transpose:
            @block.tensor
            def _(pe):
                for t in range(TILES):
                    pe.wait_ge(normed, normed0 + t + 1)
                    pe.transpose(c.bank(t // TPC)[:, (t % TPC) * P:(t % TPC + 1) * P], dst[:, t, :],
                                 c.ident[:, :]).then_inc(turned, 1)


def route(nc, c, name, experts, copies, topk, always, gate_w, comb):
    pads = 8 - topk
    wide = experts + pads
    low = -3.0e38
    with ExitStack() as ctx:
        def sem(what):
            return c.semaphore(f"{name}_{what}")

        def sb(what, shape):
            return c.sbuf(ctx, f"{name}_{what}", shape)

        logits = sb("logits", [P, TILES, wide])
        replaced = sb("replaced", [P, TILES, wide])
        top = sb("top", [P, TILES, 8])
        chosen = sb("chosen", [P, TILES, 8])
        shifted = sb("shifted", [P, TILES, experts])
        weight = sb("weight", [P, TILES, experts])
        total = sb("total", [P, TILES])
        logits_ps = c.bank(0)
        multiplied, step, exp_ready = sem("multiplied"), sem("step"), sem("exp")
        block = ctx.enter_context(nc.Block())

        @block.tensor
        def _(pe):
            for t in range(TILES):
                pe.matmul(logits_ps[:, t * experts:(t + 1) * experts], c.xt[:, t * P:(t + 1) * P], gate_w[:, :],
                          start=True, stop=True).then_inc(multiplied, 1)

        @block.vector
        def _(dve):
            dve.memset(logits[:, :, :], low).then_inc(step, 1)
            dve.wait_ge(step, 1)
            dve.wait_ge(multiplied, TILES)
            dve.tensor_copy(logits[:, :, 0:experts],
                            logits_ps[:, 0:TILES * experts].rearrange("p (t e) -> p t e", e=experts)).then_inc(step, 1)
            dve.wait_ge(step, 2)
            for t in range(TILES):
                dve.max(top[:, t, :], logits[:, t, :]).then_inc(step, 1)
            dve.memset(chosen[:, :, :], low).then_inc(step, 1)
            dve.wait_ge(step, 3 + TILES)
            dve.tensor_copy(chosen[:, :, 0:topk], top[:, :, 0:topk]).then_inc(step, 1)
            dve.tensor_tensor(shifted[:, :, :], logits[:, :, 0:experts],
                              top[:, :, 0:1].to_broadcast([P, TILES, experts]), ALU.subtract).then_inc(step, 1)
            dve.wait_ge(step, 5 + TILES)
            for t in range(TILES):
                dve.match_replace(replaced[:, t, :], chosen[:, t, :], logits[:, t, :], -low).then_inc(step, 1)
            dve.wait_ge(step, 5 + 2 * TILES)
            dve.wait_ge(exp_ready, 1)
            dve.scalar_tensor_tensor(weight[:, :, :], replaced[:, :, 0:experts], -low, weight[:, :, :],
                                     ALU.is_equal, ALU.mult).then_inc(step, 1)
            dve.wait_ge(step, 6 + 2 * TILES)
            dve.tensor_reduce(total[:, :], weight[:, :, :], AX.X, ALU.add).then_inc(step, 1)
            dve.wait_ge(step, 7 + 2 * TILES)
            dve.reciprocal(total[:, :], total[:, :]).then_inc(step, 1)
            dve.wait_ge(step, 8 + 2 * TILES)
            for k in range(copies):
                dve.tensor_tensor(comb[:, :, k:experts * copies:copies], weight[:, :, :],
                                  total[:, :].rearrange("p (t o) -> p t o", o=1).to_broadcast([P, TILES, experts]),
                                  ALU.mult)
            if always:
                dve.memset(comb[:, :, experts * copies:experts * copies + always], 1.0)

        @block.scalar
        def _(act):
            act.wait_ge(step, 5 + TILES)
            act.activation(weight[:, :, :], shifted[:, :, :], ACT.Exp).then_inc(exp_ready, 1)


def gated_experts(nc, c, name, parts, gate_act, weights, comb, biased, out_bias=None, out_bias_rows=0):
    with ExitStack() as ctx:
        def sem(what):
            return c.semaphore(f"{name}_{what}")

        w = [c.sbuf(ctx, f"{name}_w{k}", [P, weights.shape[2]]) for k in range(2)]
        gated = [c.sbuf(ctx, f"{name}_gated{k}", [P, BANK]) for k in range(2)]
        prod = [c.sbuf(ctx, f"{name}_prod{k}", [P, BANK]) for k in range(2)]
        a_ps, b_ps, y_ps = [c.bank(0), c.bank(1)], [c.bank(2), c.bank(3)], [c.bank(4), c.bank(5)]
        rows = out_bias_rows
        comb_t = c.sbuf(ctx, f"{name}_comb_t", [max(rows, 1), TOKENS])

        w_loaded, w_scaled = [sem(f"w{k}_loaded") for k in range(2)], sem("w_scaled")
        a_ready, b_ready, gated_ready, prod_ready = sem("a_ready"), sem("b_ready"), sem("gated_ready"), sem("prod_ready")
        y_ready, added = sem("y_ready"), sem("added")
        comb_turned, comb_copied, bias_ready, bias_added = sem("comb_turned"), sem("comb_copied"), sem("bias"), sem("bias_added")
        block = ctx.enter_context(nc.Block())

        pairs = (parts - 1) // 2
        last = 1 + 2 * pairs

        def each_part(eng, body):
            body(0, 0, 0)
            with eng.Fori(0, pairs) as i:
                body(i * 2 + 1, 1, i)
                body(i * 2 + 2, 0, i + 1)
            if last < parts:
                body(last, 1, pairs)

        @block.sync
        def _(sp):
            def load(e, k, use):
                wait_from(sp, y_ready, e * CHUNKS - CHUNKS)
                sp.dma_start(w[k][:, :], weights[e, :, :]).then_inc(w_loaded[k], 16)
            each_part(sp, load)

        @block.tensor
        def _(pe):
            if rows:
                for g in range(CHUNKS):
                    wait_from(pe, comb_copied, g - 1)
                    for j in range(TPC):
                        mm = pe.transpose(y_ps[g % 2][0:rows, j * P:(j + 1) * P], comb[:, g * TPC + j, 0:rows],
                                          c.ident[:, :])
                    mm.then_inc(comb_turned, 1)
                pe.wait_ge(comb_copied, CHUNKS)
                for g in range(CHUNKS):
                    wait_from(pe, bias_added, g - 1)
                    for j in range(TPC):
                        t = g * TPC + j
                        mm = pe.matmul(y_ps[g % 2][:, j * P:(j + 1) * P], comb_t[:, t * P:(t + 1) * P],
                                       out_bias[:, :], start=True, stop=True)
                    mm.then_inc(bias_ready, 1)
                pe.wait_ge(bias_added, CHUNKS)

            def down(n, g, k, e):
                pe.wait_ge(prod_ready, n + 1)
                wait_from(pe, added, n - 1)
                if biased:
                    pe.wait_ge(w_scaled, e + 1)
                for j in range(TPC):
                    mm = pe.matmul(y_ps[g % 2][:, j * P:(j + 1) * P], prod[g % 2][:, j * P:(j + 1) * P],
                                   w[k][:, 2 * P:3 * P], start=True, stop=True)
                mm.then_inc(y_ready, 1)

            def part(e, k, use):
                pe.wait_ge(w_loaded[k], use * 16 + 16)
                for g in range(CHUNKS):
                    n = e * CHUNKS + g
                    x = c.xt[:, g * BANK:(g + 1) * BANK]
                    wait_from(pe, gated_ready, n - 1)
                    pe.matmul(a_ps[g % 2], w[k][:, 0:P], x, start=True, stop=True).then_inc(a_ready, 1)
                    wait_from(pe, prod_ready, n - 1)
                    pe.matmul(b_ps[g % 2], w[k][:, P:2 * P], x, start=True, stop=True).then_inc(b_ready, 1)
                    if g:
                        down(n - 1, g - 1, k, e)
                    elif not (isinstance(e, int) and e == 0):
                        down(n - 1, CHUNKS - 1, 1 - k, e - 1)
            each_part(pe, part)
            down(parts * CHUNKS - 1, CHUNKS - 1, (parts - 1) % 2, parts - 1)

        @block.scalar
        def _(act):
            for g in range(CHUNKS if rows else 0):
                act.wait_ge(comb_turned, g + 1)
                act.copy(comb_t[:, g * BANK:(g + 1) * BANK], y_ps[g % 2][0:rows, :]).then_inc(comb_copied, 1)

            def part(e, k, use):
                for g in range(CHUNKS):
                    n = e * CHUNKS + g
                    act.wait_ge(a_ready, n + 1)
                    wait_from(act, prod_ready, n - 1)
                    act.activation(gated[g % 2][:, :], a_ps[g % 2], gate_act,
                                   bias=w[k][:, 3 * P:3 * P + 1] if biased else 0.0).then_inc(gated_ready, 1)
            each_part(act, part)

        @block.vector
        def _(dve):
            for g in range(CHUNKS if rows else 0):
                dve.wait_ge(bias_ready, g + 1)
                x = c.x[:, g * TPC:(g + 1) * TPC, :].rearrange("p t d -> p (t d)")
                dve.tensor_tensor(x, x, y_ps[g % 2], ALU.add).then_inc(bias_added, 1)
            if rows:
                dve.wait_ge(bias_added, CHUNKS)

            def add(n, g, e):
                dve.wait_ge(y_ready, n + 1)
                wait_from(dve, added, n - 3)
                for j in range(TPC):
                    t = g * TPC + j
                    op = dve.scalar_tensor_tensor(c.x[:, t, :], y_ps[g % 2][:, j * P:(j + 1) * P],
                                                  comb[:, t, e:e + 1] if isinstance(e, int) else comb[:, t, bass.ds(e, 1)],
                                                  c.x[:, t, :], ALU.mult, ALU.add)
                op.then_inc(added, 1)

            def part(e, k, use):
                if biased:
                    dve.wait_ge(w_loaded[k], use * 16 + 16)
                    dve.tensor_scalar(w[k][:, 2 * P:3 * P], w[k][:, 2 * P:3 * P], w[k][:, 3 * P + 2:3 * P + 3], None,
                                      ALU.mult).then_inc(w_scaled, 1)
                for g in range(CHUNKS):
                    n = e * CHUNKS + g
                    dve.wait_ge(gated_ready, n + 1)
                    dve.wait_ge(b_ready, n + 1)
                    wait_from(dve, y_ready, n - 1)
                    if not biased:
                        op = dve.tensor_tensor(prod[g % 2][:, :], b_ps[g % 2], gated[g % 2][:, :], ALU.mult)
                    else:
                        op = dve.scalar_tensor_tensor(prod[g % 2][:, :], b_ps[g % 2], w[k][:, 3 * P + 1:3 * P + 2],
                                                      gated[g % 2][:, :], ALU.add, ALU.mult)
                    op.then_inc(prod_ready, 1)
                    if g:
                        add(n - 1, g - 1, e)
                    elif not (isinstance(e, int) and e == 0):
                        add(n - 1, CHUNKS - 1, e - 1)
            each_part(dve, part)
            add(parts * CHUNKS - 1, CHUNKS - 1, parts - 1)


def ternary_mlp(nc, c, w1, w2, b1, b2):
    hidden = w1.shape[1]
    tiles_h = hidden // P
    eps = 1e-5
    rne = 1.5 * 2.0 ** 23
    with ExitStack() as ctx:
        def sem(what):
            return c.semaphore(f"mlp_{what}")

        def sb(what, shape):
            return c.sbuf(ctx, f"mlp_{what}", shape)

        sums, gamma, ones = sb("sums", [P, 2]), sb("gamma", [P, 2]), sb("ones", [P, P])
        h = [sb(f"h{k}", [P, tiles_h, BANK]) for k in range(2)]
        step, sums_ps_ready, h_ready, relu_ready, y_ready, added = (
            sem("step"), sem("sums"), sem("h"), sem("relu"), sem("y"), sem("added"))
        w2f = w2[:, :, :].rearrange("p f d -> p (f d)")
        block = ctx.enter_context(nc.Block())

        @block.vector
        def _(dve):
            dve.memset(ones[:, :], 1.0).then_inc(step, 1)
            dve.tensor_reduce(sums[:, 0:1], w1[:, :], AX.X, ALU.add, apply_absolute_value=True).then_inc(step, 1)
            dve.tensor_reduce(sums[:, 1:2], w2f, AX.X, ALU.add, apply_absolute_value=True).then_inc(step, 1)
            dve.wait_ge(sums_ps_ready, 1)
            dve.tensor_scalar(gamma[:, :], c.bank(7)[:, 0:2], 1.0 / (hidden * D), eps, ALU.mult, ALU.add).then_inc(step, 1)
            dve.wait_ge(step, 4)
            dve.reciprocal(gamma[:, :], gamma[:, :]).then_inc(step, 1)
            dve.wait_ge(step, 5)
            n = 5
            for k, w in enumerate((w1[:, :], w2f)):
                for args in ((gamma[:, k:k + 1], 1.0, ALU.mult, ALU.min), (-1.0, rne, ALU.max, ALU.add),
                             (rne, None, ALU.subtract)):
                    dve.tensor_scalar(w, w, *args).then_inc(step, 1)
                    n += 1
                    dve.wait_ge(step, n)

            def tail(g):
                dve.wait_ge(y_ready, g + 1)
                x = c.x[:, g * TPC:(g + 1) * TPC, :].rearrange("p t d -> p (t d)")
                dve.tensor_tensor(x, x, c.bank(4 + g % 2), ALU.add).then_inc(added, 1)

            for g in range(CHUNKS):
                tail(g)

        @block.tensor
        def _(pe):
            pe.wait_ge(step, 3)
            pe.matmul(c.bank(7)[:, 0:2], ones[:, :], sums[:, :], start=True, stop=True).then_inc(sums_ps_ready, 1)

            def down(g):
                pe.wait_ge(relu_ready, tiles_h * (g + 1))
                wait_from(pe, added, g - 1)
                for j in range(TPC):
                    y = c.bank(4 + g % 2)[:, j * P:(j + 1) * P]
                    for f in range(tiles_h):
                        pe.matmul(y, h[g % 2][:, f, j * P:(j + 1) * P], w2[:, f, :], start=(f == 0), stop=False)
                    mm = pe.matmul(y, c.ones_row[:, :], b2[:, :], start=False, stop=True)
                mm.then_inc(y_ready, 1)

            pe.wait_ge(step, 11)
            for g in range(CHUNKS):
                for f in range(tiles_h):
                    wait_from(pe, relu_ready, tiles_h * (g - 1) + f + 1)
                    pe.matmul(c.bank(f), w1[:, f * P:(f + 1) * P], c.xt[:, g * BANK:(g + 1) * BANK],
                              start=True, stop=True).then_inc(h_ready, 1)
                if g:
                    down(g - 1)
            down(CHUNKS - 1)

        @block.scalar
        def _(act):
            for g in range(CHUNKS):
                wait_from(act, y_ready, g - 1)
                for f in range(tiles_h):
                    act.wait_ge(h_ready, tiles_h * g + f + 1)
                    act.activation(h[g % 2][:, f, :], c.bank(f), ACT.Relu, bias=b1[:, f:f + 1]).then_inc(relu_ready, 1)


def linear_attention(nc, c, w, bias, w_out, b_out, mask):
    den_eps = 1e-6
    gate, key, query, value = range(4)
    with ExitStack() as ctx:
        def sem(what):
            return c.semaphore(f"lin_{what}")

        def sb(what, shape):
            return c.sbuf(ctx, f"lin_{what}", shape)

        qt, kt, vt = sb("qt", [P, SEQ]), sb("kt", [P, SEQ]), sb("vt", [P, SEQ])
        half_gate, z, zmin, ez = (sb(n, [P, BANK]) for n in ("gate", "z", "zmin", "ez"))
        zk, zkmin, ezk = (sb(n, [P, BANK]) for n in ("zk", "zkmin", "ezk"))
        half_bias = sb("half_bias", [P, 1])
        tok = [sb(f"tok{k}", [P, 2 * P + 1]) for k in range(2)]
        masked = [sb(f"masked{k}", [P, P]) for k in range(2)]
        state = [sb(f"state{k}", [P, P + 1]) for k in range(2)]
        rden = [sb(f"rden{k}", [P, 1]) for k in range(2)]
        o = [sb(f"o{k}", [P, P]) for k in range(2)]
        ot = [sb(f"ot{k}", [P, P]) for k in range(2)]
        tok_ps, a_ps, o_ps, s_ps = c.bank(4), c.bank(5), c.bank(6), c.bank(7)
        ot_ps, y_ps = c.bank(3), c.bank(2)

        projected, tanh_ready, z_ready, exp_ready, qk_ready, v_ready = (
            sem(n) for n in ("projected", "tanh", "z", "exp", "qk", "v"))
        tok_turned, tok_ready, a_done, a_masked, o_done, o_ready, s_done, s_ready = (
            sem(n) for n in ("tok_turned", "tok", "a", "masked", "o_done", "o", "s_done", "s"))
        den_step, ot_turned, ot_ready, y_done, added, setup = (
            sem(n) for n in ("den_step", "ot_turned", "ot", "y", "added", "setup"))
        block = ctx.enter_context(nc.Block())

        @block.tensor
        def _(pe):
            def out_proj(n, k):
                pe.wait_ge(o_ready, n + 1)
                pe.wait_ge(ot_ready, n)
                pe.transpose(ot_ps[:, 0:P], o[k][:, :], c.ident[:, :]).then_inc(ot_turned, 1)
                pe.wait_ge(ot_ready, n + 1)
                pe.wait_ge(added, n)
                pe.matmul(y_ps[:, 0:P], ot[k][:, :], w_out[:, :], start=True, stop=False)
                pe.matmul(y_ps[:, 0:P], c.ones_row[:, :], b_out[:, :], start=False, stop=True).then_inc(y_done, 1)

            with pe.Fori(0, BATCH) as b:
                pe.wait_ge(added, b * TPB)
                for j in range(2):
                    m = b * 2 + j
                    pe.wait_ge(qk_ready, m * 2)
                    pe.wait_ge(v_ready, m)
                    for r in (gate, key, query, value):
                        pe.matmul(c.bank(r), w[:, r * P:(r + 1) * P], c.xt[:, bass.ds(b * SEQ + j * BANK, BANK)],
                                  start=True, stop=True).then_inc(projected, 1)
                pe.wait_ge(qk_ready, b * 4 + 4)
                pe.wait_ge(v_ready, b * 2 + 2)
                for t in range(TPB):
                    n, k, s = b * TPB + t, t % 2, slice(t * P, (t + 1) * P)
                    pe.wait_ge(tok_ready, n)
                    pe.transpose(tok_ps[:, 0:P], kt[:, s], c.ident[:, :])
                    pe.transpose(tok_ps[:, P:2 * P], vt[:, s], c.ident[:, :]).then_inc(tok_turned, 1)
                    pe.wait_ge(a_masked, n)
                    pe.matmul(a_ps[:, 0:P], kt[:, s], qt[:, s], start=True, stop=True).then_inc(a_done, 1)
                    if t:
                        out_proj(n - 1, (t - 1) % 2)
                    pe.wait_ge(tok_ready, n + 1)
                    pe.wait_ge(s_ready, n)
                    pe.matmul(s_ps[:, 0:P + 1], tok[k][:, 0:P], tok[k][:, P:2 * P + 1],
                              start=True, stop=True).then_inc(s_done, 1)
                    pe.wait_ge(a_masked, n + 1)
                    pe.wait_ge(o_ready, n)
                    mm = pe.matmul(o_ps[:, 0:P + 1], masked[k][:, :], tok[k][:, P:2 * P + 1],
                                   start=True, stop=(t == 0))
                    if t:
                        mm = pe.matmul(o_ps[:, 0:P + 1], qt[:, s], state[1 - k][:, :], start=False, stop=True)
                    mm.then_inc(o_done, 1)
                out_proj(b * TPB + TPB - 1, (TPB - 1) % 2)

        @block.scalar
        def _(act):
            act.wait_ge(setup, 3)
            with act.Fori(0, BATCH) as b:
                for j in range(2):
                    m = b * 2 + j
                    act.wait_ge(projected, m * 4 + 1)
                    act.wait_ge(z_ready, m * 2)
                    act.activation(half_gate[:, :], c.bank(gate), ACT.Tanh, bias=half_bias[:, 0:1],
                                   scale=0.5).then_inc(tanh_ready, 1)
                    act.wait_ge(projected, m * 4 + 4)
                    act.wait_ge(o_done, b * TPB)
                    act.activation(vt[:, j * BANK:(j + 1) * BANK], c.bank(value), ACT.Identity,
                                   bias=bias[:, value:value + 1]).then_inc(v_ready, 1)
                    act.wait_ge(z_ready, m * 2 + 1)
                    act.wait_ge(qk_ready, m * 2)
                    act.activation(ezk[:, :], zkmin[:, :], ACT.Exp).then_inc(exp_ready, 1)
                    act.wait_ge(z_ready, m * 2 + 2)
                    act.activation(ez[:, :], zmin[:, :], ACT.Exp).then_inc(exp_ready, 1)
                for t in range(TPB):
                    n, k = b * TPB + t, t % 2
                    act.wait_ge(ot_turned, n + 1)
                    act.copy(ot[k][:, :], ot_ps[:, 0:P]).then_inc(ot_ready, 1)

        @block.vector
        def _(dve):
            dve.tensor_scalar(half_bias[:, :], bias[:, gate:gate + 1], 0.5, None, ALU.mult).then_inc(setup, 1)
            for k in range(2):
                dve.memset(tok[k][:, 2 * P:2 * P + 1], 1.0).then_inc(setup, 1)
            with dve.Fori(0, BATCH) as b:
                for j in range(2):
                    m = b * 2 + j
                    dve.wait_ge(tanh_ready, m + 1)
                    dve.tensor_scalar(half_gate[:, :], half_gate[:, :], 0.5, 0.5, ALU.mult, ALU.add).then_inc(den_step, 1)
                    dve.wait_ge(projected, m * 4 + 2)
                    dve.wait_ge(den_step, m * 3 + 1)
                    dve.scalar_tensor_tensor(zk[:, :], c.bank(key), bias[:, key:key + 1], half_gate[:, :],
                                             ALU.add, ALU.mult).then_inc(den_step, 1)
                    dve.wait_ge(projected, m * 4 + 3)
                    dve.tensor_scalar(z[:, :], c.bank(query), bias[:, query:query + 1], None, ALU.add).then_inc(den_step, 1)
                    dve.wait_ge(den_step, m * 3 + 2)
                    dve.tensor_scalar(zkmin[:, :], zk[:, :], 0.0, None, ALU.min).then_inc(z_ready, 1)
                    dve.wait_ge(den_step, m * 3 + 3)
                    dve.tensor_scalar(zmin[:, :], z[:, :], 0.0, None, ALU.min).then_inc(z_ready, 1)
                    dve.wait_ge(o_done, b * TPB)
                    for i, (dst, src, e) in enumerate(((kt, zk, ezk), (qt, z, ez))):
                        dve.wait_ge(exp_ready, m * 2 + 1 + i)
                        dve.scalar_tensor_tensor(dst[:, j * BANK:(j + 1) * BANK], src[:, :], 0.0, e[:, :],
                                                 ALU.max, ALU.add).then_inc(qk_ready, 1)
                    dve.wait_ge(qk_ready, m * 2 + 2)
                for t in range(TPB):
                    n, k = b * TPB + t, t % 2
                    dve.wait_ge(tok_turned, n + 1)
                    if t >= 1:
                        dve.wait_ge(o_done, n - 1)
                    else:
                        dve.wait_ge(o_done, n)
                    dve.tensor_copy(tok[k][:, 0:2 * P], tok_ps[:, 0:2 * P]).then_inc(tok_ready, 1)
                    dve.wait_ge(a_done, n + 1)
                    dve.tensor_tensor(masked[k][:, :], a_ps[:, 0:P], mask[:, :], ALU.mult).then_inc(a_masked, 1)
                    dve.wait_ge(s_done, n + 1)
                    dve.wait_ge(o_done, n)
                    if t:
                        dve.wait_ge(s_ready, n)
                        dve.tensor_tensor(state[k][:, :], s_ps[:, 0:P + 1], state[1 - k][:, :], ALU.add).then_inc(s_ready, 1)
                    else:
                        dve.tensor_copy(state[k][:, :], s_ps[:, 0:P + 1]).then_inc(s_ready, 1)
                    dve.wait_ge(o_done, n + 1)
                    dve.tensor_scalar(rden[k][:, :], o_ps[:, P:P + 1], den_eps, None, ALU.add).then_inc(setup, 1)
                    dve.wait_ge(setup, n * 2 + 4)
                    dve.reciprocal(rden[k][:, :], rden[k][:, :]).then_inc(setup, 1)
                    dve.wait_ge(setup, n * 2 + 5)
                    if t >= 2:
                        dve.wait_ge(ot_turned, n - 1)
                    else:
                        dve.wait_ge(ot_turned, b * TPB)
                    dve.tensor_scalar(o[k][:, :], o_ps[:, 0:P], rden[k][:, 0:1], None, ALU.mult).then_inc(o_ready, 1)
                    if t:
                        dve.wait_ge(y_done, n)
                        dve.tensor_tensor(c.x[:, n - 1, :], c.x[:, n - 1, :], y_ps[:, 0:P], ALU.add).then_inc(added, 1)
                dve.wait_ge(y_done, b * TPB + TPB)
                dve.tensor_tensor(c.x[:, b * TPB + TPB - 1, :], c.x[:, b * TPB + TPB - 1, :], y_ps[:, 0:P],
                                  ALU.add).then_inc(added, 1)


def split_in_three(eng, parts, rest, src, step, at):
    eng.tensor_copy(parts[0], src).then_inc(step, 1)
    eng.wait_ge(step, at + 1)
    eng.tensor_tensor(rest, src, parts[0], ALU.subtract).then_inc(step, 1)
    eng.wait_ge(step, at + 2)
    eng.tensor_copy(parts[1], rest).then_inc(step, 1)
    eng.wait_ge(step, at + 3)
    eng.tensor_tensor(rest, rest, parts[1], ALU.subtract).then_inc(step, 1)
    eng.wait_ge(step, at + 4)
    eng.tensor_copy(parts[2], rest).then_inc(step, 1)


def wide_attention(nc, c, weights, w_out, b_out, y):
    pairs, dh = 4, 64
    units = 2 * TPB
    scale = dh ** -0.5
    with ExitStack() as ctx:
        def sem(what):
            return c.semaphore(f"wide_{what}")

        def sb(what, shape, dt=F32):
            return c.sbuf(ctx, f"wide_{what}", shape, dt)

        w = sb("w", [P, weights.shape[2]])
        q_bias = sb("q_bias", [P, 1])
        qt = [sb(f"qt{k}", [P, SEQ]) for k in range(2)]
        kt, vt = sb("kt", [P, SEQ]), sb("vt", [P, SEQ])
        v = sb("v", [P, TPB, P])
        minus_top = sb("minus_top", [P, TPB, 2])
        l, rest = sb("l", [P, TPB, 2]), sb("rest", [P, TPB, 2])
        e = [sb(f"e{k}", [P, SEQ]) for k in range(2)]
        et = [sb(f"et{k}", [P, 2, TPB, BANK]) for k in range(2)]
        rl3 = sb("rl3", [P, TPB, P], BF16)
        rl3_t = sb("rl3_t", [P, SEQ], BF16)
        spread = sb("spread", [P, P], BF16)
        u = sb("u", [P, SEQ])
        ot = sb("ot", [P, pairs, SEQ])
        score_ps = [c.ps[:, 2 * k:2 * k + 2, :].rearrange("p b n -> p (b n)") for k in range(3)]
        turn_ps, u_ps = c.bank(6), c.bank(7)

        q_bias_ready = sem("q_bias")
        loaded, projected, qkv_ready, v_turned, v_ready, setup = (
            sem(n) for n in ("loaded", "projected", "qkv", "v_turned", "v", "setup"))
        s_done, top_ready, exp_ready, turned, et_dve, et_act = (
            sem(n) for n in ("s", "top", "exp", "turned", "et_dve", "et_act"))
        av_done, u_copied, rl_step, rl_turned, rl_copied, spread_done, scaled, y_done, y_copied = (
            sem(n) for n in ("av", "u", "rl_step", "rl_turned", "rl_copied", "spread", "scaled", "y", "y_copied"))
        block = ctx.enter_context(nc.Block())

        def turned_to(x, half):
            t, h = x // 2, x % 2
            return et[t // TPC][:, h, half * TPC:(half + 1) * TPC, (t % TPC) * P:(t % TPC + 1) * P]

        @block.sync
        def _(sp):
            with sp.Fori(0, BATCH) as b:
                with sp.Fori(0, pairs) as hp:
                    n = b * pairs + hp
                    sp.wait_ge(qkv_ready, n * 4)
                    sp.dma_start(w[:, :], weights[hp, :, :]).then_inc(loaded, 16)

        @block.tensor
        def _(pe):
            pe.wait_ge(setup, 5)
            with pe.Fori(0, BATCH) as b:
                with pe.Fori(0, pairs) as hp:
                    n = b * pairs + hp
                    pe.wait_ge(loaded, n * 16 + 16)
                    pe.wait_ge(scaled, n)
                    pe.wait_ge(y_copied, b * 2)
                    for r in range(3):
                        for half in range(2):
                            mm = pe.matmul(c.bank(2 * r + half), w[:, r * P:(r + 1) * P],
                                           c.xt[:, bass.ds(b * SEQ + half * BANK, BANK)], start=True, stop=True)
                        mm.then_inc(projected, 1)

                    def scores(x, half):
                        t, h = x // 2, x % 2
                        if half == 0 and x >= 3:
                            pe.wait_ge(exp_ready, n * units + x - 2)
                        mm = pe.matmul(score_ps[x % 3][:, half * BANK:(half + 1) * BANK], qt[h][:, t * P:(t + 1) * P],
                                       kt[:, half * BANK:(half + 1) * BANK], start=True, stop=True)
                        if half:
                            mm.then_inc(s_done, 1)

                    def turn(x, half):
                        t, h = x // 2, x % 2
                        if half == 0:
                            pe.wait_ge(exp_ready, n * units + x + 1)
                        if h == half:
                            pe.wait_ge(et_act, n * units + 2 * t + h)
                        else:
                            pe.wait_ge(et_dve, n * units + 2 * t + 1 + h)
                        for j in range(TPC):
                            k = half * TPC + j
                            mm = pe.transpose(turn_ps[:, j * P:(j + 1) * P], e[x % 2][:, k * P:(k + 1) * P], c.ident[:, :])
                        mm.then_inc(turned, 1)

                    def attend(half):
                        pe.wait_ge(et_dve, n * units + 8 * half + 8)
                        pe.wait_ge(et_act, n * units + 8 * half + 8)
                        pe.wait_ge(u_copied, n * 2 + half)
                        for t in range(TPB):
                            for h in range(2):
                                mm = pe.matmul(u_ps[dh * h:dh * h + dh, :], v[:, t, dh * h:dh * h + dh],
                                               et[half][:, h, t, :], start=(t == 0), stop=(t == TPB - 1))
                        mm.then_inc(av_done, 1)

                    pe.wait_ge(qkv_ready, n * 4 + 3)
                    for x in range(2):
                        for half in range(2):
                            scores(x, half)
                    pe.wait_ge(qkv_ready, n * 4 + 4)
                    for half in range(2):
                        pe.wait_ge(v_ready, n * 2 + half)
                        pe.wait_ge(rl_copied, n)
                        for j in range(TPC):
                            t = half * TPC + j
                            mm = pe.transpose(turn_ps[:, j * P:(j + 1) * P], vt[:, t * P:(t + 1) * P], c.ident[:, :])
                        mm.then_inc(v_turned, 1)
                    pe.wait_ge(v_ready, n * 2 + 2)
                    for x in range(units):
                        for half in range(2):
                            if x + 2 < units:
                                scores(x + 2, half)
                            turn(x, half)
                        if x == units // 2 + 1:
                            attend(0)
                    attend(1)
                    pe.wait_ge(rl_step, n * 6 + 6)
                    for t in range(TPB):
                        mm = pe.transpose(turn_ps.bitcast(BF16)[:, t * P:(t + 1) * P], rl3[:, t, :], c.ident_bf[:, :])
                    mm.then_inc(rl_turned, 1)
                    pe.wait_ge(rl_copied, n + 1)
                    for half in range(2):
                        mm = pe.matmul(score_ps[0][:, half * BANK:(half + 1) * BANK], spread[:, :],
                                       rl3_t[:, half * BANK:(half + 1) * BANK], start=True, stop=True)
                    mm.then_inc(spread_done, 1)
                pe.wait_ge(scaled, b * pairs + pairs)
                for t in range(TPB):
                    out = score_ps[0][:, t * P:(t + 1) * P]
                    for k in range(pairs):
                        pe.matmul(out, ot[:, k, t * P:(t + 1) * P], w_out[:, k, :], start=(k == 0), stop=False)
                    mm = pe.matmul(out, c.ones_row[:, :], b_out[:, :], start=False, stop=True)
                    if t % TPC == TPC - 1:
                        mm.then_inc(y_done, 1)

        @block.scalar
        def _(act):
            with act.Fori(0, BATCH) as b:
                with act.Fori(0, pairs) as hp:
                    n = b * pairs + hp
                    act.wait_ge(loaded, n * 16 + 16)
                    act.mul(q_bias[:, :], w[:, 3 * P:3 * P + 1], scale).then_inc(q_bias_ready, 1)
                    act.wait_ge(q_bias_ready, n + 1)
                    act.wait_ge(setup, 5)
                    for h in range(2):
                        rows = slice(dh * h, dh * h + dh)
                        act.wait_ge(projected, n * 3 + 1)
                        act.activation(qt[h][rows, :], score_ps[0][rows, :], ACT.Identity, scale=scale,
                                       bias=q_bias[rows, 0:1]).then_inc(qkv_ready, 1)
                    for j, dst in ((1, kt), (2, vt)):
                        act.wait_ge(projected, n * 3 + j + 1)
                        act.activation(dst[:, :], score_ps[j], ACT.Identity,
                                       bias=w[:, 3 * P + j:3 * P + j + 1]).then_inc(qkv_ready, 1)

                    def exponentials(x):
                        t, h = x // 2, x % 2
                        act.wait_ge(top_ready, n * units + x + 1)
                        act.wait_ge(turned, n * units * 2 + 2 * max(x - 1, 0))
                        act.activation(e[x % 2][:, :], score_ps[x % 3], ACT.Exp, bias=minus_top[:, t, h:h + 1],
                                       accum_out=l[:, t, h:h + 1]).then_inc(exp_ready, 1)

                    act.wait_ge(rl_step, n * 6)
                    exponentials(0)
                    for x in range(units):
                        if x + 1 < units:
                            exponentials(x + 1)
                        if x % 2:
                            act.wait_ge(av_done, n * 2)
                            for half in range(2):
                                act.wait_ge(turned, n * units * 2 + 2 * x + half + 1)
                                act.copy(turned_to(x, half), turn_ps.rearrange("p (k i) -> p k i", k=TPC)).then_inc(et_act, 1)

        @block.vector
        def _(dve):
            dve.memset(rl3[:, :, :], 0.0).then_inc(setup, 1)
            dve.memset(spread[:, :], 0.0).then_inc(setup, 1)
            dve.wait_ge(setup, 2)
            for h in range(2):
                op = dve.memset(spread[dh * h:dh * h + 3, dh * h:dh * h + dh], 1.0)
            op.then_inc(setup, 1)
            for h in range(2):
                dve.memset(qt[h][dh * (1 - h):dh * (2 - h), :], 0.0).then_inc(setup, 1)
            with dve.Fori(0, BATCH) as b:
                with dve.Fori(0, pairs) as hp:
                    n = b * pairs + hp

                    def maxima(x):
                        dve.wait_ge(s_done, n * units + x + 1)
                        dve.tensor_reduce(minus_top[:, x // 2, x % 2:x % 2 + 1], score_ps[x % 3], AX.X, ALU.max,
                                          negate=True).then_inc(top_ready, 1)

                    def copy_u(half):
                        dve.wait_ge(av_done, n * 2 + half + 1)
                        dve.tensor_copy(u[:, half * BANK:(half + 1) * BANK], u_ps).then_inc(u_copied, 1)

                    maxima(0)
                    for half in range(2):
                        dve.wait_ge(v_turned, n * 2 + half + 1)
                        dve.tensor_copy(v[:, half * TPC:(half + 1) * TPC, :].rearrange("p t d -> p (t d)"),
                                        turn_ps).then_inc(v_ready, 1)
                    for x in range(units):
                        if x + 1 < units:
                            maxima(x + 1)
                        if x % 2 == 0:
                            dve.wait_ge(av_done, n * 2)
                            for half in range(2):
                                dve.wait_ge(turned, n * units * 2 + 2 * x + half + 1)
                                dve.tensor_copy(turned_to(x, half),
                                                turn_ps.rearrange("p (k i) -> p k i", k=TPC)).then_inc(et_dve, 1)
                        if x == units // 2 + 3:
                            copy_u(0)
                    dve.wait_ge(exp_ready, n * units + units)
                    dve.reciprocal(l[:, :, :], l[:, :, :]).then_inc(rl_step, 1)
                    dve.wait_ge(rl_step, n * 6 + 1)
                    heads = rl3[:, :, :].rearrange("p t (h k) -> p t h k", h=2)
                    split_in_three(dve, [heads[:, :, :, k] for k in range(3)], rest[:, :, :], l[:, :, :],
                                   rl_step, n * 6 + 1)
                    copy_u(1)
                    dve.wait_ge(rl_turned, n + 1)
                    dve.tensor_copy(rl3_t[:, :], turn_ps.bitcast(BF16)).then_inc(rl_copied, 1)
                    dve.wait_ge(u_copied, n * 2 + 2)
                    dve.wait_ge(y_done, b * 2)
                    dve.wait_ge(spread_done, n + 1)
                    dve.tensor_tensor(ot[:, hp, :], score_ps[0], u[:, :], ALU.mult).then_inc(scaled, 1)
                for k in range(2):
                    dve.wait_ge(y_done, b * 2 + k + 1)
                    dve.tensor_copy(y[:, bass.ds(b * TPB + k * TPC, TPC), :].rearrange("p t d -> p (t d)"),
                                    c.bank(k)).then_inc(y_copied, 1)


def add_normed(nc, c, y, gain, shift):
    with ExitStack() as ctx:
        step = c.semaphore("post_step")
        block = ctx.enter_context(nc.Block())

        @block.vector
        def _(dve):
            every = [P, TILES, D]
            dve.tensor_tensor(y[:, :, :], y[:, :, :], gain[:, :].unsqueeze(1).to_broadcast(every), ALU.mult).then_inc(step, 1)
            dve.tensor_tensor(c.xn[:, :, :], c.xn[:, :, :], shift[:, :].unsqueeze(1).to_broadcast(every), ALU.add).then_inc(step, 1)
            dve.wait_ge(step, 2)
            dve.tensor_tensor(y[:, :, :], y[:, :, :], c.xn[:, :, :], ALU.add).then_inc(step, 1)
            dve.wait_ge(step, 3)
            dve.scalar_tensor_tensor(c.x[:, :, :], y[:, :, :], 2 ** -0.5, c.x[:, :, :], ALU.mult, ALU.add)


def quantise_fp4(dve, act, src, dst, blocks, bufs, step, signs_ready, at, n):
    views = {k: b[:, 0:blocks * 16].rearrange("p (b k) -> p b k", k=16) for k, b in bufs.items() if k != "scale"}
    scale, inv = bufs["scale"][:, 0, 0:blocks], bufs["scale"][:, 1, 0:blocks]
    signs, size, big, small = views["signs"], views["size"], views["big"], views["small"]
    if act is not None:
        act.wait_ge(step, at + 1)
        act.activation(signs, src, ACT.Sign).then_inc(signs_ready, 1)
        act.wait_ge(step, at + 4)
        act.activation(size, size, ACT.Abs).then_inc(signs_ready, 1)
        return
    every = [P, blocks, 16]

    def per_block(a):
        return a.rearrange("p (b o) -> p b o", o=1).to_broadcast(every)

    dve.tensor_reduce(scale, src, AX.X, ALU.max, apply_absolute_value=True).then_inc(step, 1)
    dve.wait_ge(step, at + 1)
    dve.tensor_scalar(scale, scale, 1.0 / 6.0, 1e-12, ALU.mult, ALU.max).then_inc(step, 1)
    dve.wait_ge(step, at + 2)
    dve.reciprocal(inv, scale).then_inc(step, 1)
    dve.wait_ge(step, at + 3)
    dve.tensor_tensor(size, src, per_block(inv), ALU.mult).then_inc(step, 1)
    dve.wait_ge(signs_ready, 2 * n + 2)
    dve.tensor_scalar(big, size, 5.0, 2.0, ALU.is_gt, ALU.mult).then_inc(step, 1)
    dve.tensor_scalar(small, size, 1.75, None, ALU.is_gt).then_inc(step, 1)
    now = at + 6
    for chain, mids in ((big, (3.5, 2.5)), (small, (1.25, 0.75, 0.25))):
        for mid in mids:
            dve.wait_ge(step, now)
            dve.scalar_tensor_tensor(chain, size, mid, chain, ALU.is_gt, ALU.add).then_inc(step, 1)
            now += 1
    dve.wait_ge(step, now)
    dve.scalar_tensor_tensor(small, big, 2.0, small, ALU.mult, ALU.add).then_inc(step, 1)
    dve.wait_ge(step, now + 1)
    dve.scalar_tensor_tensor(small, small, 0.5, signs, ALU.mult, ALU.mult).then_inc(step, 1)
    dve.wait_ge(step, now + 2)
    dve.tensor_tensor(dst, small, per_block(scale), ALU.mult).then_inc(step, 1)


FP4_STEPS = 14


def fp4_mlp(nc, c, w):
    hidden = 352
    tiles_h = 3
    width = [min(P, hidden - f * P) for f in range(tiles_h)]
    gate_at, up_at, down_at = 0, tiles_h * P, 2 * tiles_h * P
    total = down_at + hidden
    with ExitStack() as ctx:
        def sem(what):
            return c.semaphore(f"fp4_{what}")

        def sb(what, shape):
            return c.sbuf(ctx, f"fp4_{what}", shape)

        bufs = {k: sb(k, [P, TOKENS]) for k in ("signs", "size", "big", "small")}
        bufs["scale"] = sb("scale", [P, 2, P])
        wt = sb("wt", [P, 2, tiles_h * P])
        down = sb("down", [P, tiles_h, P])
        gated = [sb(f"gated{k}", [P, hidden]) for k in range(2)]
        h = [sb(f"h{k}", [P, TPC, hidden]) for k in range(2)]
        ht = sb("ht", [P, tiles_h, BANK])
        step, signs, turned, copied = sem("step"), sem("signs"), sem("turned"), sem("copied")
        gate_done, up_done, gate_act, h_ready = sem("gate"), sem("up"), sem("gate_act"), sem("h")
        h_turned, ht_ready, y_done, added = sem("h_turned"), sem("ht"), sem("y"), sem("added")
        block = ctx.enter_context(nc.Block())

        def blocked(ap):
            return ap.rearrange("p (b k) -> p b k", k=16)

        w_in = blocked(w[:, :])
        x_in = blocked(c.xn[:, :, :].rearrange("p t d -> p (t d)"))

        def jobs(g):
            if g == 0:
                return w_in, w_in, total // 16
            if g == 1:
                return x_in, x_in, TOKENS // 16
            hh = h[g % 2][:, :, :].rearrange("p t f -> p (t f)")
            return blocked(hh), blocked(hh), TPC * hidden // 16

        @block.tensor
        def _(pe):
            pe.wait_ge(step, FP4_STEPS)
            for f in range(tiles_h):
                for which, at in enumerate((gate_at, up_at)):
                    pe.transpose(c.bank(which)[:, f * P:(f + 1) * P], w[:, at + f * P:at + (f + 1) * P], c.ident[:, :])
                mm = pe.transpose(c.bank(2)[0:width[f], f * P:(f + 1) * P],
                                  w[:, down_at + f * P:down_at + f * P + width[f]], c.ident[:, :])
            mm.then_inc(turned, 1)
            pe.wait_ge(step, 2 * FP4_STEPS)
            for t in range(TILES):
                mm = pe.transpose(c.bank(4 + t // TPC)[:, t % TPC * P:(t % TPC + 1) * P], c.xn[:, t, :], c.ident[:, :])
                if t % TPC == TPC - 1:
                    mm.then_inc(turned, 1)
            pe.wait_ge(copied, 3 + CHUNKS)

            def tail(g):
                pe.wait_ge(step, (3 + g) * FP4_STEPS)
                wait_from(pe, ht_ready, tiles_h * g)
                for f in range(tiles_h):
                    for j in range(TPC):
                        mm = pe.transpose(c.bank(4 + f)[0:width[f], j * P:(j + 1) * P],
                                          h[g % 2][:, j, f * P:f * P + width[f]], c.ident[:, :])
                    mm.then_inc(h_turned, 1)
                wait_from(pe, added, g)
                pe.wait_ge(ht_ready, tiles_h * (g + 1))
                for j in range(TPC):
                    for f in range(tiles_h):
                        mm = pe.matmul(c.bank(7)[:, j * P:(j + 1) * P], ht[0:width[f], f, j * P:(j + 1) * P],
                                       down[0:width[f], f, :], start=(f == 0), stop=(f == tiles_h - 1))
                mm.then_inc(y_done, 1)

            for g in range(CHUNKS):
                for j in range(TPC):
                    t = g * TPC + j
                    wait_from(pe, gate_act, t - 1)
                    pe.matmul(c.bank(t % 2)[:, 0:hidden], c.xt[:, t * P:(t + 1) * P], wt[:, 0, 0:hidden],
                              start=True, stop=True).then_inc(gate_done, 1)
                    wait_from(pe, h_ready, t - 1)
                    pe.matmul(c.bank(2 + t % 2)[:, 0:hidden], c.xt[:, t * P:(t + 1) * P], wt[:, 1, 0:hidden],
                              start=True, stop=True).then_inc(up_done, 1)
                if g:
                    tail(g - 1)
            tail(CHUNKS - 1)

        @block.scalar
        def _(act):
            def signs_of(n):
                src, dst, blocks = jobs(n)
                quantise_fp4(None, act, src, dst, blocks, bufs, step, signs, n * FP4_STEPS, n)

            def gates(g):
                for j in range(TPC):
                    t = g * TPC + j
                    act.wait_ge(gate_done, t + 1)
                    wait_from(act, h_ready, t - 1)
                    act.activation(gated[t % 2][:, :], c.bank(t % 2)[:, 0:hidden], ACT.Silu).then_inc(gate_act, 1)

            signs_of(0)
            act.wait_ge(turned, 1)
            act.copy(wt[:, 0, :], c.bank(0)[:, 0:tiles_h * P]).then_inc(copied, 1)
            act.copy(wt[:, 1, :], c.bank(1)[:, 0:tiles_h * P]).then_inc(copied, 1)
            signs_of(1)
            for g in range(CHUNKS):
                act.wait_ge(turned, 2 + g)
                act.copy(c.xt[:, g * BANK:(g + 1) * BANK], c.bank(4 + g)).then_inc(copied, 1)
            gates(0)
            for g in range(CHUNKS):
                signs_of(g + 2)
                if g + 1 < CHUNKS:
                    gates(g + 1)
                wait_from(act, y_done, g)
                for f in range(tiles_h):
                    act.wait_ge(h_turned, tiles_h * g + f + 1)
                    act.copy(ht[0:width[f], f, :], c.bank(4 + f)[0:width[f], :]).then_inc(ht_ready, 1)

        @block.vector
        def _(dve):
            def products(g):
                wait_from(dve, h_turned, tiles_h * (g - 1))
                for j in range(TPC):
                    t = g * TPC + j
                    dve.wait_ge(gate_act, t + 1)
                    dve.wait_ge(up_done, t + 1)
                    dve.tensor_tensor(h[g % 2][:, j, :], c.bank(2 + t % 2)[:, 0:hidden], gated[t % 2][:, :],
                                      ALU.mult).then_inc(h_ready, 1)
            def quantise(n):
                src, dst, blocks = jobs(n)
                quantise_fp4(dve, None, src, dst, blocks, bufs, step, signs, n * FP4_STEPS, n)

            def add(g):
                dve.wait_ge(y_done, g + 1)
                x = c.x[:, g * TPC:(g + 1) * TPC, :].rearrange("p t d -> p (t d)")
                dve.tensor_tensor(x, x, c.bank(7), ALU.add).then_inc(added, 1)

            quantise(0)
            dve.wait_ge(turned, 1)
            for f in range(tiles_h):
                op = dve.tensor_copy(down[0:width[f], f, :], c.bank(2)[0:width[f], f * P:(f + 1) * P])
            op.then_inc(copied, 1)
            quantise(1)
            products(0)
            for g in range(CHUNKS):
                dve.wait_ge(h_ready, TPC * (g + 1))
                wait_from(dve, step, (g + 2) * FP4_STEPS)
                quantise(g + 2)
                if g + 1 < CHUNKS:
                    products(g + 1)
                if g:
                    add(g - 1)
            add(CHUNKS - 1)


HEADS, DH = 16, 8
NARROW = BATCH * HEADS
SCALE = DH ** -0.5
BLK = 64
NBLK = SEQ // BLK
FAR = -1e30
MASK_ROW, TOP_ROW = 64, 96
Q_PARTS, K_PARTS = (0, 0, 0, 1, 1, 2), (0, 1, 2, 0, 1, 0)


def narrow_prepare(nc, c, w, tables, q_stack, k_stack, v, diag):
    rotated = tables is not None
    with ExitStack() as ctx:
        def sem(what):
            return c.semaphore(f"{'rot' if rotated else 'blk'}_{what}")

        def sb(what, shape, dt=F32):
            return c.sbuf(ctx, f"prep_{'rot' if rotated else 'blk'}_{what}", shape, dt)

        full = [sb(f"full{k}", [P, BANK]) for k in range(2)]
        parts = [[sb(f"parts{k}{s}", [P, 3, BANK], BF16) for s in range(2)] for k in range(2)]
        rest = [sb(f"rest{k}", [P, BANK]) for k in range(2)]
        scratch = [nc.dram_tensor(f"parts_{'rot' if rotated else 'blk'}{k}", (D, 3, TOKENS), BF16, kind="Internal")
                   for k in range(2)]
        if rotated:
            cos, sin, bias, v_bias = tables
            turned_part = sb("turned", [P, BANK])
        else:
            onehot, headsel, q_tok = sb("onehot", [P, SEQ]), sb("headsel", [P, HEADS]), sb("q_tok", [P, BANK])
            sums, ksum, qsum_heads = sb("sums", [P, 2, NBLK]), sb("ksum", [P, P]), sb("qsum_heads", [P, HEADS, NBLK])
            masks = sb("masks", [P, HEADS * NBLK])
        cleared, projected, full_ready, rope_step = sem("cleared"), sem("projected"), sem("full"), sem("rope")
        split = [sem("q_split"), sem("k_split")]
        written = [[sem(f"written{k}{s}") for s in range(2)] for k in range(2)]
        stacked, v_ready, tok_ready, diag_step = sem("stacked"), sem("v"), sem("tok"), sem("diag")
        sums_ready, mask_done, mask_step, mask_rows, const, hot = (
            sem("sums"), sem("mask_done"), sem("mask_step"), sem("mask_rows"), sem("const"), sem("hot"))
        stacked_dma, hot_copied = sem("stacked_dma"), sem("hot_copied")
        all_cleared = 3 if rotated else 4
        block = ctx.enter_context(nc.Block())

        @block.tensor
        def _(pe):
            for g in range(CHUNKS):
                x = c.xt[:, g * BANK:(g + 1) * BANK]
                for k in range(2):
                    wait_from(pe, full_ready, 2 * (g - 1) + k + 1)
                    if rotated:
                        pe.matmul(c.bank(2 * k), w[:, 2 * k * P:(2 * k + 1) * P], x, start=True, stop=True)
                        pe.matmul(c.bank(2 * k + 1), w[:, (2 * k + 1) * P:(2 * k + 2) * P], x,
                                  start=True, stop=True).then_inc(projected, 1)
                    else:
                        pe.matmul(c.bank(2 * k), w[:, k * P:(k + 1) * P], x, start=True, stop=True).then_inc(projected, 1)
                wait_from(pe, v_ready, g)
                wait_from(pe, tok_ready, g if not rotated else 0)
                wait_from(pe, diag_step, 2 * g - 1 if not rotated else 0)
                at = 4 * P if rotated else 2 * P
                for j in range(TPC):
                    t = g * TPC + j
                    cols = slice(j * P, (j + 1) * P)
                    mm = pe.matmul(c.bank(4)[:, cols], c.xt[:, t * P:(t + 1) * P], w[:, at:at + P],
                                   start=True, stop=not rotated)
                    if rotated:
                        mm = pe.matmul(c.bank(4)[:, cols], c.ones_row[:, :], v_bias[:, :], start=False, stop=True)
                    else:
                        for k in range(2):
                            mm = pe.matmul(c.bank(6 + k)[:, cols], c.xt[:, t * P:(t + 1) * P],
                                           w[:, k * P:(k + 1) * P], start=True, stop=True)
                mm.then_inc(projected, 1)
                if not rotated and g % 2:
                    pe.wait_ge(mask_step, g // 2 * 4 + 2)
                    pe.matmul(c.bank(1)[:, 0:HEADS * NBLK], ksum[:, :], qsum_heads[:, :, :].rearrange("p h b -> p (h b)"),
                              start=True, stop=True).then_inc(mask_done, 1)

        @block.scalar
        def _(act):
            act.wait_ge(cleared, all_cleared)
            if not rotated:
                act.wait_ge(const, 32)
                act.copy(k_stack[MASK_ROW:MASK_ROW + NBLK, 0, :], onehot[MASK_ROW:MASK_ROW + NBLK, :]).then_inc(hot, 1)
                act.wait_ge(hot, 1)
                rest_of = [NBLK, NARROW - 1, SEQ]
                act.dma_start(k_stack[MASK_ROW:MASK_ROW + NBLK, 1:NARROW, :],
                              k_stack[MASK_ROW:MASK_ROW + NBLK, 0:1, :].to_broadcast(rest_of)).then_inc(hot_copied, 16)
            for g in range(CHUNKS):
                b, t0 = g // 2, g % 2 * TPC
                if not rotated:
                    for k in range(2):
                        act.wait_ge(projected, 3 * g + k + 1)
                        wait_from(act, split[k], 5 * g)
                        wait_from(act, sums_ready, 2 * (g - 1) + k + 1)
                        act.copy(full[k][:, :], c.bank(2 * k)).then_inc(full_ready, 1)
                act.wait_ge(projected, 3 * g + 3)
                values = c.bank(4).rearrange("p (t h d) -> p h t d", t=TPC, h=HEADS)
                heads = slice(b * HEADS, (b + 1) * HEADS)
                if rotated:
                    act.copy(v[:, heads, t0:t0 + TPC, 0:DH], values).then_inc(v_ready, 1)
                else:
                    wait_from(act, diag_step, 2 * (g - 1) + 1)
                    act.copy(q_tok[:, :], c.bank(6)).then_inc(tok_ready, 1)
                    for s in range(2):
                        rows = slice(s * BLK, (s + 1) * BLK)
                        op = act.copy(v[rows, heads, t0:t0 + TPC, s * DH:(s + 1) * DH], values[rows])
                    op.then_inc(v_ready, 1)
                    if g % 2:
                        rows = slice(MASK_ROW, MASK_ROW + NBLK)
                        act.wait_ge(mask_step, g // 2 * 4 + 4)
                        act.copy(q_stack[rows, heads, :].rearrange("p h (b i) -> p (h b) i", i=BLK),
                                 masks[rows, :].rearrange("p (n o) -> p n o", o=1).to_broadcast([NBLK, HEADS * NBLK, BLK])).then_inc(mask_rows, 1)
            if not rotated:
                act.wait_ge(hot_copied, 16)

        @block.vector
        def _(dve):
            dve.memset(q_stack[:, :, :].rearrange("p n i -> p (n i)").bitcast(F32), 0.0).then_inc(cleared, 1)
            if not rotated:
                dve.memset(ksum[:, :], 0.0).then_inc(cleared, 1)
                dve.wait_ge(cleared, all_cleared)
                dve.wait_ge(const, 32)
            for g in range(CHUNKS):
                b, s = g // 2, g % 2
                pos = slice(s * BANK, (s + 1) * BANK)
                if rotated:
                    for k in range(2):
                        n = 2 * g + k
                        dve.wait_ge(projected, 3 * g + k + 1)
                        wait_from(dve, rope_step, 3 * n)
                        wait_from(dve, split[k], 5 * g)
                        dve.scalar_tensor_tensor(full[k][:, :], c.bank(2 * k), bias[:, 2 * k:2 * k + 1], cos[:, pos],
                                                 ALU.add, ALU.mult).then_inc(rope_step, 1)
                        dve.scalar_tensor_tensor(turned_part[:, :], c.bank(2 * k + 1), bias[:, 2 * k + 1:2 * k + 2],
                                                 sin[:, pos], ALU.add, ALU.mult).then_inc(rope_step, 1)
                        dve.wait_ge(rope_step, 3 * n + 2)
                        dve.tensor_tensor(full[k][:, :], full[k][:, :], turned_part[:, :], ALU.add).then_inc(rope_step, 1)
                        dve.wait_ge(rope_step, 3 * n + 3)
                        dve.sem_inc(full_ready, 1)
                dve.wait_ge(full_ready, 2 * g + 1)
                wait_from(dve, written[0][s], 16 * b)
                split_in_three(dve, [parts[0][s][:, k, :] for k in range(3)], rest[0][:, :], full[0][:, :], split[0], 5 * g)
                if not rotated:
                    dve.wait_ge(full_ready, 2 * g + 2)
                    wait_from(dve, mask_step, 4 * b)
                    for k in range(2):
                        out = sums[:, k, s * NBLK // 2:(s + 1) * NBLK // 2]
                        dve.tensor_reduce(out, full[k][:, :].rearrange("p (b i) -> p b i", i=BLK), AX.X,
                                          ALU.add).then_inc(sums_ready, 1)
                    dve.wait_ge(tok_ready, g + 1)
                    dve.wait_ge(split[0], 5 * g + 5)
                    dve.tensor_tensor(rest[0][:, :], c.bank(7), q_tok[:, :], ALU.mult).then_inc(diag_step, 1)
                    dve.wait_ge(diag_step, 2 * g + 1)
                    dve.tensor_reduce(diag[:, b * HEADS:(b + 1) * HEADS, s * TPC:(s + 1) * TPC],
                                      rest[0][:, :].rearrange("p (t h d) -> p h t d", t=TPC, h=HEADS), AX.X,
                                      ALU.add).then_inc(diag_step, 1)
                    if s:
                        dve.wait_ge(sums_ready, 2 * g + 2)
                        dve.tensor_copy(ksum[:, MASK_ROW:MASK_ROW + NBLK], sums[:, 1, :]).then_inc(mask_step, 1)
                        shape = [P, HEADS, NBLK]
                        dve.tensor_tensor(qsum_heads[:, :, :], sums[:, 0:1, :].to_broadcast(shape),
                                          headsel[:, :].rearrange("p (h o) -> p h o", o=1).to_broadcast(shape),
                                          ALU.mult).then_inc(mask_step, 1)
                        rows = slice(MASK_ROW, MASK_ROW + NBLK)
                        dve.wait_ge(mask_done, b + 1)
                        wait_from(dve, mask_rows, b)
                        dve.tensor_scalar(masks[rows, :], c.bank(1)[rows, 0:HEADS * NBLK], SCALE / BLK ** 2, 0.01,
                                          ALU.mult, ALU.is_le).then_inc(mask_step, 1)
                        dve.wait_ge(mask_step, b * 4 + 3)
                        dve.tensor_scalar(masks[rows, :], masks[rows, :], FAR, None, ALU.mult).then_inc(mask_step, 1)

        @block.gpsimd
        def _(pool):
            width = v.shape[3]
            flat = k_stack[:, :, :].rearrange("p n i -> p (n i)").bitcast(F32)
            pool.memset(v[:, :, :, :].rearrange("p n t d -> p (n t d)"), 0.0).then_inc(stacked, 1)
            pool.wait_ge(stacked, 1)
            pool.memset(v[:, :, :, width - 1:width], 1.0).then_inc(cleared, 1)
            pool.memset(flat, 0.0).then_inc(cleared, 1)
            pool.wait_ge(cleared, all_cleared)
            pool.memset(k_stack[TOP_ROW:TOP_ROW + 3, :, :].rearrange("p n i -> p (n i)"), -1.0).then_inc(stacked, 1)
            pool.wait_ge(stacked, 2)
            for g in range(CHUNKS):
                pool.wait_ge(full_ready, 2 * g + 2)
                wait_from(pool, written[1][g % 2], 16 * (g // 2))
                split_in_three(pool, [parts[1][g % 2][:, k, :] for k in range(3)], rest[1][:, :], full[1][:, :],
                               split[1], 5 * g)

        @block.sync
        def _(sp):
            if not rotated:
                sp.dma_start(onehot[MASK_ROW:MASK_ROW + NBLK, :], c.ins["l2a_onehot"]).then_inc(const, 16)
                sp.dma_start(headsel[:, :], c.ins["l2a_headsel"]).then_inc(const, 16)
            for g in range(CHUNKS):
                for k in range(2):
                    sp.wait_ge(split[k], 5 * g + 5)
                    sp.dma_start(scratch[k][:, :, g * BANK:(g + 1) * BANK], parts[k][g % 2][:, :, :]).then_inc(written[k][g % 2], 16)
                if g % 2:
                    b = g // 2
                    sp.wait_ge(cleared, all_cleared)
                    for k, (which, stack) in enumerate(((Q_PARTS, q_stack), (K_PARTS, k_stack))):
                        for s in range(2):
                            sp.wait_ge(written[k][s], 16 * (b + 1))
                        for r in range(6):
                            src = scratch[k][:, which[r], b * SEQ:(b + 1) * SEQ].rearrange("(h d) t -> d h t", d=DH)
                            sp.dma_start(stack[r * DH:(r + 1) * DH, b * HEADS:(b + 1) * HEADS, :], src).then_inc(stacked_dma, 16)
            sp.wait_ge(stacked_dma, 16 * 12 * BATCH)


def narrow_attention(nc, c, causal, q_stack, k_stack, v, diag, raw, w_out, b_out):
    name = "cau" if causal else "blm"
    threshold = 0.01
    cols = v.shape[3]
    u_cols = cols if causal else TPB * cols
    if causal:
        first_units = [(t, lo, min((t + 1) * P, lo + BANK)) for t in range(TPB) for lo in range(0, (t + 1) * P, BANK)]
        second_units = [(iq, j, min(j + 4, 2 * iq + 2)) for iq in range(4) for j in range(0, 2 * iq + 2, 4)]
    else:
        first_units = [(t, lo, lo + BANK) for t in range(TPB) for lo in (0, BANK)]
        second_units = [(iq, j, j + 4) for iq in range(4) for j in (0, 4)]
    P1, P2 = len(first_units), len(second_units)
    last_of = [max(w for w, u in enumerate(second_units) if u[0] == iq) for iq in range(4)]
    with ExitStack() as ctx:
        def sem(what):
            return c.semaphore(f"{name}_{what}")

        def sb(what, shape, dt=F32):
            return c.sbuf(ctx, f"{name}_{what}", shape, dt)

        o = c.xn[:, :, :].rearrange("p t d -> p (t d)").rearrange("p (n t d) -> p n t d", n=NARROW, t=TPB)
        e = [c.xt[:, :].rearrange("p (j i) -> p j i", j=TPB), sb("e", [P, TPB, 2 * P])[:, :, :]]
        u = [sb(f"u{k}", [P, TPB, u_cols]) for k in range(2)]
        tops = sb("tops", [P, TPB, 2 if causal else NBLK])
        top, top_rest = sb("top", [P, TPB]), sb("top_rest", [P, TPB])
        top3 = sb("top3", [P, TPB, P], BF16)
        l = sb("l", [P, TPB])
        ot = sb("ot", [P, BANK])
        if causal:
            masks = sb("masks", [P, 5 * P], BF16)
        else:
            diff = [sb(f"diff{k}", [P, TPB, NBLK + 1]) for k in range(2)]
            on = [sb(f"on{k}", [P, TPB]) for k in range(2)]
            off, keep_own = sb("off", [P, TPB]), sb("keep_own", [P, TPB])
            prob, big = sb("prob", [P, TPB, NBLK]), sb("big", [P, TPB * NBLK], BF16)
            keep, kept = sb("keep", [P, TPB, NBLK]), sb("kept", [P, TPB * TPB, 2, DH])
            total, own = sb("total", [P, TPB, DH]), sb("own", [P, TPB, DH])
            same_block = sb("same_block", [P, P], BF16)
        first_ps = [c.bank(k) for k in range(2)]
        second_ps = [c.ps[:, 2 + 2 * k:4 + 2 * k, :].rearrange("p b n -> p (b n)") for k in range(2)]
        av_ps, turn_ps = c.bank(6), c.bank(7)

        setup, held, s1_done, maxed, top_step, top_turned, rows_ready = (
            sem(x) for x in ("setup", "held", "s1", "maxed", "top_step", "top_turned", "rows"))
        s2_done, exp_done, av_done, u_copied, near_exp, counted, post = (
            sem(x) for x in ("s2", "exp", "av", "u", "near", "counted", "post"))
        regrouped, o_turned, ot_ready, y_done, added = (sem(x) for x in ("regrouped", "o_turned", "ot", "y", "added"))
        TOP_STEPS = 6 if causal else 11
        POST_A, POST_B = (3, 0) if causal else (7, 9)
        POST = POST_A + POST_B
        block = ctx.enter_context(nc.Block())

        def each_head(eng, body):
            body(0, 0, True)
            with eng.Fori(0, NARROW // 2 - 1) as i:
                body(i * 2 + 1, 1, True)
                body(i * 2 + 2, 0, True)
            body(NARROW - 1, 1, False)

        @block.tensor
        def _(pe):
            def first(n, x):
                t, lo, hi = first_units[x]
                out = first_ps[x % 2]
                wait_from(pe, maxed, n * P1 + x - 1)
                pe.sem_inc(held, 1)
                q = q_stack[:, bass.ds(n, 1), t * P:(t + 1) * P].rearrange("p o i -> p (o i)")

                def keys(a, b):
                    return k_stack[:, bass.ds(n, 1), a:b].rearrange("p o i -> p (o i)")
                if causal and hi == (t + 1) * P:
                    if hi - P > lo:
                        pe.matmul(out[:, 0:hi - P - lo], q, keys(lo, hi - P), start=True, stop=True)
                    pe.matmul(out[:, hi - P - lo:hi - lo], q, keys(hi - P, hi), start=True, stop=False)
                    mm = pe.matmul(out[:, hi - P - lo:hi - lo], c.ident_bf[:, :], masks[:, 0:P], start=False, stop=True)
                else:
                    mm = pe.matmul(out[:, 0:hi - lo], q, keys(lo, hi), start=True, stop=True)
                mm.then_inc(s1_done, 1)

            def second(n, x):
                iq, j0, j1 = second_units[x]
                wait_from(pe, exp_done, n * P2 + x - 1)
                pe.sem_inc(held, 1)
                q = q_stack[:, bass.ds(n, 1), iq * 2 * P:(iq + 1) * 2 * P].rearrange("p o i -> p (o i)")
                for j in range(j0, j1):
                    out = second_ps[x % 2][:, (j - j0) * 2 * P:(j - j0 + 1) * 2 * P]
                    k = k_stack[:, bass.ds(n, 1), j * P:(j + 1) * P].rearrange("p o i -> p (o i)")
                    masked = causal and j >= 2 * iq
                    mm = pe.matmul(out, k, q, start=True, stop=not masked)
                    if masked:
                        at = P + (j - 2 * iq) * 2 * P
                        mm = pe.matmul(out, c.ident_bf[:, :], masks[:, at:at + 2 * P], start=False, stop=True)
                mm.then_inc(s2_done, 1)

            def turn_top(n):
                pe.wait_ge(top_step, (n + 1) * TOP_STEPS)
                wait_from(pe, post, (n - 1) * POST)
                for t in range(TPB):
                    mm = pe.transpose(turn_ps.bitcast(BF16)[:, t * P:(t + 1) * P], top3[:, t, :], c.ident_bf[:, :])
                mm.then_inc(top_turned, 1)

            def attend(n, iq):
                pe.wait_ge(exp_done, n * P2 + last_of[iq] + 1)
                wait_from(pe, u_copied, n * 4 + iq)
                pe.sem_inc(held, 1)
                for i in range(2):
                    tiles = range(2 * iq + i + 1) if causal else range(TPB)
                    for j in tiles:
                        at = i * u_cols + (0 if causal else j * cols)
                        mm = pe.matmul(av_ps[:, at:at + cols], e[iq % 2][:, j, i * P:(i + 1) * P],
                                       v[:, bass.ds(n, 1), j, :].rearrange("p o d -> p (o d)"),
                                       start=(j == 0 or not causal), stop=(j == tiles[-1] or not causal))
                mm.then_inc(av_done, 1)

            def count(n):
                pe.wait_ge(rows_ready, n + 2 if not (isinstance(n, int) and n == NARROW - 1) else n + 1)
                pe.wait_ge(post, n * POST + POST_A)
                pe.matmul(turn_ps[:, 0:TPB * NBLK], same_block[:, :], big[:, :], start=True, stop=True).then_inc(counted, 1)

            pe.wait_ge(setup, 3)
            for x in range(P1):
                first(0, x)

            def step(n, k, more):
                ahead = list(range(P1)) if more else []
                for x in ahead[:2]:
                    first(n + 1, x)
                turn_top(n)
                pe.wait_ge(rows_ready, n + 1)
                ahead = ahead[2:]
                for x in range(P2):
                    second(n, x)
                    for _ in range(2):
                        if ahead:
                            first(n + 1, ahead.pop(0))
                    for iq in range(4):
                        if last_of[iq] + 1 == x:
                            attend(n, iq)
                    if x == 1 and not causal and not (isinstance(n, int) and n == 0):
                        count(n - 1)
                while ahead:
                    first(n + 1, ahead.pop(0))
                attend(n, 3)

            each_head(pe, step)
            if not causal:
                count(NARROW - 1)
            for g in range(CHUNKS):
                if g == 0:
                    pe.wait_ge(regrouped, BATCH)
                wait_from(pe, ot_ready, g)
                for j in range(TPC):
                    t = g * TPC + j
                    mm = pe.transpose(c.bank(0)[:, j * P:(j + 1) * P], c.xt[:, t * P:(t + 1) * P], c.ident[:, :])
                mm.then_inc(o_turned, 1)
                pe.wait_ge(ot_ready, g + 1)
                wait_from(pe, added, g)
                for j in range(TPC):
                    out = c.bank(1)[:, j * P:(j + 1) * P]
                    mm = pe.matmul(out, ot[:, j * P:(j + 1) * P], w_out[:, :], start=True, stop=b_out is None)
                    if b_out is not None:
                        mm = pe.matmul(out, c.ones_row[:, :], b_out[:, :], start=False, stop=True)
                mm.then_inc(y_done, 1)

        @block.scalar
        def _(act):
            def copy_u(n, k, iq):
                act.wait_ge(av_done, n * 4 + iq + 1)
                if iq == 0:
                    wait_from(act, post, (n - 1) * POST)
                act.copy(u[k][:, 2 * iq:2 * iq + 2, :].rearrange("p t c -> p (t c)"),
                         av_ps[:, 0:2 * u_cols]).then_inc(u_copied, 1)

            def step(n, k, more):
                if not causal:
                    act.wait_ge(top_step, (n + 1) * TOP_STEPS)
                    act.activation(diff[k][:, :, :], diff[k][:, :, :], ACT.Exp, scale=SCALE).then_inc(near_exp, 1)
                if not (isinstance(n, int) and n == 0):
                    copy_u(n - 1, 1 - k, 3)
                for x, (iq, j0, j1) in enumerate(second_units):
                    act.wait_ge(s2_done, n * P2 + x + 1)
                    wait_from(act, av_done, n * 4 + iq - 1)
                    act.activation(e[iq % 2][:, j0:j1, :].rearrange("p j i -> p (j i)"),
                                   second_ps[x % 2][:, 0:(j1 - j0) * 2 * P], ACT.Exp, scale=SCALE).then_inc(exp_done, 1)
                    for q in range(3):
                        if last_of[q] + 1 == x:
                            copy_u(n, k, q)

            each_head(act, step)
            copy_u(NARROW - 1, 1, 3)
            for g in range(CHUNKS):
                act.wait_ge(o_turned, g + 1)
                wait_from(act, y_done, g)
                act.copy(ot[:, :], c.bank(0)).then_inc(ot_ready, 1)

        @block.vector
        def _(dve):
            def maxima(n, x):
                t, lo, hi = first_units[x]
                dve.wait_ge(s1_done, n * P1 + x + 1)
                if causal:
                    dve.tensor_reduce(tops[:, t, lo // BANK:lo // BANK + 1], first_ps[x % 2][:, 0:hi - lo], AX.X,
                                      ALU.max).then_inc(maxed, 1)
                else:
                    dve.tensor_reduce(tops[:, t, lo // BLK:hi // BLK], first_ps[x % 2].rearrange("p (b j) -> p b j", j=BLK),
                                      AX.X, ALU.max).then_inc(maxed, 1)

            def tops_of(n, k):
                at = n * TOP_STEPS
                dve.wait_ge(maxed, (n + 1) * P1)
                dve.tensor_reduce(top[:, :], tops[:, :, :], AX.X, ALU.max).then_inc(top_step, 1)
                dve.wait_ge(top_step, at + 1)
                if not causal:
                    own_score = diag[:, bass.ds(n, 1), :].rearrange("p o t -> p (o t)")
                    dve.tensor_tensor(top[:, :], top[:, :], own_score, ALU.max).then_inc(top_step, 1)
                    dve.wait_ge(top_step, at + 2)
                    dve.tensor_tensor(diff[k][:, :, 0:NBLK], tops[:, :, :], per_tile(top, NBLK), ALU.subtract).then_inc(top_step, 1)
                    dve.tensor_tensor(diff[k][:, :, NBLK], own_score, top[:, :], ALU.subtract).then_inc(top_step, 1)
                    flat = tops[:, :, :].rearrange("p t b -> p (t b)")
                    for s in range(2):
                        rows = slice(s * BLK, (s + 1) * BLK)
                        dve.tensor_scalar(on[k][rows, :], flat[rows, s::NBLK + 2], FAR / 2, None, ALU.is_gt).then_inc(top_step, 1)
                    at += 5
                split_in_three(dve, [top3[:, :, TOP_ROW + r] for r in range(3)], top_rest[:, :], top[:, :], top_step, at + 1)

            def rows_of(n):
                dve.wait_ge(top_turned, n + 1)
                rows = slice(TOP_ROW, TOP_ROW + 3)
                dve.tensor_scalar(q_stack[rows, bass.ds(n, 1), :].rearrange("p o i -> p (o i)"),
                                  turn_ps.bitcast(BF16)[rows, :], 1.0, None, ALU.mult).then_inc(rows_ready, 1)

            def per_tile(a, width):
                return a[:, :].rearrange("p (t o) -> p t o", o=1).to_broadcast([P, TPB, width])

            def post_a(n, k):
                at = n * POST
                wait_from(dve, post, at)
                dve.wait_ge(u_copied, n * 4 + 4)
                if causal:
                    dve.tensor_copy(l[:, :], u[k][:, :, DH]).then_inc(post, 1)
                    dve.wait_ge(post, at + 1)
                    dve.reciprocal(l[:, :], l[:, :]).then_inc(post, 1)
                    dve.wait_ge(post, at + 2)
                    dve.tensor_tensor(o[:, bass.ds(n, 1), :, :].rearrange("p o t d -> p (o t) d"), u[k][:, :, 0:DH],
                                      per_tile(l, DH), ALU.mult).then_inc(post, 1)
                    return
                dve.wait_ge(near_exp, n + 1)
                dve.tensor_reduce(l[:, :], u[k][:, :, 2 * DH::cols], AX.X, ALU.add).then_inc(post, 1)
                dve.tensor_scalar(off[:, :], on[k][:, :], -1.0, 1.0, ALU.mult, ALU.add).then_inc(post, 1)
                dve.wait_ge(post, at + 2)
                dve.tensor_tensor(off[:, :], off[:, :], diff[k][:, :, NBLK], ALU.mult).then_inc(post, 1)
                dve.wait_ge(post, at + 3)
                dve.tensor_tensor(l[:, :], l[:, :], off[:, :], ALU.add).then_inc(post, 1)
                dve.wait_ge(post, at + 4)
                dve.reciprocal(l[:, :], l[:, :]).then_inc(post, 1)
                dve.wait_ge(post, at + 5)
                dve.tensor_tensor(prob[:, :, :], diff[k][:, :, 0:NBLK], per_tile(l, NBLK), ALU.mult).then_inc(post, 1)
                dve.wait_ge(post, at + 6)
                dve.tensor_scalar(big[:, :], prob[:, :, :].rearrange("p t b -> p (t b)"), threshold, None,
                                  ALU.is_gt).then_inc(post, 1)

            def post_b(n, k):
                if causal:
                    return
                at = n * POST + POST_A
                dve.wait_ge(counted, n + 1)
                dve.scalar_tensor_tensor(keep[:, :, :], turn_ps[:, 0:TPB * NBLK].rearrange("p (t b) -> p t b", b=NBLK), 0.5,
                                         per_tile(l, NBLK), ALU.is_gt, ALU.mult).then_inc(post, 1)
                dve.wait_ge(post, at + 1)
                every = [P, TPB * TPB, 2, DH]
                sums = u[k][:, :, :].rearrange("p t c -> p (t c)").rearrange("p (m c) -> p m c", c=cols)[:, :, 0:2 * DH]
                keep_wide = keep[:, :, :].rearrange("p t b -> p (t b)").rearrange("p (m s o) -> p m s o", s=2, o=1)
                dve.tensor_tensor(kept[:, :, :, :], sums.rearrange("p m (s d) -> p m s d", s=2),
                                  keep_wide.to_broadcast(every), ALU.mult).then_inc(post, 1)
                flat = keep[:, :, :].rearrange("p t b -> p (t b)")
                for s in range(2):
                    rows = slice(s * BLK, (s + 1) * BLK)
                    op = dve.tensor_tensor(keep_own[rows, :], flat[rows, s::NBLK + 2], on[k][rows, :], ALU.mult)
                op.then_inc(post, 1)
                dve.wait_ge(post, at + 2)
                dve.tensor_reduce(total[:, :, :], kept[:, :, :, :].rearrange("p m s d -> p (m s d)").rearrange(
                    "p (t b d) -> p t d b", t=TPB, d=DH), AX.X, ALU.add).then_inc(post, 1)
                dve.wait_ge(post, at + 3)
                dve.tensor_tensor(keep_own[:, :], l[:, :], keep_own[:, :], ALU.subtract).then_inc(post, 1)
                dve.wait_ge(post, at + 5)
                dve.tensor_tensor(keep_own[:, :], keep_own[:, :], diff[k][:, :, NBLK], ALU.mult).then_inc(post, 1)
                dve.wait_ge(post, at + 6)
                for s in range(2):
                    rows = slice(s * BLK, (s + 1) * BLK)
                    mine = v[rows, bass.ds(n, 1), :, s * DH:(s + 1) * DH].rearrange("p o t d -> p (o t) d")
                    op = dve.tensor_tensor(own[rows, :, :], mine, keep_own[rows, :].rearrange("p (t o) -> p t o", o=1)
                                           .to_broadcast([BLK, TPB, DH]), ALU.mult).then_inc(post, 1)
                dve.wait_ge(post, at + 8)
                dve.tensor_tensor(o[:, bass.ds(n, 1), :, :].rearrange("p o t d -> p (o t) d"), total[:, :, :], own[:, :, :],
                                  ALU.add).then_inc(post, 1)

            dve.memset(top3[:, :, :], 0.0).then_inc(setup, 1)
            dve.memset(tops[:, :, :], -3e38).then_inc(setup, 1)
            if causal:
                dve.tensor_copy(masks[:, :], raw[:, :]).then_inc(setup, 1)
            else:
                dve.tensor_copy(same_block[:, :], raw[:, :]).then_inc(setup, 1)
            dve.wait_ge(setup, 3)
            for x in range(P1):
                maxima(0, x)
            tops_of(0, 0)

            def step(n, k, more):
                started = not (isinstance(n, int) and n == 0)
                if more:
                    maxima(n + 1, 0)
                    maxima(n + 1, 1)
                rows_of(n)
                if started:
                    post_a(n - 1, 1 - k)
                for x in range(2, P1):
                    if more:
                        maxima(n + 1, x)
                    if x == 5 and started:
                        post_b(n - 1, 1 - k)
                if more:
                    tops_of(n + 1, 1 - k)

            each_head(dve, step)
            post_a(NARROW - 1, 1)
            post_b(NARROW - 1, 1)
            dve.wait_ge(post, NARROW * POST)
            for b in range(BATCH):
                dve.tensor_copy(c.xt[:, b * SEQ:(b + 1) * SEQ].rearrange("p (t h d) -> p h t d", t=TPB, h=HEADS),
                                o[:, b * HEADS:(b + 1) * HEADS, :, :]).then_inc(regrouped, 1)
            for g in range(CHUNKS):
                dve.wait_ge(y_done, g + 1)
                x = c.x[:, g * TPC:(g + 1) * TPC, :].rearrange("p t d -> p (t d)")
                dve.tensor_tensor(x, x, c.bank(1), ALU.add).then_inc(added, 1)


class Stage:

    def __init__(self, c, ctx, name):
        self.c, self.ctx, self.name, self.loads = c, ctx, name, []

    def tile(self, what, shape, dram=None, dt=F32):
        t = self.c.sbuf(self.ctx, f"{self.name}_{what}", shape, dt)
        whole = t[tuple(slice(None) for _ in shape)]
        self.loads.append((whole, self.c.ins[what] if dram is None else dram))
        return t


def stage_l0_attn(nc, c):
    with ExitStack() as ctx:
        s = Stage(c, ctx, "lin")
        w = s.tile("l0a_w", [P, 4 * P])
        bias = s.tile("l0a_bias", [P, 4])
        w_out = s.tile("l0a_w_out", [P, P])
        b_out = s.tile("l0a_b_out", [1, P])
        gain_shift = s.tile("l0a_gain_shift", [P, 2])
        mask = s.tile("upper", [P, P])
        layer_norm(nc, c, "ln_lin1", c.x, transpose=False, loads=s.loads)
        layer_norm(nc, c, "ln_lin2", c.xn, gain=gain_shift[:, 0:1], shift=gain_shift[:, 1:2])
        linear_attention(nc, c, w, bias, w_out, b_out, mask)


def stage_l0_ffn(nc, c):
    with ExitStack() as ctx:
        s = Stage(c, ctx, "fp4")
        w = s.tile("l0f_w", [P, 2 * 3 * P + 352])
        layer_norm(nc, c, "ln_fp4", c.x, transpose=False, loads=s.loads)
        fp4_mlp(nc, c, w)


def stage_l1_attn(nc, c):
    with ExitStack() as ctx:
        s = Stage(c, ctx, "wide")
        w_out = s.tile("l1a_w_out", [P, 4, P])
        b_out = s.tile("l1a_b_out", [1, P])
        gain = s.tile("l1a_gain", [P, D])
        shift = s.tile("l1a_shift", [P, D])
        y = c.sbuf(ctx, "wide_y", [P, TILES, D])
        layer_norm(nc, c, "ln_wide", c.x, loads=s.loads)
        wide_attention(nc, c, c.ins["l1a_w"], w_out, b_out, y)
        layer_norm(nc, c, "ln_post", y, transpose=False, dst=y)
        add_normed(nc, c, y, gain, shift)


def stage_l1_ffn(nc, c):
    with ExitStack() as ctx:
        s = Stage(c, ctx, "moe1")
        gate = s.tile("l1f_gate", [P, 15])
        out_bias = s.tile("l1f_out_bias", [16, P])
        comb = c.sbuf(ctx, "moe1_comb", [P, TILES, 17])
        layer_norm(nc, c, "ln_moe1", c.x, loads=s.loads)
        route(nc, c, "route1", 15, 1, 3, 2, gate, comb)
        gated_experts(nc, c, "moe1", 17, ACT.Gelu, c.ins["l1f_weights"], comb, True, out_bias, 16)


def stage_l3_ffn(nc, c):
    with ExitStack() as ctx:
        s = Stage(c, ctx, "moe3")
        gate = s.tile("l3f_gate", [P, 8])
        comb = c.sbuf(ctx, "moe3_comb", [P, TILES, 16])
        layer_norm(nc, c, "ln_moe3", c.x, loads=s.loads)
        route(nc, c, "route3", 8, 2, 2, 0, gate, comb)
        gated_experts(nc, c, "moe3", 16, ACT.Silu, c.ins["l3f_weights"], comb, False)


def stage_l3_attn(nc, c):
    with ExitStack() as ctx:
        s = Stage(c, ctx, "rot")
        w_out = s.tile("l3a_w_out", [P, P])
        b_out = s.tile("l3a_b_out", [1, P])
        raw = s.tile("l3a_masks", [P, 5 * P])
        q_stack = c.sbuf(ctx, "rot_q_stack", [P, NARROW, SEQ], BF16)
        k_stack = c.sbuf(ctx, "rot_k_stack", [P, NARROW, SEQ], BF16)
        v = c.sbuf(ctx, "rot_v", [P, NARROW, TPB, DH + 1])
        with ExitStack() as prep:
            s.ctx = prep
            w = s.tile("l3a_w", [P, 5 * P])
            cos = s.tile("l3a_cos", [P, SEQ])
            sin = s.tile("l3a_sin", [P, SEQ])
            bias = s.tile("l3a_bias", [P, 4])
            v_bias = s.tile("l3a_v_bias", [1, P])
            layer_norm(nc, c, "ln_rot", c.x, loads=s.loads)
            narrow_prepare(nc, c, w, (cos, sin, bias, v_bias), q_stack, k_stack, v, None)
        narrow_attention(nc, c, True, q_stack, k_stack, v, None, raw, w_out, b_out)


def stage_l2_attn(nc, c):
    with ExitStack() as ctx:
        s = Stage(c, ctx, "blk")
        w_out = s.tile("l2a_w_out", [P, P])
        raw = s.tile("l2a_same", [P, P])
        q_stack = c.sbuf(ctx, "blk_q_stack", [P, NARROW, SEQ], BF16)
        k_stack = c.sbuf(ctx, "blk_k_stack", [P, NARROW, SEQ], BF16)
        v = c.sbuf(ctx, "blk_v", [P, NARROW, TPB, 2 * DH + 1])
        diag = c.sbuf(ctx, "blk_diag", [P, NARROW, TPB])
        with ExitStack() as prep:
            s.ctx = prep
            w = s.tile("l2a_w", [P, 3 * P])
            layer_norm(nc, c, "ln_blk", c.x, loads=s.loads)
            narrow_prepare(nc, c, w, None, q_stack, k_stack, v, diag)
        narrow_attention(nc, c, False, q_stack, k_stack, v, diag, raw, w_out, None)


def stage_l2_ffn(nc, c):
    with ExitStack() as ctx:
        s = Stage(c, ctx, "mlp2")
        w1 = s.tile("l2f_w1", [P, 512])
        w2 = s.tile("l2f_w2", [P, 4, P])
        b1 = s.tile("l2f_b1", [P, 4])
        b2 = s.tile("l2f_b2", [1, P])
        layer_norm(nc, c, "ln_mlp2", c.x, loads=s.loads)
        ternary_mlp(nc, c, w1, w2, b1, b2)


def packs(i):
    cat, asc = np.concatenate, np.ascontiguousarray
    o = {"x": i["L0_attn_x"].reshape(TOKENS, D), "ident": np.eye(P, dtype=np.float32)}

    q, k, v = np.split(i["L0_attn_w_qkv"], 3, axis=1)
    bq, bk, bv = np.split(i["L0_attn_b_qkv"], 3)
    o["l0a_w"] = cat([i["L0_attn_w_gate"], k, q, v], axis=1)
    o["l0a_bias"] = np.stack([i["L0_attn_b_gate"], bk, bq, bv], axis=1)
    o["l0a_w_out"] = i["L0_attn_w_proj"]
    o["l0a_b_out"] = i["L0_attn_b_proj"][None]
    o["l0a_gain_shift"] = np.stack([i["L0_attn_ln_g"], i["L0_attn_ln_b"]], axis=1)
    o["upper"] = np.triu(np.ones((P, P), np.float32))

    pad = np.zeros((3 * P - 352, D), np.float32)
    o["l0f_w"] = cat([cat([i[n], pad]).reshape(3, P, D).transpose(1, 0, 2).reshape(P, 3 * D)
                      for n in ("L0_ffn_w_gate", "L0_ffn_w_up")] + [i["L0_ffn_w_down"]], axis=1)

    qk = i["L1_attn_W_qk"].reshape(D, 4, 2 * 64, 2)
    bqk = i["L1_attn_b_qk"].reshape(4, 2 * 64, 2)
    wv, bv = i["L1_attn_W_v"].reshape(D, 4, P), i["L1_attn_b_v"].reshape(4, P)
    o["l1a_w"] = np.stack([cat([qk[:, k, :, 0], qk[:, k, :, 1], wv[:, k], bqk[k], bv[k][:, None]], axis=1)
                           for k in range(4)])
    o["l1a_w_out"] = i["L1_attn_W_out"].reshape(4, P, D).transpose(1, 0, 2)
    o["l1a_b_out"] = i["L1_attn_b_out"][None]
    o["l1a_gain"] = np.broadcast_to(i["L1_attn_ln_gamma"], (P, D))
    o["l1a_shift"] = np.broadcast_to(i["L1_attn_ln_beta"], (P, D))

    fc1, fc2, s1, s2 = i["L1_ffn_fc1_w"], i["L1_ffn_fc2_w"], i["L1_ffn_s_fc1_w"], i["L1_ffn_s_fc2_w"]
    packed = [cat([fc1[e, P:].T, fc1[e, :P].T, fc2[e].T], axis=1) for e in range(15)]
    packed += [cat([s1[2 * P + k * P:3 * P + k * P].T, s1[k * P:(k + 1) * P].T, s2[:, k * P:(k + 1) * P].T], axis=1)
               for k in range(2)]
    b, sb_, m, sm = i["L1_ffn_fc1_b"], i["L1_ffn_s_fc1_b"], i["L1_ffn_geglu_mult"], i["L1_ffn_s_geglu_mult"]
    rows = [np.stack([b[e, P:], b[e, :P], m[e]], axis=1) for e in range(15)]
    rows += [np.stack([sb_[2 * P + k * P:3 * P + k * P], sb_[k * P:(k + 1) * P], sm[k * P:(k + 1) * P]], axis=1)
             for k in range(2)]
    o["l1f_weights"] = np.stack([cat([w, r], axis=1) for w, r in zip(packed, rows)])
    o["l1f_gate"] = i["L1_ffn_gate_w"].T
    o["l1f_out_bias"] = cat([i["L1_ffn_fc2_b"], i["L1_ffn_s_fc2_b"][None]], axis=0)

    o["l2a_w"] = cat([i["L2_attn_" + n].T for n in ("wq", "wk", "wv")], axis=1)
    o["l2a_w_out"] = i["L2_attn_wo"].T
    tok, feat = np.arange(SEQ), np.arange(P)
    o["l2a_onehot"] = (np.arange(NBLK)[:, None] == tok // BLK).astype(np.float32)
    o["l2a_headsel"] = (feat[:, None] // DH == np.arange(HEADS)).astype(np.float32)
    o["l2a_same"] = (feat[:, None] // BLK == feat // BLK).astype(np.float32)

    swap = feat ^ 1
    wq, wk, bq, bk = (i["L3_attn_" + n] for n in ("Wq", "Wk", "bq", "bk"))
    o["l3a_w"] = cat([wq.T, wq[swap].T, wk.T, wk[swap].T, i["L3_attn_Wv"].T], axis=1)
    o["l3a_bias"] = np.stack([bq, bq[swap], bk, bk[swap]], axis=1)
    o["l3a_v_bias"] = i["L3_attn_bv"][None]
    o["l3a_w_out"] = i["L3_attn_Wp"].T
    o["l3a_b_out"] = i["L3_attn_bp"][None]
    theta = np.array([10.0 ** k for k in range(DH // 2)], np.float32)
    angle = (theta[feat % DH // 2][:, None] * tok.astype(np.float32)).astype(np.float64)
    o["l3a_cos"] = np.cos(angle).astype(np.float32)
    o["l3a_sin"] = (np.where(feat % 2, 1.0, -1.0)[:, None] * np.sin(angle)).astype(np.float32)
    after = np.where(feat > feat[:, None], FAR, 0.0)
    before = after.T
    o["l3a_masks"] = cat([after, before, 0 * after, 0 * after + FAR, before], axis=1).astype(np.float32)

    w0, w1, wo = i["L3_ffn_w0_kernel"], i["L3_ffn_w1_kernel"], i["L3_ffn_wo_kernel"]
    o["l3f_weights"] = np.stack([cat([w0[e][:, k * P:(k + 1) * P], w1[e][:, k * P:(k + 1) * P],
                                      wo[e][k * P:(k + 1) * P]], axis=1) for e in range(8) for k in range(2)])
    o["l3f_gate"] = i["L3_ffn_gate_kernel"]

    o["l2f_w1"] = i["L2_ffn_W1"].T
    o["l2f_w2"] = i["L2_ffn_W2"].T.reshape(4, P, D).transpose(1, 0, 2)
    o["l2f_b1"] = i["L2_ffn_b1"].reshape(4, P).T
    o["l2f_b2"] = i["L2_ffn_b2"][None]
    return {k: asc(v) for k, v in o.items()}


def layers(nc, ins, out):
    with ExitStack() as ctx:
        c = Chip(nc, ctx, ins, out)
        start(nc, c)
        stage_l0_attn(nc, c)
        stage_l0_ffn(nc, c)
        stage_l1_attn(nc, c)
        stage_l1_ffn(nc, c)
        c.clear_semaphores()
        stage_l2_attn(nc, c)
        stage_l2_ffn(nc, c)
        stage_l3_attn(nc, c)
        stage_l3_ffn(nc, c)
        finish(nc, c)


def kernel(**inputs):
    import concourse.bacc as bacc
    from concourse.bass_utils import run_bass_kernel_spmd as run

    nc = bacc.Bacc("TRN2", target_bir_lowering=False, num_devices=1)
    laid_out = packs({name: np.asarray(a) for name, a in inputs.items()})
    arrays = {f"in_{name}_dram": a for name, a in laid_out.items()}
    ins = {name: nc.dram_tensor(f"in_{name}_dram", a.shape, mybir.dt.from_np(a.dtype), kind="ExternalInput").ap()
           for name, a in laid_out.items()}
    out = nc.dram_tensor("out_dram", (TOKENS, D), F32, kind="ExternalOutput").ap()
    layers(nc, ins, out)
    r = run(nc, [arrays], core_ids=[0])
    return r.results[0]["out_dram"].reshape(BATCH, SEQ, D)
```

```python
from contextlib import ExitStack

import numpy as np

import concourse.bass as bass
from concourse import mybir

F32 = mybir.dt.float32
BF16 = mybir.dt.bfloat16
ALU = mybir.AluOpType
ACT = mybir.ActivationFunctionType
AX = mybir.AxisListType

P = 128
BATCH, SEQ, D = 2, 1024, 128
TOKENS = BATCH * SEQ
TILES = TOKENS // P
TPB = SEQ // P
BANK = 512
CHUNKS = TOKENS // BANK
TPC = BANK // P
LN_EPS = 1e-5


def wait_from(eng, sem, value):
    if not isinstance(value, int) or value > 0:
        eng.wait_ge(sem, value)


class Chip:

    def __init__(self, nc, ctx, ins, out):
        self.nc, self.ctx, self.ins, self.out = nc, ctx, ins, out
        self.x = self.sbuf(ctx, "x_res", [P, TILES, D])
        self.xn = self.sbuf(ctx, "x_norm", [P, TILES, D])
        self.xt = self.sbuf(ctx, "x_norm_t", [P, TOKENS])
        self.ident = self.sbuf(ctx, "identity", [P, P])
        self.ones_row = self.sbuf(ctx, "ones_row", [1, P])
        self.ident_bf = self.sbuf(ctx, "identity_bf", [P, P], BF16)
        self.stats = self.sbuf(ctx, "ln_stats", [P, TILES, 6])
        self.moments = self.sbuf(ctx, "ln_moments", [P, TILES, 2])
        self.std = self.sbuf(ctx, "ln_std", [P, TILES])
        self.rstd = self.sbuf(ctx, "ln_rstd", [P, TILES])
        self.newton = self.sbuf(ctx, "ln_newton", [P, TILES])
        self.eps = self.sbuf(ctx, "ln_eps", [P, 1])
        self.semaphores = []
        self.share_ln_semaphores("first")
        self.ps = ctx.enter_context(nc.psum_tensor("psum", [P, 8, BANK], F32))

    def sbuf(self, ctx, name, shape, dt=F32):
        return ctx.enter_context(self.nc.sbuf_tensor(name, shape, dt))

    def semaphore(self, name):
        self.semaphores.append(self.nc.alloc_semaphore(name=name))
        return self.semaphores[-1]

    def share_ln_semaphores(self, half):
        self.ln = {what: self.semaphore(f"ln_{half}_{what}") for what in
                   ("stats", "moments", "std", "rstd", "normed", "turned", "loaded")}
        self.ln_count = dict.fromkeys(self.ln, 0)

    def clear_semaphores(self):
        self.nc.clear_and_free_semaphores(self.semaphores)
        self.nc.all_engine_barrier()
        self.semaphores = []
        self.share_ln_semaphores("second")

    def bank(self, k):
        return self.ps[:, k, :]


def start(nc, c):
    with ExitStack() as ctx:
        loaded = c.semaphore("start_loaded")
        ident_ready = c.semaphore("ident_ready")
        block = ctx.enter_context(nc.Block())

        @block.sync
        def _(sp):
            sp.dma_start(c.x[:, :, :], c.ins["x"].rearrange("(t p) d -> p t d", p=P)).then_inc(loaded, 16)
            sp.dma_start(c.ident[:, :], c.ins["ident"]).then_inc(ident_ready, 16)
            sp.wait_ge(loaded, 16)

        @block.vector
        def _(dve):
            dve.memset(c.ones_row[:, :], 1.0)
            dve.memset(c.eps[:, :], LN_EPS)
            dve.wait_ge(ident_ready, 16)
            dve.tensor_copy(c.ident_bf[:, :], c.ident[:, :])


def finish(nc, c):
    with ExitStack() as ctx:
        stored = c.semaphore("output_stored")
        block = ctx.enter_context(nc.Block())

        @block.sync
        def _(sp):
            sp.dma_start(c.out.rearrange("(t p) d -> p t d", p=P), c.x[:, :, :]).then_inc(stored, 16)
            sp.wait_ge(stored, 16)


def layer_norm(nc, c, name, src, transpose=True, gain=None, shift=None, loads=(), dst=None,
               clears=()):
    dst = c.xn if dst is None else dst
    with ExitStack() as ctx:
        stats_ready, moments_ready, std_ready = c.ln["stats"], c.ln["moments"], c.ln["std"]
        rstd_ready, normed, turned, loaded = c.ln["rstd"], c.ln["normed"], c.ln["turned"], c.ln["loaded"]
        stats0, moments0, std0, rstd0, normed0, turned0, loaded0 = c.ln_count.values()
        for what, more in (("stats", TILES), ("moments", TILES), ("std", 1), ("rstd", 5), ("normed", TILES),
                           ("turned", TILES if transpose else 0), ("loaded", 16 * len(loads))):
            c.ln_count[what] += more
        block = ctx.enter_context(nc.Block())

        @block.sync
        def _(sp):
            for dst, dram in loads:
                sp.dma_start(dst, dram).then_inc(loaded, 16)
            if loads:
                sp.wait_ge(loaded, loaded0 + 16 * len(loads))

        @block.vector
        def _(dve):
            for t in range(TILES):
                dve.bn_stats(c.stats[:, t, :], src[:, t, :]).then_inc(stats_ready, 1)
            for t in range(TILES):
                dve.wait_ge(stats_ready, stats0 + t + 1)
                dve.bn_aggr(c.moments[:, t, :], c.stats[:, t, :]).then_inc(moments_ready, 1)
            dve.wait_ge(std_ready, std0 + 1)
            dve.reciprocal(c.rstd[:, :], c.std[:, :]).then_inc(rstd_ready, 1)
            dve.wait_ge(rstd_ready, rstd0 + 1)
            dve.tensor_tensor(c.newton[:, :], c.rstd[:, :], c.rstd[:, :], ALU.mult).then_inc(rstd_ready, 1)
            dve.wait_ge(rstd_ready, rstd0 + 2)
            dve.scalar_tensor_tensor(c.newton[:, :], c.moments[:, :, 1], LN_EPS, c.newton[:, :],
                                     ALU.add, ALU.mult).then_inc(rstd_ready, 1)
            dve.wait_ge(rstd_ready, rstd0 + 3)
            dve.tensor_scalar(c.newton[:, :], c.newton[:, :], -0.5, 1.5, ALU.mult, ALU.add).then_inc(rstd_ready, 1)
            dve.wait_ge(rstd_ready, rstd0 + 4)
            dve.tensor_tensor(c.rstd[:, :], c.rstd[:, :], c.newton[:, :], ALU.mult).then_inc(rstd_ready, 1)
            dve.wait_ge(rstd_ready, rstd0 + 5)
            for t in range(TILES):
                dve.tensor_scalar(dst[:, t, :], src[:, t, :], c.moments[:, t, 0:1], c.rstd[:, t:t + 1],
                                  ALU.subtract, ALU.mult).then_inc(normed, 1)

        @block.scalar
        def _(act):
            act.wait_ge(moments_ready, moments0 + TILES)
            act.activation(c.std[:, :], c.moments[:, :, 1], ACT.Sqrt, bias=c.eps[:, 0:1]).then_inc(std_ready, 1)
            if transpose:
                for g in range(CHUNKS):
                    act.wait_ge(turned, turned0 + TPC * (g + 1))
                    out = c.xt[:, g * BANK:(g + 1) * BANK]
                    if gain is None:
                        act.activation(out, c.bank(g), ACT.Identity)
                    else:
                        act.activation(out, c.bank(g), ACT.Identity, bias=shift, scale=gain)

        if clears:
            @block.gpsimd
            def _(pool):
                for what, value in clears:
                    pool.memset(what, value)

        if transpose:
            @block.tensor
            def _(pe):
                for t in range(TILES):
                    pe.wait_ge(normed, normed0 + t + 1)
                    pe.transpose(c.bank(t // TPC)[:, (t % TPC) * P:(t % TPC + 1) * P], dst[:, t, :],
                                 c.ident[:, :]).then_inc(turned, 1)


def route(nc, c, name, experts, copies, topk, always, gate_w, comb):
    pads = 8 - topk
    wide = experts + pads
    low = -3.0e38
    with ExitStack() as ctx:
        def sem(what):
            return c.semaphore(f"{name}_{what}")

        def sb(what, shape):
            return c.sbuf(ctx, f"{name}_{what}", shape)

        logits = sb("logits", [P, TILES, wide])
        replaced = sb("replaced", [P, TILES, wide])
        top = sb("top", [P, TILES, 8])
        chosen = sb("chosen", [P, TILES, 8])
        shifted = sb("shifted", [P, TILES, experts])
        weight = sb("weight", [P, TILES, experts])
        total = sb("total", [P, TILES])
        logits_ps = c.bank(0)
        multiplied, step, exp_ready = sem("multiplied"), sem("step"), sem("exp")
        block = ctx.enter_context(nc.Block())

        @block.tensor
        def _(pe):
            for t in range(TILES):
                pe.matmul(logits_ps[:, t * experts:(t + 1) * experts], c.xt[:, t * P:(t + 1) * P], gate_w[:, :],
                          start=True, stop=True).then_inc(multiplied, 1)

        @block.vector
        def _(dve):
            dve.memset(logits[:, :, :], low).then_inc(step, 1)
            dve.wait_ge(step, 1)
            dve.wait_ge(multiplied, TILES)
            dve.tensor_copy(logits[:, :, 0:experts],
                            logits_ps[:, 0:TILES * experts].rearrange("p (t e) -> p t e", e=experts)).then_inc(step, 1)
            dve.wait_ge(step, 2)
            for t in range(TILES):
                dve.max(top[:, t, :], logits[:, t, :]).then_inc(step, 1)
            dve.memset(chosen[:, :, :], low).then_inc(step, 1)
            dve.wait_ge(step, 3 + TILES)
            dve.tensor_copy(chosen[:, :, 0:topk], top[:, :, 0:topk]).then_inc(step, 1)
            dve.tensor_tensor(shifted[:, :, :], logits[:, :, 0:experts],
                              top[:, :, 0:1].to_broadcast([P, TILES, experts]), ALU.subtract).then_inc(step, 1)
            dve.wait_ge(step, 5 + TILES)
            for t in range(TILES):
                dve.match_replace(replaced[:, t, :], chosen[:, t, :], logits[:, t, :], -low).then_inc(step, 1)
            dve.wait_ge(step, 5 + 2 * TILES)
            dve.wait_ge(exp_ready, 1)
            dve.scalar_tensor_tensor(weight[:, :, :], replaced[:, :, 0:experts], -low, weight[:, :, :],
                                     ALU.is_equal, ALU.mult).then_inc(step, 1)
            dve.wait_ge(step, 6 + 2 * TILES)
            dve.tensor_reduce(total[:, :], weight[:, :, :], AX.X, ALU.add).then_inc(step, 1)
            dve.wait_ge(step, 7 + 2 * TILES)
            dve.reciprocal(total[:, :], total[:, :]).then_inc(step, 1)
            dve.wait_ge(step, 8 + 2 * TILES)
            for k in range(copies):
                dve.tensor_tensor(comb[:, :, k:experts * copies:copies], weight[:, :, :],
                                  total[:, :].rearrange("p (t o) -> p t o", o=1).to_broadcast([P, TILES, experts]),
                                  ALU.mult)
            if always:
                dve.memset(comb[:, :, experts * copies:experts * copies + always], 1.0)

        @block.scalar
        def _(act):
            act.wait_ge(step, 5 + TILES)
            act.activation(weight[:, :, :], shifted[:, :, :], ACT.Exp).then_inc(exp_ready, 1)


def gated_experts(nc, c, name, parts, gate_act, weights, comb, biased, out_bias=None, out_bias_rows=0):
    with ExitStack() as ctx:
        def sem(what):
            return c.semaphore(f"{name}_{what}")

        w = [c.sbuf(ctx, f"{name}_w{k}", [P, weights.shape[2]]) for k in range(2)]
        gated = [c.sbuf(ctx, f"{name}_gated{k}", [P, BANK]) for k in range(2)]
        prod = [c.sbuf(ctx, f"{name}_prod{k}", [P, BANK]) for k in range(2)]
        a_ps, b_ps, y_ps = [c.bank(0), c.bank(1)], [c.bank(2), c.bank(3)], [c.bank(4), c.bank(5)]
        rows = out_bias_rows
        comb_t = c.sbuf(ctx, f"{name}_comb_t", [max(rows, 1), TOKENS])

        w_loaded, w_scaled = [sem(f"w{k}_loaded") for k in range(2)], sem("w_scaled")
        a_ready, b_ready, gated_ready, prod_ready = sem("a_ready"), sem("b_ready"), sem("gated_ready"), sem("prod_ready")
        y_ready, added = sem("y_ready"), sem("added")
        comb_turned, comb_copied, bias_ready, bias_added = sem("comb_turned"), sem("comb_copied"), sem("bias"), sem("bias_added")
        block = ctx.enter_context(nc.Block())

        pairs = (parts - 1) // 2
        last = 1 + 2 * pairs

        def each_part(eng, body):
            body(0, 0, 0)
            with eng.Fori(0, pairs) as i:
                body(i * 2 + 1, 1, i)
                body(i * 2 + 2, 0, i + 1)
            if last < parts:
                body(last, 1, pairs)

        @block.sync
        def _(sp):
            def load(e, k, use):
                wait_from(sp, y_ready, e * CHUNKS - CHUNKS + 1)
                sp.dma_start(w[k][:, :], weights[e, :, :]).then_inc(w_loaded[k], 16)
            each_part(sp, load)

        @block.tensor
        def _(pe):
            for first in (y_ready,):
                pe.sem_inc(first, 1)
            if rows:
                for g in range(CHUNKS):
                    wait_from(pe, comb_copied, g - 1)
                    for j in range(TPC):
                        mm = pe.transpose(y_ps[g % 2][0:rows, j * P:(j + 1) * P], comb[:, g * TPC + j, 0:rows],
                                          c.ident[:, :])
                    mm.then_inc(comb_turned, 1)
                pe.wait_ge(comb_copied, CHUNKS)
                for g in range(CHUNKS):
                    wait_from(pe, bias_added, g - 1)
                    for j in range(TPC):
                        t = g * TPC + j
                        mm = pe.matmul(y_ps[g % 2][:, j * P:(j + 1) * P], comb_t[:, t * P:(t + 1) * P],
                                       out_bias[:, :], start=True, stop=True)
                    mm.then_inc(bias_ready, 1)
                pe.wait_ge(bias_added, CHUNKS)

            def down(n, g, k, e):
                pe.wait_ge(prod_ready, n + 1)
                wait_from(pe, added, n - 1)
                if biased:
                    pe.wait_ge(w_scaled, e + 1)
                for j in range(TPC):
                    mm = pe.matmul(y_ps[g % 2][:, j * P:(j + 1) * P], prod[g % 2][:, j * P:(j + 1) * P],
                                   w[k][:, 2 * P:3 * P], start=True, stop=True)
                mm.then_inc(y_ready, 1)

            def part(e, k, use):
                pe.wait_ge(w_loaded[k], use * 16 + 16)
                for g in range(CHUNKS):
                    n = e * CHUNKS + g
                    x = c.xt[:, g * BANK:(g + 1) * BANK]
                    wait_from(pe, gated_ready, n - 1)
                    pe.matmul(a_ps[g % 2], w[k][:, 0:P], x, start=True, stop=True).then_inc(a_ready, 1)
                    wait_from(pe, prod_ready, n - 1)
                    pe.matmul(b_ps[g % 2], w[k][:, P:2 * P], x, start=True, stop=True).then_inc(b_ready, 1)
                    if g:
                        down(n - 1, g - 1, k, e)
                    elif not (isinstance(e, int) and e == 0):
                        down(n - 1, CHUNKS - 1, 1 - k, e - 1)
            each_part(pe, part)
            down(parts * CHUNKS - 1, CHUNKS - 1, (parts - 1) % 2, parts - 1)

        @block.scalar
        def _(act):
            for g in range(CHUNKS if rows else 0):
                act.wait_ge(comb_turned, g + 1)
                act.copy(comb_t[:, g * BANK:(g + 1) * BANK], y_ps[g % 2][0:rows, :]).then_inc(comb_copied, 1)

            def part(e, k, use):
                for g in range(CHUNKS):
                    n = e * CHUNKS + g
                    act.wait_ge(a_ready, n + 1)
                    wait_from(act, prod_ready, n - 1)
                    act.activation(gated[g % 2][:, :], a_ps[g % 2], gate_act,
                                   bias=w[k][:, 3 * P:3 * P + 1] if biased else 0.0).then_inc(gated_ready, 1)
            each_part(act, part)

        @block.vector
        def _(dve):
            for g in range(CHUNKS if rows else 0):
                dve.wait_ge(bias_ready, g + 1)
                x = c.x[:, g * TPC:(g + 1) * TPC, :].rearrange("p t d -> p (t d)")
                dve.tensor_tensor(x, x, y_ps[g % 2], ALU.add).then_inc(bias_added, 1)
            if rows:
                dve.wait_ge(bias_added, CHUNKS)

            def add(n, g, e):
                dve.wait_ge(y_ready, n + 2)
                wait_from(dve, added, n - 3)
                for j in range(TPC):
                    t = g * TPC + j
                    op = dve.scalar_tensor_tensor(c.x[:, t, :], y_ps[g % 2][:, j * P:(j + 1) * P],
                                                  comb[:, t, e:e + 1] if isinstance(e, int) else comb[:, t, bass.ds(e, 1)],
                                                  c.x[:, t, :], ALU.mult, ALU.add)
                op.then_inc(added, 1)

            def part(e, k, use):
                if biased:
                    dve.wait_ge(w_loaded[k], use * 16 + 16)
                    dve.tensor_scalar(w[k][:, 2 * P:3 * P], w[k][:, 2 * P:3 * P], w[k][:, 3 * P + 2:3 * P + 3], None,
                                      ALU.mult).then_inc(w_scaled, 1)
                for g in range(CHUNKS):
                    n = e * CHUNKS + g
                    dve.wait_ge(gated_ready, n + 1)
                    dve.wait_ge(b_ready, n + 1)
                    wait_from(dve, y_ready, n)
                    if not biased:
                        op = dve.tensor_tensor(prod[g % 2][:, :], b_ps[g % 2], gated[g % 2][:, :], ALU.mult)
                    else:
                        op = dve.scalar_tensor_tensor(prod[g % 2][:, :], b_ps[g % 2], w[k][:, 3 * P + 1:3 * P + 2],
                                                      gated[g % 2][:, :], ALU.add, ALU.mult)
                    op.then_inc(prod_ready, 1)
                    if g:
                        add(n - 1, g - 1, e)
                    elif not (isinstance(e, int) and e == 0):
                        add(n - 1, CHUNKS - 1, e - 1)
            each_part(dve, part)
            add(parts * CHUNKS - 1, CHUNKS - 1, parts - 1)


def ternary_mlp(nc, c, w1, w2, b1, b2):
    hidden = w1.shape[1]
    tiles_h = hidden // P
    eps = 1e-5
    rne = 1.5 * 2.0 ** 23
    with ExitStack() as ctx:
        def sem(what):
            return c.semaphore(f"mlp_{what}")

        def sb(what, shape):
            return c.sbuf(ctx, f"mlp_{what}", shape)

        sums, gamma, ones = sb("sums", [P, 2]), sb("gamma", [P, 2]), sb("ones", [P, P])
        h = [sb(f"h{k}", [P, tiles_h, BANK]) for k in range(2)]
        step, sums_ps_ready, h_ready, relu_ready, y_ready, added = (
            sem("step"), sem("sums"), sem("h"), sem("relu"), sem("y"), sem("added"))
        w2f = w2[:, :, :].rearrange("p f d -> p (f d)")
        block = ctx.enter_context(nc.Block())

        @block.vector
        def _(dve):
            dve.memset(ones[:, :], 1.0).then_inc(step, 1)
            dve.tensor_reduce(sums[:, 0:1], w1[:, :], AX.X, ALU.add, apply_absolute_value=True).then_inc(step, 1)
            dve.tensor_reduce(sums[:, 1:2], w2f, AX.X, ALU.add, apply_absolute_value=True).then_inc(step, 1)
            dve.wait_ge(sums_ps_ready, 1)
            dve.tensor_scalar(gamma[:, :], c.bank(7)[:, 0:2], 1.0 / (hidden * D), eps, ALU.mult, ALU.add).then_inc(step, 1)
            dve.wait_ge(step, 4)
            dve.reciprocal(gamma[:, :], gamma[:, :]).then_inc(step, 1)
            dve.wait_ge(step, 5)
            n = 5
            for k, w in enumerate((w1[:, :], w2f)):
                for args in ((gamma[:, k:k + 1], 1.0, ALU.mult, ALU.min), (-1.0, rne, ALU.max, ALU.add),
                             (rne, None, ALU.subtract)):
                    dve.tensor_scalar(w, w, *args).then_inc(step, 1)
                    n += 1
                    dve.wait_ge(step, n)

            def tail(g):
                dve.wait_ge(y_ready, g + 1)
                x = c.x[:, g * TPC:(g + 1) * TPC, :].rearrange("p t d -> p (t d)")
                dve.tensor_tensor(x, x, c.bank(4 + g % 2), ALU.add).then_inc(added, 1)

            for g in range(CHUNKS):
                tail(g)

        @block.tensor
        def _(pe):
            pe.wait_ge(step, 3)
            pe.matmul(c.bank(7)[:, 0:2], ones[:, :], sums[:, :], start=True, stop=True).then_inc(sums_ps_ready, 1)

            def down(g):
                pe.wait_ge(relu_ready, tiles_h * (g + 1))
                wait_from(pe, added, g - 1)
                for j in range(TPC):
                    y = c.bank(4 + g % 2)[:, j * P:(j + 1) * P]
                    for f in range(tiles_h):
                        pe.matmul(y, h[g % 2][:, f, j * P:(j + 1) * P], w2[:, f, :], start=(f == 0), stop=False)
                    mm = pe.matmul(y, c.ones_row[:, :], b2[:, :], start=False, stop=True)
                mm.then_inc(y_ready, 1)

            pe.wait_ge(step, 11)
            for g in range(CHUNKS):
                for f in range(tiles_h):
                    wait_from(pe, relu_ready, tiles_h * (g - 1) + f + 1)
                    pe.matmul(c.bank(f), w1[:, f * P:(f + 1) * P], c.xt[:, g * BANK:(g + 1) * BANK],
                              start=True, stop=True).then_inc(h_ready, 1)
                if g:
                    down(g - 1)
            down(CHUNKS - 1)

        @block.scalar
        def _(act):
            for g in range(CHUNKS):
                wait_from(act, y_ready, g - 1)
                for f in range(tiles_h):
                    act.wait_ge(h_ready, tiles_h * g + f + 1)
                    act.activation(h[g % 2][:, f, :], c.bank(f), ACT.Relu, bias=b1[:, f:f + 1]).then_inc(relu_ready, 1)


def linear_attention(nc, c, w, bias, w_out, b_out, mask):
    den_eps = 1e-6
    gate, key, query, value = range(4)
    with ExitStack() as ctx:
        def sem(what):
            return c.semaphore(f"lin_{what}")

        def sb(what, shape):
            return c.sbuf(ctx, f"lin_{what}", shape)

        qt, kt, vt = sb("qt", [P, SEQ]), sb("kt", [P, SEQ]), sb("vt", [P, SEQ])
        half_gate, z, zmin, ez = (sb(n, [P, BANK]) for n in ("gate", "z", "zmin", "ez"))
        zk, zkmin, ezk = (sb(n, [P, BANK]) for n in ("zk", "zkmin", "ezk"))
        half_bias = sb("half_bias", [P, 1])
        tok = [sb(f"tok{k}", [P, 2 * P + 1]) for k in range(2)]
        masked = [sb(f"masked{k}", [P, P]) for k in range(2)]
        state = [sb(f"state{k}", [P, P + 1]) for k in range(2)]
        rden = [sb(f"rden{k}", [P, 1]) for k in range(2)]
        o = [sb(f"o{k}", [P, P]) for k in range(2)]
        ot = [sb(f"ot{k}", [P, P]) for k in range(2)]
        tok_ps, a_ps, o_ps, s_ps = c.bank(4), c.bank(5), c.bank(6), c.bank(7)
        ot_ps, y_ps = c.bank(3), c.bank(2)

        projected, tanh_ready, z_ready, exp_ready, qk_ready, v_ready = (
            sem(n) for n in ("projected", "tanh", "z", "exp", "qk", "v"))
        tok_turned, tok_ready, a_done, a_masked, o_done, o_ready, s_done, s_ready = (
            sem(n) for n in ("tok_turned", "tok", "a", "masked", "o_done", "o", "s_done", "s"))
        den_step, ot_turned, ot_ready, y_done, added, setup = (
            sem(n) for n in ("den_step", "ot_turned", "ot", "y", "added", "setup"))
        block = ctx.enter_context(nc.Block())

        @block.tensor
        def _(pe):
            for first in (o_done, ot_turned):
                pe.sem_inc(first, 1)
            def out_proj(n, k):
                pe.wait_ge(o_ready, n + 2)
                pe.wait_ge(ot_ready, n + 1)
                pe.transpose(ot_ps[:, 0:P], o[k][:, :], c.ident[:, :]).then_inc(ot_turned, 1)
                pe.wait_ge(ot_ready, n + 2)
                pe.wait_ge(added, n + 1)
                pe.matmul(y_ps[:, 0:P], ot[k][:, :], w_out[:, :], start=True, stop=False)
                pe.matmul(y_ps[:, 0:P], c.ones_row[:, :], b_out[:, :], start=False, stop=True).then_inc(y_done, 1)

            with pe.Fori(0, BATCH) as b:
                pe.wait_ge(added, b * TPB + 1)
                for j in range(2):
                    m = b * 2 + j
                    pe.wait_ge(qk_ready, m * 2 + 1)
                    pe.wait_ge(v_ready, m + 1)
                    for r in (gate, key, query, value):
                        pe.matmul(c.bank(r), w[:, r * P:(r + 1) * P], c.xt[:, bass.ds(b * SEQ + j * BANK, BANK)],
                                  start=True, stop=True).then_inc(projected, 1)
                pe.wait_ge(qk_ready, b * 4 + 5)
                pe.wait_ge(v_ready, b * 2 + 3)
                for t in range(TPB):
                    n, k, s = b * TPB + t, t % 2, slice(t * P, (t + 1) * P)
                    pe.wait_ge(tok_ready, n + 1)
                    pe.transpose(tok_ps[:, 0:P], kt[:, s], c.ident[:, :])
                    pe.transpose(tok_ps[:, P:2 * P], vt[:, s], c.ident[:, :]).then_inc(tok_turned, 1)
                    pe.wait_ge(a_masked, n + 1)
                    pe.matmul(a_ps[:, 0:P], kt[:, s], qt[:, s], start=True, stop=True).then_inc(a_done, 1)
                    if t:
                        out_proj(n - 1, (t - 1) % 2)
                    pe.wait_ge(tok_ready, n + 2)
                    pe.wait_ge(s_ready, n + 1)
                    pe.matmul(s_ps[:, 0:P + 1], tok[k][:, 0:P], tok[k][:, P:2 * P + 1],
                              start=True, stop=True).then_inc(s_done, 1)
                    pe.wait_ge(a_masked, n + 2)
                    pe.wait_ge(o_ready, n + 1)
                    mm = pe.matmul(o_ps[:, 0:P + 1], masked[k][:, :], tok[k][:, P:2 * P + 1],
                                   start=True, stop=(t == 0))
                    if t:
                        mm = pe.matmul(o_ps[:, 0:P + 1], qt[:, s], state[1 - k][:, :], start=False, stop=True)
                    mm.then_inc(o_done, 1)
                out_proj(b * TPB + TPB - 1, (TPB - 1) % 2)

        @block.scalar
        def _(act):
            for first in (v_ready, ot_ready):
                act.sem_inc(first, 1)
            act.wait_ge(setup, 3)
            with act.Fori(0, BATCH) as b:
                for j in range(2):
                    m = b * 2 + j
                    act.wait_ge(projected, m * 4 + 1)
                    act.wait_ge(z_ready, m * 2 + 1)
                    act.activation(half_gate[:, :], c.bank(gate), ACT.Tanh, bias=half_bias[:, 0:1],
                                   scale=0.5).then_inc(tanh_ready, 1)
                    act.wait_ge(projected, m * 4 + 4)
                    act.wait_ge(o_done, b * TPB + 1)
                    act.activation(vt[:, j * BANK:(j + 1) * BANK], c.bank(value), ACT.Identity,
                                   bias=bias[:, value:value + 1]).then_inc(v_ready, 1)
                    act.wait_ge(z_ready, m * 2 + 2)
                    act.wait_ge(qk_ready, m * 2 + 1)
                    act.activation(ezk[:, :], zkmin[:, :], ACT.Exp).then_inc(exp_ready, 1)
                    act.wait_ge(z_ready, m * 2 + 3)
                    act.activation(ez[:, :], zmin[:, :], ACT.Exp).then_inc(exp_ready, 1)
                for t in range(TPB):
                    n, k = b * TPB + t, t % 2
                    act.wait_ge(ot_turned, n + 2)
                    act.copy(ot[k][:, :], ot_ps[:, 0:P]).then_inc(ot_ready, 1)

        @block.vector
        def _(dve):
            for first in (added, qk_ready, tok_ready, a_masked, s_ready, o_ready, z_ready):
                dve.sem_inc(first, 1)
            dve.tensor_scalar(half_bias[:, :], bias[:, gate:gate + 1], 0.5, None, ALU.mult).then_inc(setup, 1)
            for k in range(2):
                dve.memset(tok[k][:, 2 * P:2 * P + 1], 1.0).then_inc(setup, 1)
            with dve.Fori(0, BATCH) as b:
                for j in range(2):
                    m = b * 2 + j
                    dve.wait_ge(tanh_ready, m + 1)
                    dve.tensor_scalar(half_gate[:, :], half_gate[:, :], 0.5, 0.5, ALU.mult, ALU.add).then_inc(den_step, 1)
                    dve.wait_ge(projected, m * 4 + 2)
                    dve.wait_ge(den_step, m * 3 + 1)
                    dve.scalar_tensor_tensor(zk[:, :], c.bank(key), bias[:, key:key + 1], half_gate[:, :],
                                             ALU.add, ALU.mult).then_inc(den_step, 1)
                    dve.wait_ge(projected, m * 4 + 3)
                    dve.tensor_scalar(z[:, :], c.bank(query), bias[:, query:query + 1], None, ALU.add).then_inc(den_step, 1)
                    dve.wait_ge(den_step, m * 3 + 2)
                    dve.tensor_scalar(zkmin[:, :], zk[:, :], 0.0, None, ALU.min).then_inc(z_ready, 1)
                    dve.wait_ge(den_step, m * 3 + 3)
                    dve.tensor_scalar(zmin[:, :], z[:, :], 0.0, None, ALU.min).then_inc(z_ready, 1)
                    dve.wait_ge(o_done, b * TPB + 1)
                    for i, (dst, src, e) in enumerate(((kt, zk, ezk), (qt, z, ez))):
                        dve.wait_ge(exp_ready, m * 2 + 1 + i)
                        dve.scalar_tensor_tensor(dst[:, j * BANK:(j + 1) * BANK], src[:, :], 0.0, e[:, :],
                                                 ALU.max, ALU.add).then_inc(qk_ready, 1)
                    dve.wait_ge(qk_ready, m * 2 + 3)
                for t in range(TPB):
                    n, k = b * TPB + t, t % 2
                    dve.wait_ge(tok_turned, n + 1)
                    if t >= 1:
                        dve.wait_ge(o_done, n)
                    else:
                        dve.wait_ge(o_done, n + 1)
                    dve.tensor_copy(tok[k][:, 0:2 * P], tok_ps[:, 0:2 * P]).then_inc(tok_ready, 1)
                    dve.wait_ge(a_done, n + 1)
                    dve.tensor_tensor(masked[k][:, :], a_ps[:, 0:P], mask[:, :], ALU.mult).then_inc(a_masked, 1)
                    dve.wait_ge(s_done, n + 1)
                    dve.wait_ge(o_done, n + 1)
                    if t:
                        dve.wait_ge(s_ready, n + 1)
                        dve.tensor_tensor(state[k][:, :], s_ps[:, 0:P + 1], state[1 - k][:, :], ALU.add).then_inc(s_ready, 1)
                    else:
                        dve.tensor_copy(state[k][:, :], s_ps[:, 0:P + 1]).then_inc(s_ready, 1)
                    dve.wait_ge(o_done, n + 2)
                    dve.tensor_scalar(rden[k][:, :], o_ps[:, P:P + 1], den_eps, None, ALU.add).then_inc(setup, 1)
                    dve.wait_ge(setup, n * 2 + 4)
                    dve.reciprocal(rden[k][:, :], rden[k][:, :]).then_inc(setup, 1)
                    dve.wait_ge(setup, n * 2 + 5)
                    if t >= 2:
                        dve.wait_ge(ot_turned, n)
                    else:
                        dve.wait_ge(ot_turned, b * TPB + 1)
                    dve.tensor_scalar(o[k][:, :], o_ps[:, 0:P], rden[k][:, 0:1], None, ALU.mult).then_inc(o_ready, 1)
                    if t:
                        dve.wait_ge(y_done, n)
                        dve.tensor_tensor(c.x[:, n - 1, :], c.x[:, n - 1, :], y_ps[:, 0:P], ALU.add).then_inc(added, 1)
                dve.wait_ge(y_done, b * TPB + TPB)
                dve.tensor_tensor(c.x[:, b * TPB + TPB - 1, :], c.x[:, b * TPB + TPB - 1, :], y_ps[:, 0:P],
                                  ALU.add).then_inc(added, 1)


def split_in_three(eng, parts, rest, src, step, at):
    eng.tensor_copy(parts[0], src).then_inc(step, 1)
    eng.wait_ge(step, at + 1)
    eng.tensor_tensor(rest, src, parts[0], ALU.subtract).then_inc(step, 1)
    eng.wait_ge(step, at + 2)
    eng.tensor_copy(parts[1], rest).then_inc(step, 1)
    eng.wait_ge(step, at + 3)
    eng.tensor_tensor(rest, rest, parts[1], ALU.subtract).then_inc(step, 1)
    eng.wait_ge(step, at + 4)
    eng.tensor_copy(parts[2], rest).then_inc(step, 1)


def wide_attention(nc, c, weights, w_out, b_out, y):
    pairs, dh = 4, 64
    units = 2 * TPB
    scale = dh ** -0.5
    with ExitStack() as ctx:
        def sem(what):
            return c.semaphore(f"wide_{what}")

        def sb(what, shape, dt=F32):
            return c.sbuf(ctx, f"wide_{what}", shape, dt)

        w = sb("w", [P, weights.shape[2]])
        q_bias = sb("q_bias", [P, 1])
        qt = [sb(f"qt{k}", [P, SEQ]) for k in range(2)]
        kt, vt = sb("kt", [P, SEQ]), sb("vt", [P, SEQ])
        v = sb("v", [P, TPB, P])
        minus_top = sb("minus_top", [P, TPB, 2])
        l, rest = sb("l", [P, TPB, 2]), sb("rest", [P, TPB, 2])
        e = [sb(f"e{k}", [P, SEQ]) for k in range(2)]
        et = [sb(f"et{k}", [P, 2, TPB, BANK]) for k in range(2)]
        rl3 = sb("rl3", [P, TPB, P], BF16)
        rl3_t = sb("rl3_t", [P, SEQ], BF16)
        spread = sb("spread", [P, P], BF16)
        u = sb("u", [P, SEQ])
        ot = sb("ot", [P, pairs, SEQ])
        score_ps = [c.ps[:, 2 * k:2 * k + 2, :].rearrange("p b n -> p (b n)") for k in range(3)]
        turn_ps, u_ps = [c.bank(6), c.bank(7)], c.bank(7)

        q_bias_ready = sem("q_bias")
        loaded, projected, qkv_ready, v_turned, v_ready, setup = (
            sem(n) for n in ("loaded", "projected", "qkv", "v_turned", "v", "setup"))
        s_done, top_ready, exp_ready, turned, et_dve, et_act = (
            sem(n) for n in ("s", "top", "exp", "turned", "et_dve", "et_act"))
        av_done, u_copied, rl_step, rl_turned, rl_copied, spread_done, scaled, y_done, y_copied = (
            sem(n) for n in ("av", "u", "rl_step", "rl_turned", "rl_copied", "spread", "scaled", "y", "y_copied"))
        block = ctx.enter_context(nc.Block())

        def turned_to(x, half):
            t, h = x // 2, x % 2
            return et[t // TPC][:, h, half * TPC:(half + 1) * TPC, (t % TPC) * P:(t % TPC + 1) * P]

        @block.sync
        def _(sp):
            with sp.Fori(0, BATCH) as b:
                with sp.Fori(0, pairs) as hp:
                    n = b * pairs + hp
                    sp.wait_ge(qkv_ready, n * 4 + 1)
                    sp.dma_start(w[:, :], weights[hp, :, :]).then_inc(loaded, 16)

        @block.tensor
        def _(pe):
            for first in (turned, av_done, y_done):
                pe.sem_inc(first, 1)
            pe.wait_ge(setup, 5)
            with pe.Fori(0, BATCH) as b:
                with pe.Fori(0, pairs) as hp:
                    n = b * pairs + hp
                    pe.wait_ge(loaded, n * 16 + 16)
                    pe.wait_ge(scaled, n + 1)
                    pe.wait_ge(y_copied, b * 2 + 1)
                    for r in range(3):
                        for half in range(2):
                            mm = pe.matmul(c.bank(2 * r + half), w[:, r * P:(r + 1) * P],
                                           c.xt[:, bass.ds(b * SEQ + half * BANK, BANK)], start=True, stop=True)
                        mm.then_inc(projected, 1)

                    def scores(x, half):
                        t, h = x // 2, x % 2
                        if half == 0 and x >= 3:
                            pe.wait_ge(exp_ready, n * units + x - 2)
                        mm = pe.matmul(score_ps[x % 3][:, half * BANK:(half + 1) * BANK], qt[h][:, t * P:(t + 1) * P],
                                       kt[:, half * BANK:(half + 1) * BANK], start=True, stop=True)
                        if half:
                            mm.then_inc(s_done, 1)

                    def turn(x, half):
                        t, h = x // 2, x % 2
                        if half == 0:
                            pe.wait_ge(exp_ready, n * units + x + 1)
                        if h:
                            pe.wait_ge(et_dve, n * units + 2 * t + half + 1)
                        elif t:
                            pe.wait_ge(et_act, n * units + 2 * t + half)
                        if half and x == units // 2 + 1:
                            pe.wait_ge(u_copied, n * 2 + 2)
                        for j in range(TPC):
                            k = half * TPC + j
                            mm = pe.transpose(turn_ps[half][:, j * P:(j + 1) * P], e[x % 2][:, k * P:(k + 1) * P], c.ident[:, :])
                        mm.then_inc(turned, 1)

                    def attend(half):
                        pe.wait_ge(et_dve, n * units + (16 if half else 10))
                        pe.wait_ge(et_act, n * units + 8 * half + 9)
                        pe.wait_ge(u_copied, n * 2 + half + 1)
                        for t in range(TPB):
                            for h in range(2):
                                mm = pe.matmul(u_ps[dh * h:dh * h + dh, :], v[:, t, dh * h:dh * h + dh],
                                               et[half][:, h, t, :], start=(t == 0), stop=(t == TPB - 1))
                        mm.then_inc(av_done, 1)

                    pe.wait_ge(qkv_ready, n * 4 + 4)
                    for x in range(2):
                        for half in range(2):
                            scores(x, half)
                    pe.wait_ge(qkv_ready, n * 4 + 5)
                    for half in range(2):
                        pe.wait_ge(v_ready, n * 2 + half + 1)
                        pe.wait_ge(rl_copied, n + 1)
                        for j in range(TPC):
                            t = half * TPC + j
                            mm = pe.transpose(turn_ps[half][:, j * P:(j + 1) * P], vt[:, t * P:(t + 1) * P], c.ident[:, :])
                        mm.then_inc(v_turned, 1)
                    pe.wait_ge(v_ready, n * 2 + 3)
                    for x in range(units):
                        for half in range(2):
                            if half and x == units // 2 + 1:
                                attend(0)
                            if x + 2 < units:
                                scores(x + 2, half)
                            turn(x, half)
                    attend(1)
                    pe.wait_ge(rl_step, n * 6 + 7)
                    for t in range(TPB):
                        mm = pe.transpose(turn_ps[0].bitcast(BF16)[:, t * P:(t + 1) * P], rl3[:, t, :], c.ident_bf[:, :])
                    mm.then_inc(rl_turned, 1)
                    pe.wait_ge(rl_copied, n + 2)
                    for half in range(2):
                        mm = pe.matmul(score_ps[0][:, half * BANK:(half + 1) * BANK], spread[:, :],
                                       rl3_t[:, half * BANK:(half + 1) * BANK], start=True, stop=True)
                    mm.then_inc(spread_done, 1)
                pe.wait_ge(scaled, b * pairs + pairs + 1)
                for t in range(TPB):
                    out = score_ps[0][:, t * P:(t + 1) * P]
                    for k in range(pairs):
                        pe.matmul(out, ot[:, k, t * P:(t + 1) * P], w_out[:, k, :], start=(k == 0), stop=False)
                    mm = pe.matmul(out, c.ones_row[:, :], b_out[:, :], start=False, stop=True)
                    if t % TPC == TPC - 1:
                        mm.then_inc(y_done, 1)

        @block.scalar
        def _(act):
            for first in (qkv_ready, et_act):
                act.sem_inc(first, 1)
            with act.Fori(0, BATCH) as b:
                with act.Fori(0, pairs) as hp:
                    n = b * pairs + hp
                    act.wait_ge(loaded, n * 16 + 16)
                    act.mul(q_bias[:, :], w[:, 3 * P:3 * P + 1], scale).then_inc(q_bias_ready, 1)
                    act.wait_ge(q_bias_ready, n + 1)
                    act.wait_ge(setup, 5)
                    for h in range(2):
                        rows = slice(dh * h, dh * h + dh)
                        act.wait_ge(projected, n * 3 + 1)
                        act.activation(qt[h][rows, :], score_ps[0][rows, :], ACT.Identity, scale=scale,
                                       bias=q_bias[rows, 0:1]).then_inc(qkv_ready, 1)
                    for j, dst in ((1, kt), (2, vt)):
                        act.wait_ge(projected, n * 3 + j + 1)
                        act.activation(dst[:, :], score_ps[j], ACT.Identity,
                                       bias=w[:, 3 * P + j:3 * P + j + 1]).then_inc(qkv_ready, 1)

                    def exponentials(x):
                        t, h = x // 2, x % 2
                        act.wait_ge(top_ready, n * units + x + 1)
                        act.wait_ge(turned, n * units * 2 + 2 * max(x - 1, 0) + 1)
                        act.activation(e[x % 2][:, :], score_ps[x % 3], ACT.Exp, bias=minus_top[:, t, h:h + 1],
                                       accum_out=l[:, t, h:h + 1]).then_inc(exp_ready, 1)

                    act.wait_ge(rl_step, n * 6 + 1)
                    exponentials(0)
                    for x in range(units):
                        if x + 1 < units:
                            exponentials(x + 1)
                        if x % 2:
                            act.wait_ge(av_done, n * 2 + 1)
                            for half in range(2):
                                act.wait_ge(turned, n * units * 2 + 2 * x + half + 2)
                                act.copy(turned_to(x, half), turn_ps[half].rearrange("p (k i) -> p k i", k=TPC)).then_inc(et_act, 1)

        @block.vector
        def _(dve):
            for first in (scaled, y_copied, u_copied, v_ready, rl_copied, rl_step):
                dve.sem_inc(first, 1)
            dve.memset(rl3[:, :, :], 0.0).then_inc(setup, 1)
            dve.memset(spread[:, :], 0.0).then_inc(setup, 1)
            dve.wait_ge(setup, 2)
            for h in range(2):
                op = dve.memset(spread[dh * h:dh * h + 3, dh * h:dh * h + dh], 1.0)
            op.then_inc(setup, 1)
            for h in range(2):
                dve.memset(qt[h][dh * (1 - h):dh * (2 - h), :], 0.0).then_inc(setup, 1)
            with dve.Fori(0, BATCH) as b:
                with dve.Fori(0, pairs) as hp:
                    n = b * pairs + hp

                    def maxima(x):
                        dve.wait_ge(s_done, n * units + x + 1)
                        dve.tensor_reduce(minus_top[:, x // 2, x % 2:x % 2 + 1], score_ps[x % 3], AX.X, ALU.max,
                                          negate=True).then_inc(top_ready, 1)

                    def copy_u(half):
                        dve.wait_ge(av_done, n * 2 + half + 2)
                        dve.tensor_copy(u[:, half * BANK:(half + 1) * BANK], u_ps).then_inc(u_copied, 1)

                    maxima(0)
                    for half in range(2):
                        dve.wait_ge(v_turned, n * 2 + half + 1)
                        dve.tensor_copy(v[:, half * TPC:(half + 1) * TPC, :].rearrange("p t d -> p (t d)"),
                                        turn_ps[half]).then_inc(v_ready, 1)
                    for x in range(units):
                        if x + 1 < units:
                            maxima(x + 1)
                        if x % 2 == 0:
                            dve.wait_ge(av_done, n * 2 + 1)
                            for half in range(2):
                                dve.wait_ge(turned, n * units * 2 + 2 * x + half + 2)
                                dve.tensor_copy(turned_to(x, half),
                                                turn_ps[half].rearrange("p (k i) -> p k i", k=TPC)).then_inc(et_dve, 1)
                        if x == units // 2 + 1:
                            copy_u(0)
                    dve.wait_ge(exp_ready, n * units + units)
                    dve.reciprocal(l[:, :, :], l[:, :, :]).then_inc(rl_step, 1)
                    dve.wait_ge(rl_step, n * 6 + 2)
                    heads = rl3[:, :, :].rearrange("p t (h k) -> p t h k", h=2)
                    split_in_three(dve, [heads[:, :, :, k] for k in range(3)], rest[:, :, :], l[:, :, :],
                                   rl_step, n * 6 + 2)
                    copy_u(1)
                    dve.wait_ge(rl_turned, n + 1)
                    dve.tensor_copy(rl3_t[:, :], turn_ps[0].bitcast(BF16)).then_inc(rl_copied, 1)
                    dve.wait_ge(u_copied, n * 2 + 3)
                    dve.wait_ge(y_done, b * 2 + 1)
                    dve.wait_ge(spread_done, n + 1)
                    dve.tensor_tensor(ot[:, hp, :], score_ps[0], u[:, :], ALU.mult).then_inc(scaled, 1)
                for k in range(2):
                    dve.wait_ge(y_done, b * 2 + k + 2)
                    dve.tensor_copy(y[:, bass.ds(b * TPB + k * TPC, TPC), :].rearrange("p t d -> p (t d)"),
                                    c.bank(k)).then_inc(y_copied, 1)


def add_normed(nc, c, y, gain, shift):
    with ExitStack() as ctx:
        step = c.semaphore("post_step")
        block = ctx.enter_context(nc.Block())

        @block.vector
        def _(dve):
            every = [P, TILES, D]
            dve.tensor_tensor(y[:, :, :], y[:, :, :], gain[:, :].unsqueeze(1).to_broadcast(every), ALU.mult).then_inc(step, 1)
            dve.tensor_tensor(c.xn[:, :, :], c.xn[:, :, :], shift[:, :].unsqueeze(1).to_broadcast(every), ALU.add).then_inc(step, 1)
            dve.wait_ge(step, 2)
            dve.tensor_tensor(y[:, :, :], y[:, :, :], c.xn[:, :, :], ALU.add).then_inc(step, 1)
            dve.wait_ge(step, 3)
            dve.scalar_tensor_tensor(c.x[:, :, :], y[:, :, :], 2 ** -0.5, c.x[:, :, :], ALU.mult, ALU.add)


def quantise_fp4(dve, act, src, dst, blocks, bufs, step, signs_ready, at, n):
    views = {k: b[:, 0:blocks * 16].rearrange("p (b k) -> p b k", k=16) for k, b in bufs.items() if k != "scale"}
    scale, inv = bufs["scale"][:, 0, 0:blocks], bufs["scale"][:, 1, 0:blocks]
    signs, size, big, small = views["signs"], views["size"], views["big"], views["small"]
    if act is not None:
        act.wait_ge(step, at + 1)
        act.activation(signs, src, ACT.Sign).then_inc(signs_ready, 1)
        act.wait_ge(step, at + 4)
        act.activation(size, size, ACT.Abs).then_inc(signs_ready, 1)
        return
    every = [P, blocks, 16]

    def per_block(a):
        return a.rearrange("p (b o) -> p b o", o=1).to_broadcast(every)

    dve.tensor_reduce(scale, src, AX.X, ALU.max, apply_absolute_value=True).then_inc(step, 1)
    dve.wait_ge(step, at + 1)
    dve.tensor_scalar(scale, scale, 1.0 / 6.0, 1e-12, ALU.mult, ALU.max).then_inc(step, 1)
    dve.wait_ge(step, at + 2)
    dve.reciprocal(inv, scale).then_inc(step, 1)
    dve.wait_ge(step, at + 3)
    dve.tensor_tensor(size, src, per_block(inv), ALU.mult).then_inc(step, 1)
    dve.wait_ge(signs_ready, 2 * n + 2)
    dve.tensor_scalar(big, size, 5.0, 2.0, ALU.is_gt, ALU.mult).then_inc(step, 1)
    dve.tensor_scalar(small, size, 1.75, None, ALU.is_gt).then_inc(step, 1)
    now = at + 6
    for chain, mids in ((big, (3.5, 2.5)), (small, (1.25, 0.75, 0.25))):
        for mid in mids:
            dve.wait_ge(step, now)
            dve.scalar_tensor_tensor(chain, size, mid, chain, ALU.is_gt, ALU.add).then_inc(step, 1)
            now += 1
    dve.wait_ge(step, now)
    dve.scalar_tensor_tensor(small, big, 2.0, small, ALU.mult, ALU.add).then_inc(step, 1)
    dve.wait_ge(step, now + 1)
    dve.scalar_tensor_tensor(small, small, 0.5, signs, ALU.mult, ALU.mult).then_inc(step, 1)
    dve.wait_ge(step, now + 2)
    dve.tensor_tensor(dst, small, per_block(scale), ALU.mult).then_inc(step, 1)


FP4_STEPS = 14


def fp4_mlp(nc, c, w):
    hidden = 352
    tiles_h = 3
    width = [min(P, hidden - f * P) for f in range(tiles_h)]
    gate_at, up_at, down_at = 0, tiles_h * P, 2 * tiles_h * P
    total = down_at + hidden
    with ExitStack() as ctx:
        def sem(what):
            return c.semaphore(f"fp4_{what}")

        def sb(what, shape):
            return c.sbuf(ctx, f"fp4_{what}", shape)

        bufs = {k: sb(k, [P, TOKENS]) for k in ("signs", "size", "big", "small")}
        bufs["scale"] = sb("scale", [P, 2, P])
        wt = sb("wt", [P, 2, tiles_h * P])
        down = sb("down", [P, tiles_h, P])
        gated = [sb(f"gated{k}", [P, hidden]) for k in range(2)]
        h = [sb(f"h{k}", [P, TPC, hidden]) for k in range(2)]
        ht = sb("ht", [P, tiles_h, BANK])
        step, signs, turned, copied = sem("step"), sem("signs"), sem("turned"), sem("copied")
        gate_done, up_done, gate_act, h_ready = sem("gate"), sem("up"), sem("gate_act"), sem("h")
        h_turned, ht_ready, y_done, added = sem("h_turned"), sem("ht"), sem("y"), sem("added")
        block = ctx.enter_context(nc.Block())

        def blocked(ap):
            return ap.rearrange("p (b k) -> p b k", k=16)

        w_in = blocked(w[:, :])
        x_in = blocked(c.xn[:, :, :].rearrange("p t d -> p (t d)"))

        def jobs(g):
            if g == 0:
                return w_in, w_in, total // 16
            if g == 1:
                return x_in, x_in, TOKENS // 16
            hh = h[g % 2][:, :, :].rearrange("p t f -> p (t f)")
            return blocked(hh), blocked(hh), TPC * hidden // 16

        @block.tensor
        def _(pe):
            pe.wait_ge(step, FP4_STEPS)
            for f in range(tiles_h):
                for which, at in enumerate((gate_at, up_at)):
                    pe.transpose(c.bank(which)[:, f * P:(f + 1) * P], w[:, at + f * P:at + (f + 1) * P], c.ident[:, :])
                mm = pe.transpose(c.bank(2)[0:width[f], f * P:(f + 1) * P],
                                  w[:, down_at + f * P:down_at + f * P + width[f]], c.ident[:, :])
            mm.then_inc(turned, 1)
            pe.wait_ge(step, 2 * FP4_STEPS)
            for t in range(TILES):
                mm = pe.transpose(c.bank(4 + t // TPC)[:, t % TPC * P:(t % TPC + 1) * P], c.xn[:, t, :], c.ident[:, :])
                if t % TPC == TPC - 1:
                    mm.then_inc(turned, 1)
            pe.wait_ge(copied, 3 + CHUNKS)

            def tail(g):
                pe.wait_ge(step, (3 + g) * FP4_STEPS)
                wait_from(pe, ht_ready, tiles_h * g)
                for f in range(tiles_h):
                    for j in range(TPC):
                        mm = pe.transpose(c.bank(4 + f)[0:width[f], j * P:(j + 1) * P],
                                          h[g % 2][:, j, f * P:f * P + width[f]], c.ident[:, :])
                    mm.then_inc(h_turned, 1)
                wait_from(pe, added, g)
                pe.wait_ge(ht_ready, tiles_h * (g + 1))
                for j in range(TPC):
                    for f in range(tiles_h):
                        mm = pe.matmul(c.bank(7)[:, j * P:(j + 1) * P], ht[0:width[f], f, j * P:(j + 1) * P],
                                       down[0:width[f], f, :], start=(f == 0), stop=(f == tiles_h - 1))
                mm.then_inc(y_done, 1)

            for g in range(CHUNKS):
                for j in range(TPC):
                    t = g * TPC + j
                    wait_from(pe, gate_act, t - 1)
                    pe.matmul(c.bank(t % 2)[:, 0:hidden], c.xt[:, t * P:(t + 1) * P], wt[:, 0, 0:hidden],
                              start=True, stop=True).then_inc(gate_done, 1)
                    wait_from(pe, h_ready, t - 1)
                    pe.matmul(c.bank(2 + t % 2)[:, 0:hidden], c.xt[:, t * P:(t + 1) * P], wt[:, 1, 0:hidden],
                              start=True, stop=True).then_inc(up_done, 1)
                if g:
                    tail(g - 1)
            tail(CHUNKS - 1)

        @block.scalar
        def _(act):
            def signs_of(n):
                src, dst, blocks = jobs(n)
                quantise_fp4(None, act, src, dst, blocks, bufs, step, signs, n * FP4_STEPS, n)

            def gates(g):
                for j in range(TPC):
                    t = g * TPC + j
                    act.wait_ge(gate_done, t + 1)
                    wait_from(act, h_ready, t - 1)
                    act.activation(gated[t % 2][:, :], c.bank(t % 2)[:, 0:hidden], ACT.Silu).then_inc(gate_act, 1)

            signs_of(0)
            act.wait_ge(turned, 1)
            act.copy(wt[:, 0, :], c.bank(0)[:, 0:tiles_h * P]).then_inc(copied, 1)
            act.copy(wt[:, 1, :], c.bank(1)[:, 0:tiles_h * P]).then_inc(copied, 1)
            signs_of(1)
            for g in range(CHUNKS):
                act.wait_ge(turned, 2 + g)
                act.copy(c.xt[:, g * BANK:(g + 1) * BANK], c.bank(4 + g)).then_inc(copied, 1)
            gates(0)
            for g in range(CHUNKS):
                signs_of(g + 2)
                if g + 1 < CHUNKS:
                    gates(g + 1)
                wait_from(act, y_done, g)
                for f in range(tiles_h):
                    act.wait_ge(h_turned, tiles_h * g + f + 1)
                    act.copy(ht[0:width[f], f, :], c.bank(4 + f)[0:width[f], :]).then_inc(ht_ready, 1)

        @block.vector
        def _(dve):
            def products(g):
                wait_from(dve, h_turned, tiles_h * (g - 1))
                for j in range(TPC):
                    t = g * TPC + j
                    dve.wait_ge(gate_act, t + 1)
                    dve.wait_ge(up_done, t + 1)
                    dve.tensor_tensor(h[g % 2][:, j, :], c.bank(2 + t % 2)[:, 0:hidden], gated[t % 2][:, :],
                                      ALU.mult).then_inc(h_ready, 1)
            def quantise(n):
                src, dst, blocks = jobs(n)
                quantise_fp4(dve, None, src, dst, blocks, bufs, step, signs, n * FP4_STEPS, n)

            def add(g):
                dve.wait_ge(y_done, g + 1)
                x = c.x[:, g * TPC:(g + 1) * TPC, :].rearrange("p t d -> p (t d)")
                dve.tensor_tensor(x, x, c.bank(7), ALU.add).then_inc(added, 1)

            quantise(0)
            dve.wait_ge(turned, 1)
            for f in range(tiles_h):
                op = dve.tensor_copy(down[0:width[f], f, :], c.bank(2)[0:width[f], f * P:(f + 1) * P])
            op.then_inc(copied, 1)
            quantise(1)
            products(0)
            for g in range(CHUNKS):
                dve.wait_ge(h_ready, TPC * (g + 1))
                wait_from(dve, step, (g + 2) * FP4_STEPS)
                quantise(g + 2)
                if g + 1 < CHUNKS:
                    products(g + 1)
                if g:
                    add(g - 1)
            add(CHUNKS - 1)


HEADS, DH = 16, 8
NARROW = BATCH * HEADS
SCALE = DH ** -0.5
BLK = 64
NBLK = SEQ // BLK
FAR = -1e30
MASK_ROW, TOP_ROW = 64, 96
Q_PARTS, K_PARTS = (0, 0, 0, 1, 1, 2), (0, 1, 2, 0, 1, 0)


def narrow_clears(k_stack, v):
    two = float(np.array([0xBF80BF80], np.uint32).view(np.float32)[0])
    return ((k_stack[:, :, :].rearrange("p n i -> p (n i)").bitcast(F32), two),
            (v[:, :, :, :].rearrange("p n t d -> p (n t d)"), 0.0))


def narrow_prepare(nc, c, w, tables, q_stack, k_stack, v, diag):
    rotated = tables is not None
    with ExitStack() as ctx:
        def sem(what):
            return c.semaphore(f"{'rot' if rotated else 'blk'}_{what}")

        def sb(what, shape, dt=F32):
            return c.sbuf(ctx, f"prep_{'rot' if rotated else 'blk'}_{what}", shape, dt)

        full = [sb(f"full{k}", [P, BANK]) for k in range(2)]
        parts = [[sb(f"parts{k}{s}", [P, 3, BANK], BF16) for s in range(2)] for k in range(2)]
        rest = [sb(f"rest{k}", [P, BANK]) for k in range(2)]
        scratch = [nc.dram_tensor(f"parts_{'rot' if rotated else 'blk'}{k}", (D, 3, TOKENS), BF16, kind="Internal")
                   for k in range(2)]
        if rotated:
            cos, sin, bias, v_bias = tables
            turned_part = sb("turned", [P, BANK])
        else:
            onehot, headsel, q_tok = sb("onehot", [P, SEQ]), sb("headsel", [P, HEADS]), sb("q_tok", [P, BANK])
            sums, ksum, qsum_heads = sb("sums", [P, 2, NBLK]), sb("ksum", [P, P]), sb("qsum_heads", [P, HEADS, NBLK])
            masks = sb("masks", [P, HEADS * NBLK])
        cleared, projected, full_ready, rope_step = sem("cleared"), sem("projected"), sem("full"), sem("rope")
        split = [sem("q_split"), sem("k_split")]
        written = [[sem(f"written{k}{s}") for s in range(2)] for k in range(2)]
        v_ready, tok_ready, diag_step = sem("v"), sem("tok"), sem("diag")
        sums_ready, mask_done, mask_step, mask_rows, const, hot = (
            sem("sums"), sem("mask_done"), sem("mask_step"), sem("mask_rows"), sem("const"), sem("hot"))
        stacked_dma, hot_copied = sem("stacked_dma"), sem("hot_copied")
        all_cleared = 2 if rotated else 3
        block = ctx.enter_context(nc.Block())

        @block.tensor
        def _(pe):
            for g in range(CHUNKS):
                x = c.xt[:, g * BANK:(g + 1) * BANK]
                for k in range(2):
                    wait_from(pe, full_ready, 2 * (g - 1) + k + 1)
                    if rotated:
                        pe.matmul(c.bank(2 * k), w[:, 2 * k * P:(2 * k + 1) * P], x, start=True, stop=True)
                        pe.matmul(c.bank(2 * k + 1), w[:, (2 * k + 1) * P:(2 * k + 2) * P], x,
                                  start=True, stop=True).then_inc(projected, 1)
                    else:
                        pe.matmul(c.bank(2 * k), w[:, k * P:(k + 1) * P], x, start=True, stop=True).then_inc(projected, 1)
                wait_from(pe, v_ready, g)
                wait_from(pe, tok_ready, g if not rotated else 0)
                wait_from(pe, diag_step, 2 * g - 1 if not rotated else 0)
                at = 4 * P if rotated else 2 * P
                for j in range(TPC):
                    t = g * TPC + j
                    cols = slice(j * P, (j + 1) * P)
                    mm = pe.matmul(c.bank(4)[:, cols], c.xt[:, t * P:(t + 1) * P], w[:, at:at + P],
                                   start=True, stop=not rotated)
                    if rotated:
                        mm = pe.matmul(c.bank(4)[:, cols], c.ones_row[:, :], v_bias[:, :], start=False, stop=True)
                    else:
                        for k in range(2):
                            mm = pe.matmul(c.bank(6 + k)[:, cols], c.xt[:, t * P:(t + 1) * P],
                                           w[:, k * P:(k + 1) * P], start=True, stop=True)
                mm.then_inc(projected, 1)
                if not rotated and g % 2:
                    pe.wait_ge(mask_step, g // 2 * 4 + 2)
                    pe.matmul(c.bank(1)[:, 0:HEADS * NBLK], ksum[:, :], qsum_heads[:, :, :].rearrange("p h b -> p (h b)"),
                              start=True, stop=True).then_inc(mask_done, 1)

        @block.scalar
        def _(act):
            act.wait_ge(cleared, all_cleared)
            if not rotated:
                act.wait_ge(const, 32)
                act.copy(k_stack[MASK_ROW:MASK_ROW + NBLK, 0, :], onehot[MASK_ROW:MASK_ROW + NBLK, :]).then_inc(hot, 1)
                act.wait_ge(hot, 1)
                rest_of = [NBLK, NARROW - 1, SEQ]
                act.dma_start(k_stack[MASK_ROW:MASK_ROW + NBLK, 1:NARROW, :],
                              k_stack[MASK_ROW:MASK_ROW + NBLK, 0:1, :].to_broadcast(rest_of)).then_inc(hot_copied, 16)
            for g in range(CHUNKS):
                b, t0 = g // 2, g % 2 * TPC
                if not rotated:
                    for k in range(2):
                        act.wait_ge(projected, 3 * g + k + 1)
                        wait_from(act, split[k], 5 * g)
                        wait_from(act, sums_ready, 2 * (g - 1) + k + 1)
                        act.copy(full[k][:, :], c.bank(2 * k)).then_inc(full_ready, 1)
                act.wait_ge(projected, 3 * g + 3)
                values = c.bank(4).rearrange("p (t h d) -> p h t d", t=TPC, h=HEADS)
                heads = slice(b * HEADS, (b + 1) * HEADS)
                if rotated:
                    act.copy(v[:, heads, t0:t0 + TPC, 0:DH], values).then_inc(v_ready, 1)
                else:
                    wait_from(act, diag_step, 2 * (g - 1) + 1)
                    act.copy(q_tok[:, :], c.bank(6)).then_inc(tok_ready, 1)
                    for s in range(2):
                        rows = slice(s * BLK, (s + 1) * BLK)
                        op = act.copy(v[rows, heads, t0:t0 + TPC, s * DH:(s + 1) * DH], values[rows])
                    op.then_inc(v_ready, 1)
                    if g % 2:
                        rows = slice(MASK_ROW, MASK_ROW + NBLK)
                        act.wait_ge(mask_step, g // 2 * 4 + 4)
                        act.copy(q_stack[rows, heads, :].rearrange("p h (b i) -> p (h b) i", i=BLK),
                                 masks[rows, :].rearrange("p (n o) -> p n o", o=1).to_broadcast([NBLK, HEADS * NBLK, BLK])).then_inc(mask_rows, 1)
            if not rotated:
                act.wait_ge(hot_copied, 16)

        @block.vector
        def _(dve):
            if not rotated:
                dve.memset(ksum[:, :], 0.0).then_inc(cleared, 1)
                dve.wait_ge(cleared, all_cleared)
                dve.wait_ge(const, 32)
            for g in range(CHUNKS):
                b, s = g // 2, g % 2
                pos = slice(s * BANK, (s + 1) * BANK)
                if rotated:
                    for k in range(2):
                        n = 2 * g + k
                        dve.wait_ge(projected, 3 * g + k + 1)
                        wait_from(dve, rope_step, 3 * n)
                        wait_from(dve, split[k], 5 * g)
                        dve.scalar_tensor_tensor(full[k][:, :], c.bank(2 * k), bias[:, 2 * k:2 * k + 1], cos[:, pos],
                                                 ALU.add, ALU.mult).then_inc(rope_step, 1)
                        dve.scalar_tensor_tensor(turned_part[:, :], c.bank(2 * k + 1), bias[:, 2 * k + 1:2 * k + 2],
                                                 sin[:, pos], ALU.add, ALU.mult).then_inc(rope_step, 1)
                        dve.wait_ge(rope_step, 3 * n + 2)
                        dve.tensor_tensor(full[k][:, :], full[k][:, :], turned_part[:, :], ALU.add).then_inc(rope_step, 1)
                        dve.wait_ge(rope_step, 3 * n + 3)
                        dve.sem_inc(full_ready, 1)
                dve.wait_ge(full_ready, 2 * g + 1)
                wait_from(dve, written[0][s], 16 * b)
                split_in_three(dve, [parts[0][s][:, k, :] for k in range(3)], rest[0][:, :], full[0][:, :], split[0], 5 * g)
                if not rotated:
                    dve.wait_ge(full_ready, 2 * g + 2)
                    wait_from(dve, mask_step, 4 * b)
                    for k in range(2):
                        out = sums[:, k, s * NBLK // 2:(s + 1) * NBLK // 2]
                        dve.tensor_reduce(out, full[k][:, :].rearrange("p (b i) -> p b i", i=BLK), AX.X,
                                          ALU.add).then_inc(sums_ready, 1)
                    dve.wait_ge(tok_ready, g + 1)
                    dve.wait_ge(split[0], 5 * g + 5)
                    dve.tensor_tensor(rest[0][:, :], c.bank(7), q_tok[:, :], ALU.mult).then_inc(diag_step, 1)
                    dve.wait_ge(diag_step, 2 * g + 1)
                    dve.tensor_reduce(diag[:, b * HEADS:(b + 1) * HEADS, s * TPC:(s + 1) * TPC],
                                      rest[0][:, :].rearrange("p (t h d) -> p h t d", t=TPC, h=HEADS), AX.X,
                                      ALU.add).then_inc(diag_step, 1)
                    if s:
                        dve.wait_ge(sums_ready, 2 * g + 2)
                        dve.tensor_copy(ksum[:, MASK_ROW:MASK_ROW + NBLK], sums[:, 1, :]).then_inc(mask_step, 1)
                        shape = [P, HEADS, NBLK]
                        dve.tensor_tensor(qsum_heads[:, :, :], sums[:, 0:1, :].to_broadcast(shape),
                                          headsel[:, :].rearrange("p (h o) -> p h o", o=1).to_broadcast(shape),
                                          ALU.mult).then_inc(mask_step, 1)
                        rows = slice(MASK_ROW, MASK_ROW + NBLK)
                        dve.wait_ge(mask_done, b + 1)
                        wait_from(dve, mask_rows, b)
                        dve.tensor_scalar(masks[rows, :], c.bank(1)[rows, 0:HEADS * NBLK], SCALE / BLK ** 2, 0.01,
                                          ALU.mult, ALU.is_le).then_inc(mask_step, 1)
                        dve.wait_ge(mask_step, b * 4 + 3)
                        dve.tensor_scalar(masks[rows, :], masks[rows, :], FAR, None, ALU.mult).then_inc(mask_step, 1)

        @block.gpsimd
        def _(pool):
            width = v.shape[3]
            pool.memset(v[:, :, :, width - 1:width], 1.0).then_inc(cleared, 1)
            pool.memset(q_stack[:, :, :].rearrange("p n i -> p (n i)").bitcast(F32), 0.0).then_inc(cleared, 1)
            for g in range(CHUNKS):
                pool.wait_ge(full_ready, 2 * g + 2)
                wait_from(pool, written[1][g % 2], 16 * (g // 2))
                split_in_three(pool, [parts[1][g % 2][:, k, :] for k in range(3)], rest[1][:, :], full[1][:, :],
                               split[1], 5 * g)

        @block.sync
        def _(sp):
            if not rotated:
                sp.dma_start(onehot[MASK_ROW:MASK_ROW + NBLK, :], c.ins["l2a_onehot"]).then_inc(const, 16)
                sp.dma_start(headsel[:, :], c.ins["l2a_headsel"]).then_inc(const, 16)
            for g in range(CHUNKS):
                for k in range(2):
                    sp.wait_ge(split[k], 5 * g + 5)
                    sp.dma_start(scratch[k][:, :, g * BANK:(g + 1) * BANK], parts[k][g % 2][:, :, :]).then_inc(written[k][g % 2], 16)
                if g % 2:
                    b = g // 2
                    sp.wait_ge(cleared, all_cleared)
                    for k, (which, stack) in enumerate(((Q_PARTS, q_stack), (K_PARTS, k_stack))):
                        for s in range(2):
                            sp.wait_ge(written[k][s], 16 * (b + 1))
                        for r in range(6):
                            src = scratch[k][:, which[r], b * SEQ:(b + 1) * SEQ].rearrange("(h d) t -> d h t", d=DH)
                            sp.dma_start(stack[r * DH:(r + 1) * DH, b * HEADS:(b + 1) * HEADS, :], src).then_inc(stacked_dma, 16)
            sp.wait_ge(stacked_dma, 16 * 12 * BATCH)


def narrow_attention(nc, c, causal, q_stack, k_stack, v, diag, raw, w_out, b_out):
    name = "cau" if causal else "blm"
    threshold = 0.01
    cols = v.shape[3]
    sets = 1 if causal else 2
    keys_apart = 4 * sets
    u_cols = keys_apart * cols
    if causal:
        first_units = [(t, lo, min((t + 1) * P, lo + BANK)) for t in range(TPB) for lo in range(0, (t + 1) * P, BANK)]
        second_units = [(iq, j, min(j + 4, 2 * iq + 2)) for iq in range(4) for j in range(0, 2 * iq + 2, 4)]
    else:
        first_units = [(t, lo, lo + BANK) for t in range(TPB) for lo in (0, BANK)]
        second_units = [(iq, j, j + 4) for iq in range(4) for j in (0, 4)]
    P1, P2 = len(first_units), len(second_units)
    last_of = [max(w for w, u in enumerate(second_units) if u[0] == iq) for iq in range(4)]
    with ExitStack() as ctx:
        def sem(what):
            return c.semaphore(f"{name}_{what}")

        def sb(what, shape, dt=F32):
            return c.sbuf(ctx, f"{name}_{what}", shape, dt)

        o = c.xn[:, :, :].rearrange("p t d -> p (t d)").rearrange("p (n t d) -> p n t d", n=NARROW, t=TPB)
        e = [c.xt[:, :].rearrange("p (j i) -> p j i", j=TPB), sb("e", [P, TPB, 2 * P])[:, :, :]]
        ut = [sb(f"ut{k}", [P, sets * 2 * P]) for k in range(2)]
        u = [sb(f"u{k}", [P, TPB, u_cols]) for k in range(2)]
        v_now = [sb(f"v_now{k}", [P, TPB, 32]) for k in range(2)]
        tops = sb("tops", [P, TPB, 2 if causal else NBLK])
        top, top_rest = sb("top", [P, TPB]), sb("top_rest", [P, TPB])
        top3 = sb("top3", [P, TPB, P], BF16)
        l = sb("l", [P, TPB])
        ot = sb("ot", [P, BANK])
        if causal:
            masks = sb("masks", [P, 5 * P], BF16)
            total = sb("total", [P, TPB, DH + 1])
        else:
            diff = [sb(f"diff{k}", [P, TPB, NBLK + 1]) for k in range(2)]
            on = [sb(f"on{k}", [P, TPB]) for k in range(2)]
            off, keep_own = sb("off", [P, TPB]), sb("keep_own", [P, TPB])
            prob, big = sb("prob", [P, TPB, NBLK]), sb("big", [P, TPB * NBLK], BF16)
            keep, kept = sb("keep", [P, TPB, NBLK]), sb("kept", [P, TPB * TPB, 2, DH])
            total, own = sb("total", [P, TPB, DH]), sb("own", [P, TPB, DH])
            same_block = sb("same_block", [P, P], BF16)
        first_ps = [c.bank(k) for k in range(2)]
        second_ps = [c.ps[:, 2 + 2 * k:4 + 2 * k, :].rearrange("p b n -> p (b n)") for k in range(2)]
        av_ps, turn_ps = c.bank(6), c.bank(7)

        kept_ready, pool_held = sem("kept"), sem("pool_held")
        v_ready, ut_ready, u_turned = sem("v_ready"), sem("ut"), sem("u_turned")
        setup, held, s1_done, maxed, top_step, top_turned, rows_ready = (
            sem(x) for x in ("setup", "held", "s1", "maxed", "top_step", "top_turned", "rows"))
        s2_done, exp_done, av_done, u_copied, near_exp, counted, post = (
            sem(x) for x in ("s2", "exp", "av", "u", "near", "counted", "post"))
        regrouped, o_turned, ot_ready, y_done, added = (sem(x) for x in ("regrouped", "o_turned", "ot", "y", "added"))
        TOP_STEPS = 6 if causal else 11
        POST_A, POST_B = (3, 0) if causal else (7, 8)
        POST = POST_A + POST_B
        block = ctx.enter_context(nc.Block())

        def rows_of_quarter(iq):
            return 2 * 32 if causal and iq == 0 else P

        def each_head(eng, body):
            body(0, 0, True)
            with eng.Fori(0, NARROW // 2 - 1) as i:
                body(i * 2 + 1, 1, True)
                body(i * 2 + 2, 0, True)
            body(NARROW - 1, 1, False)

        @block.tensor
        def _(pe):
            def first(n, x):
                t, lo, hi = first_units[x]
                out = first_ps[x % 2]
                wait_from(pe, maxed, n * P1 + x - 1)
                pe.sem_inc(held, 1)
                q = q_stack[:, bass.ds(n, 1), t * P:(t + 1) * P].rearrange("p o i -> p (o i)")

                def keys(a, b):
                    return k_stack[:, bass.ds(n, 1), a:b].rearrange("p o i -> p (o i)")
                if causal and hi == (t + 1) * P:
                    if hi - P > lo:
                        pe.matmul(out[:, 0:hi - P - lo], q, keys(lo, hi - P), start=True, stop=True)
                    pe.matmul(out[:, hi - P - lo:hi - lo], q, keys(hi - P, hi), start=True, stop=False)
                    mm = pe.matmul(out[:, hi - P - lo:hi - lo], c.ident_bf[:, :], masks[:, 0:P], start=False, stop=True)
                else:
                    mm = pe.matmul(out[:, 0:hi - lo], q, keys(lo, hi), start=True, stop=True)
                mm.then_inc(s1_done, 1)

            def second(n, x):
                iq, j0, j1 = second_units[x]
                wait_from(pe, exp_done, n * P2 + x - 1)
                pe.sem_inc(held, 1)
                q = q_stack[:, bass.ds(n, 1), iq * 2 * P:(iq + 1) * 2 * P].rearrange("p o i -> p (o i)")
                for j in range(j0, j1):
                    out = second_ps[x % 2][:, (j - j0) * 2 * P:(j - j0 + 1) * 2 * P]
                    k = k_stack[:, bass.ds(n, 1), j * P:(j + 1) * P].rearrange("p o i -> p (o i)")
                    masked = causal and j >= 2 * iq
                    mm = pe.matmul(out, k, q, start=True, stop=not masked)
                    if masked:
                        at = P + (j - 2 * iq) * 2 * P
                        mm = pe.matmul(out, c.ident_bf[:, :], masks[:, at:at + 2 * P], start=False, stop=True)
                mm.then_inc(s2_done, 1)

            def turn_top(n):
                pe.wait_ge(top_step, (n + 1) * TOP_STEPS)
                wait_from(pe, u_copied, n * 4 - 1)
                for t in range(TPB):
                    mm = pe.transpose(turn_ps.bitcast(BF16)[:, t * P:(t + 1) * P], top3[:, t, :], c.ident_bf[:, :])
                mm.then_inc(top_turned, 1)

            def attend(n, k, iq):
                if iq == 0:
                    pe.wait_ge(v_ready, n + 1)
                pe.wait_ge(exp_done, n * P2 + last_of[iq] + 1)
                wait_from(pe, ut_ready, n * 4 + iq)
                tiles = 2 * iq + 2 if causal else TPB
                for j in range(tiles):
                    at = 0 if causal else j // 4 * 2 * P
                    mm = pe.matmul(av_ps[j % 4 * 32:j % 4 * 32 + 32, at:at + 2 * P], v_now[k][:, j, :],
                                   e[iq % 2][:, j, :], start=(j < 4 or not causal), stop=(j + 4 >= tiles or not causal))
                mm.then_inc(av_done, 1)

            def turn_u(n, iq):
                pe.wait_ge(ut_ready, n * 4 + iq + 1)
                if iq == 1 and not causal and not (isinstance(n, int) and n == 0):
                    pe.wait_ge(post, (n - 1) * POST + POST_A + 2)
                elif iq == 3 and not (isinstance(n, int) and n == NARROW - 1):
                    pe.wait_ge(rows_ready, n + 2)
                else:
                    wait_from(pe, u_copied, n * 4 + iq)
                for i in range(2):
                    for x in range(sets):
                        at = (i * sets + x) * P
                        mm = pe.transpose(turn_ps[:, at:at + P], ut[iq % 2][:, (x * 2 + i) * P:(x * 2 + i + 1) * P],
                                          c.ident[:, :])
                mm.then_inc(u_turned, 1)

            def count(n):
                last = isinstance(n, int) and n == NARROW - 1
                pe.wait_ge(u_copied, NARROW * 4 if last else n * 4 + 5)
                pe.wait_ge(post, n * POST + POST_A + 1)
                pe.matmul(turn_ps[:, 0:TPB * NBLK], same_block[:, :], big[:, :], start=True, stop=True).then_inc(counted, 1)

            pe.wait_ge(setup, 6)
            for x in range(P1):
                first(0, x)

            turn_top(0)

            def step(n, k, more):
                started = not (isinstance(n, int) and n == 0)
                ahead = list(range(P1)) if more else []

                def firsts(count):
                    for x in range(min(count, len(ahead))):
                        first(n + 1, ahead.pop(0))
                firsts(1)
                if started:
                    attend(n - 1, 1 - k, 3)
                firsts(1)
                pe.wait_ge(rows_ready, n + 1)
                for x in range(P2):
                    second(n, x)
                    firsts(2)
                    if x == 4 and not causal and started:
                        count(n - 1)
                    if x == 0 and started:
                        turn_u(n - 1, 3)
                    for iq in range(3):
                        if last_of[iq] + 2 == x:
                            turn_u(n, iq)
                    for iq in range(3):
                        if last_of[iq] + 1 == x:
                            attend(n, k, iq)
                firsts(P1)
                if more:
                    turn_top(n + 1)

            each_head(pe, step)
            attend(NARROW - 1, 1, 3)
            turn_u(NARROW - 1, 3)
            if not causal:
                count(NARROW - 1)
            for g in range(CHUNKS):
                if g == 0:
                    pe.wait_ge(regrouped, BATCH)
                wait_from(pe, ot_ready, g)
                for j in range(TPC):
                    t = g * TPC + j
                    mm = pe.transpose(c.bank(0)[:, j * P:(j + 1) * P], c.xt[:, t * P:(t + 1) * P], c.ident[:, :])
                mm.then_inc(o_turned, 1)
                pe.wait_ge(ot_ready, g + 1)
                wait_from(pe, added, g)
                for j in range(TPC):
                    out = c.bank(1)[:, j * P:(j + 1) * P]
                    mm = pe.matmul(out, ot[:, j * P:(j + 1) * P], w_out[:, :], start=True, stop=b_out is None)
                    if b_out is not None:
                        mm = pe.matmul(out, c.ones_row[:, :], b_out[:, :], start=False, stop=True)
                mm.then_inc(y_done, 1)

        @block.scalar
        def _(act):
            def copy_ut(n, iq):
                act.wait_ge(av_done, n * 4 + iq + 1)
                wait_from(act, u_turned, n * 4 + iq - 1)
                rows = rows_of_quarter(iq)
                act.copy(ut[iq % 2][0:rows, :], av_ps[0:rows, 0:sets * 2 * P]).then_inc(ut_ready, 1)

            def copy_u(n, k, iq):
                act.wait_ge(u_turned, n * 4 + iq + 1)
                if iq == 0:
                    wait_from(act, post, (n - 1) * POST + 1)
                here = rows_of_quarter(iq) // 32 * sets
                act.copy(u[k][:, 2 * iq:2 * iq + 2, :].rearrange("p t (m c) -> p t m c", c=cols)[:, :, 0:here, :],
                         turn_ps[:, 0:2 * sets * P].rearrange("p (t m c) -> p t m c", t=2, c=32)[:, :, 0:here, 0:cols]
                         ).then_inc(u_copied, 1)

            act.wait_ge(setup, 6)

            def step(n, k, more):
                if not (isinstance(n, int) and n == 0):
                    copy_ut(n - 1, 3)
                if not causal:
                    act.wait_ge(top_step, (n + 1) * TOP_STEPS)
                    act.activation(diff[k][:, :, :], diff[k][:, :, :], ACT.Exp, scale=SCALE).then_inc(near_exp, 1)
                for x, (iq, j0, j1) in enumerate(second_units):
                    act.wait_ge(s2_done, n * P2 + x + 1)
                    wait_from(act, av_done, n * 4 + iq - 1)
                    act.activation(e[iq % 2][:, j0:j1, :].rearrange("p j i -> p (j i)"),
                                   second_ps[x % 2][:, 0:(j1 - j0) * 2 * P], ACT.Exp, scale=SCALE).then_inc(exp_done, 1)
                    if x == 0 and not (isinstance(n, int) and n == 0):
                        copy_u(n - 1, 1 - k, 3)
                    for q in range(3):
                        if last_of[q] + 2 == x:
                            copy_u(n, k, q)
                    for q in range(3):
                        if last_of[q] + 1 == x:
                            copy_ut(n, q)

            each_head(act, step)
            copy_ut(NARROW - 1, 3)
            copy_u(NARROW - 1, 1, 3)
            for g in range(CHUNKS):
                act.wait_ge(o_turned, g + 1)
                wait_from(act, y_done, g)
                act.copy(ot[:, :], c.bank(0)).then_inc(ot_ready, 1)

        @block.vector
        def _(dve):
            for first in (post,):
                dve.sem_inc(first, 1)
            def maxima(n, x):
                t, lo, hi = first_units[x]
                dve.wait_ge(s1_done, n * P1 + x + 1)
                if causal:
                    dve.tensor_reduce(tops[:, t, lo // BANK:lo // BANK + 1], first_ps[x % 2][:, 0:hi - lo], AX.X,
                                      ALU.max).then_inc(maxed, 1)
                else:
                    dve.tensor_reduce(tops[:, t, lo // BLK:hi // BLK], first_ps[x % 2].rearrange("p (b j) -> p b j", j=BLK),
                                      AX.X, ALU.max).then_inc(maxed, 1)

            def tops_of(n, k):
                at = n * TOP_STEPS
                dve.wait_ge(maxed, (n + 1) * P1)
                dve.tensor_reduce(top[:, :], tops[:, :, :], AX.X, ALU.max).then_inc(top_step, 1)
                dve.wait_ge(top_step, at + 1)
                if not causal:
                    own_score = diag[:, bass.ds(n, 1), :].rearrange("p o t -> p (o t)")
                    dve.tensor_tensor(top[:, :], top[:, :], own_score, ALU.max).then_inc(top_step, 1)
                    dve.wait_ge(top_step, at + 2)
                    dve.tensor_tensor(diff[k][:, :, 0:NBLK], tops[:, :, :], per_tile(top, NBLK), ALU.subtract).then_inc(top_step, 1)
                    dve.tensor_tensor(diff[k][:, :, NBLK], own_score, top[:, :], ALU.subtract).then_inc(top_step, 1)
                    flat = tops[:, :, :].rearrange("p t b -> p (t b)")
                    for s in range(2):
                        rows = slice(s * BLK, (s + 1) * BLK)
                        dve.tensor_scalar(on[k][rows, :], flat[rows, s::NBLK + 2], FAR / 2, None, ALU.is_gt).then_inc(top_step, 1)
                    at += 5
                split_in_three(dve, [top3[:, :, TOP_ROW + r] for r in range(3)], top_rest[:, :], top[:, :], top_step, at + 1)

            def rows_of(n):
                dve.wait_ge(top_turned, n + 1)
                rows = slice(TOP_ROW, TOP_ROW + 3)
                dve.tensor_scalar(q_stack[rows, bass.ds(n, 1), :].rearrange("p o i -> p (o i)"),
                                  turn_ps.bitcast(BF16)[rows, :], 1.0, None, ALU.mult).then_inc(rows_ready, 1)

            def take_v(n, k):
                wait_from(dve, av_done, (n - 1) * 4)
                dve.tensor_scalar(v_now[k][:, :, 0:cols], v[:, bass.ds(n, 1), :, :].rearrange("p o t d -> p (o t) d"),
                                  1.0, None, ALU.mult).then_inc(v_ready, 1)

            def per_tile(a, width):
                return a[:, :].rearrange("p (t o) -> p t o", o=1).to_broadcast([P, TPB, width])

            def post_a(n, k):
                at = n * POST
                wait_from(dve, post, at + 1)
                dve.wait_ge(u_copied, n * 4 + 4)
                if causal:
                    dve.tensor_reduce(total[:, :, :], u[k][:, :, :].rearrange("p t (m c) -> p t c m", c=cols), AX.X,
                                      ALU.add).then_inc(post, 1)
                    dve.wait_ge(post, at + 2)
                    dve.reciprocal(l[:, :], total[:, :, DH]).then_inc(post, 1)
                    dve.wait_ge(post, at + 3)
                    dve.tensor_tensor(o[:, bass.ds(n, 1), :, :].rearrange("p o t d -> p (o t) d"), total[:, :, 0:DH],
                                      per_tile(l, DH), ALU.mult).then_inc(post, 1)
                    return
                dve.wait_ge(near_exp, n + 1)
                dve.tensor_reduce(l[:, :], u[k][:, :, 2 * DH::cols], AX.X, ALU.add).then_inc(post, 1)
                dve.tensor_scalar(off[:, :], on[k][:, :], -1.0, 1.0, ALU.mult, ALU.add).then_inc(post, 1)
                dve.wait_ge(post, at + 3)
                dve.tensor_tensor(off[:, :], off[:, :], diff[k][:, :, NBLK], ALU.mult).then_inc(post, 1)
                dve.wait_ge(post, at + 4)
                dve.tensor_tensor(l[:, :], l[:, :], off[:, :], ALU.add).then_inc(post, 1)
                dve.wait_ge(post, at + 5)
                dve.reciprocal(l[:, :], l[:, :]).then_inc(post, 1)
                dve.wait_ge(post, at + 6)
                dve.tensor_tensor(prob[:, :, :], diff[k][:, :, 0:NBLK], per_tile(l, NBLK), ALU.mult).then_inc(post, 1)
                dve.wait_ge(post, at + 7)
                dve.tensor_scalar(big[:, :], prob[:, :, :].rearrange("p t b -> p (t b)"), threshold, None,
                                  ALU.is_gt).then_inc(post, 1)

            def post_b(n, k):
                at = n * POST + POST_A
                dve.wait_ge(counted, n + 1)
                dve.scalar_tensor_tensor(keep[:, :, :], turn_ps[:, 0:TPB * NBLK].rearrange("p (t b) -> p t b", b=NBLK), 0.5,
                                         per_tile(l, NBLK), ALU.is_gt, ALU.mult).then_inc(post, 1)
                dve.wait_ge(post, at + 2)
                flat = keep[:, :, :].rearrange("p t b -> p (t b)")
                for s in range(2):
                    rows = slice(s * BLK, (s + 1) * BLK)
                    op = dve.tensor_tensor(keep_own[rows, :], flat[rows, s::NBLK + 2], on[k][rows, :], ALU.mult)
                op.then_inc(post, 1)
                dve.wait_ge(post, at + 3)
                dve.tensor_tensor(keep_own[:, :], l[:, :], keep_own[:, :], ALU.subtract).then_inc(post, 1)
                dve.wait_ge(post, at + 4)
                dve.tensor_tensor(keep_own[:, :], keep_own[:, :], diff[k][:, :, NBLK], ALU.mult).then_inc(post, 1)
                dve.wait_ge(post, at + 5)
                for s in range(2):
                    rows = slice(s * BLK, (s + 1) * BLK)
                    mine = v[rows, bass.ds(n, 1), :, s * DH:(s + 1) * DH].rearrange("p o t d -> p (o t) d")
                    dve.tensor_tensor(own[rows, :, :], mine, keep_own[rows, :].rearrange("p (t o) -> p t o", o=1)
                                      .to_broadcast([BLK, TPB, DH]), ALU.mult).then_inc(post, 1)

            def post_c(n):
                at = n * POST + POST_A
                dve.wait_ge(kept_ready, n + 1)
                dve.tensor_reduce(total[:, :, :], kept[:, :, :, :].rearrange("p m s d -> p (m s d)").rearrange(
                    "p (t b d) -> p t d b", t=TPB, d=DH), AX.X, ALU.add).then_inc(post, 1)
                dve.wait_ge(post, at + 8)
                dve.tensor_tensor(o[:, bass.ds(n, 1), :, :].rearrange("p o t d -> p (o t) d"), total[:, :, :], own[:, :, :],
                                  ALU.add).then_inc(post, 1)

            dve.memset(top3[:, :, :], 0.0).then_inc(setup, 1)
            dve.memset(tops[:, :, :], -3e38).then_inc(setup, 1)
            if causal:
                dve.tensor_copy(masks[:, :], raw[:, :]).then_inc(setup, 1)
            else:
                dve.tensor_copy(same_block[:, :], raw[:, :]).then_inc(setup, 1)
            for k in range(2):
                dve.memset(v_now[k][:, :, :], 0.0).then_inc(setup, 1)
            if causal:
                for k in range(2):
                    dve.memset(u[k][:, :, :], 0.0)
                dve.memset(ut[0][:, :], 0.0).then_inc(setup, 1)
            else:
                dve.sem_inc(setup, 1)
            dve.wait_ge(setup, 6)
            take_v(0, 0)
            for x in range(P1):
                maxima(0, x)
            tops_of(0, 0)

            rows_of(0)

            def step(n, k, more):
                started = not (isinstance(n, int) and n == 0)
                for x in range(P1):
                    if more:
                        maxima(n + 1, x)
                    if x == 2 and more:
                        take_v(n + 1, 1 - k)
                    if x == 5 and started:
                        post_a(n - 1, 1 - k)
                    if x == 11 and started and not causal:
                        post_b(n - 1, 1 - k)
                if more:
                    tops_of(n + 1, 1 - k)
                if started and not causal:
                    post_c(n - 1)
                if more:
                    rows_of(n + 1)

            each_head(dve, step)
            post_a(NARROW - 1, 1)
            if not causal:
                post_b(NARROW - 1, 1)
                post_c(NARROW - 1)
            dve.wait_ge(post, NARROW * POST + 1)
            for b in range(BATCH):
                dve.tensor_copy(c.xt[:, b * SEQ:(b + 1) * SEQ].rearrange("p (t h d) -> p h t d", t=TPB, h=HEADS),
                                o[:, b * HEADS:(b + 1) * HEADS, :, :]).then_inc(regrouped, 1)
            for g in range(CHUNKS):
                dve.wait_ge(y_done, g + 1)
                x = c.x[:, g * TPC:(g + 1) * TPC, :].rearrange("p t d -> p (t d)")
                dve.tensor_tensor(x, x, c.bank(1), ALU.add).then_inc(added, 1)

        if not causal:
            @block.gpsimd
            def _(pool):
                def step(n, k, more):
                    if not (isinstance(n, int) and n == 0):
                        pool.wait_ge(post, (n - 1) * POST + POST_A + 8)
                    pool.wait_ge(post, n * POST + POST_A + 2)
                    pool.sem_inc(pool_held, 1)
                    every = [P, TPB * TPB, 2, DH]
                    sums = u[k][:, :, :].rearrange("p t c -> p (t c)").rearrange("p (m c) -> p m c", c=cols)[:, :, 0:2 * DH]
                    keep_wide = keep[:, :, :].rearrange("p t b -> p (t b)").rearrange("p (m s o) -> p m s o", s=2, o=1)
                    pool.tensor_tensor(kept[:, :, :, :], sums.rearrange("p m (s d) -> p m s d", s=2),
                                       keep_wide.to_broadcast(every), ALU.mult).then_inc(kept_ready, 1)

                each_head(pool, step)


class Stage:

    def __init__(self, c, ctx, name):
        self.c, self.ctx, self.name, self.loads = c, ctx, name, []

    def tile(self, what, shape, dram=None, dt=F32):
        t = self.c.sbuf(self.ctx, f"{self.name}_{what}", shape, dt)
        whole = t[tuple(slice(None) for _ in shape)]
        self.loads.append((whole, self.c.ins[what] if dram is None else dram))
        return t


def stage_l0_attn(nc, c):
    with ExitStack() as ctx:
        s = Stage(c, ctx, "lin")
        w = s.tile("l0a_w", [P, 4 * P])
        bias = s.tile("l0a_bias", [P, 4])
        w_out = s.tile("l0a_w_out", [P, P])
        b_out = s.tile("l0a_b_out", [1, P])
        gain_shift = s.tile("l0a_gain_shift", [P, 2])
        mask = s.tile("upper", [P, P])
        layer_norm(nc, c, "ln_lin1", c.x, transpose=False, loads=s.loads)
        layer_norm(nc, c, "ln_lin2", c.xn, gain=gain_shift[:, 0:1], shift=gain_shift[:, 1:2])
        linear_attention(nc, c, w, bias, w_out, b_out, mask)


def stage_l0_ffn(nc, c):
    with ExitStack() as ctx:
        s = Stage(c, ctx, "fp4")
        w = s.tile("l0f_w", [P, 2 * 3 * P + 352])
        layer_norm(nc, c, "ln_fp4", c.x, transpose=False, loads=s.loads)
        fp4_mlp(nc, c, w)


def stage_l1_attn(nc, c):
    with ExitStack() as ctx:
        s = Stage(c, ctx, "wide")
        w_out = s.tile("l1a_w_out", [P, 4, P])
        b_out = s.tile("l1a_b_out", [1, P])
        gain = s.tile("l1a_gain", [P, D])
        shift = s.tile("l1a_shift", [P, D])
        y = c.sbuf(ctx, "wide_y", [P, TILES, D])
        layer_norm(nc, c, "ln_wide", c.x, loads=s.loads)
        wide_attention(nc, c, c.ins["l1a_w"], w_out, b_out, y)
        layer_norm(nc, c, "ln_post", y, transpose=False, dst=y)
        add_normed(nc, c, y, gain, shift)


def stage_l1_ffn(nc, c):
    with ExitStack() as ctx:
        s = Stage(c, ctx, "moe1")
        gate = s.tile("l1f_gate", [P, 15])
        out_bias = s.tile("l1f_out_bias", [16, P])
        comb = c.sbuf(ctx, "moe1_comb", [P, TILES, 17])
        layer_norm(nc, c, "ln_moe1", c.x, loads=s.loads)
        route(nc, c, "route1", 15, 1, 3, 2, gate, comb)
        gated_experts(nc, c, "moe1", 17, ACT.Gelu, c.ins["l1f_weights"], comb, True, out_bias, 16)


def stage_l3_ffn(nc, c):
    with ExitStack() as ctx:
        s = Stage(c, ctx, "moe3")
        gate = s.tile("l3f_gate", [P, 8])
        comb = c.sbuf(ctx, "moe3_comb", [P, TILES, 16])
        layer_norm(nc, c, "ln_moe3", c.x, loads=s.loads)
        route(nc, c, "route3", 8, 2, 2, 0, gate, comb)
        gated_experts(nc, c, "moe3", 16, ACT.Silu, c.ins["l3f_weights"], comb, False)


def stage_l3_attn(nc, c):
    with ExitStack() as ctx:
        s = Stage(c, ctx, "rot")
        w_out = s.tile("l3a_w_out", [P, P])
        b_out = s.tile("l3a_b_out", [1, P])
        raw = s.tile("l3a_masks", [P, 5 * P])
        q_stack = c.sbuf(ctx, "rot_q_stack", [P, NARROW, SEQ], BF16)
        k_stack = c.sbuf(ctx, "rot_k_stack", [P, NARROW, SEQ], BF16)
        v = c.sbuf(ctx, "rot_v", [P, NARROW, TPB, DH + 1])
        with ExitStack() as prep:
            s.ctx = prep
            w = s.tile("l3a_w", [P, 5 * P])
            cos = s.tile("l3a_cos", [P, SEQ])
            sin = s.tile("l3a_sin", [P, SEQ])
            bias = s.tile("l3a_bias", [P, 4])
            v_bias = s.tile("l3a_v_bias", [1, P])
            layer_norm(nc, c, "ln_rot", c.x, loads=s.loads, clears=narrow_clears(k_stack, v))
            narrow_prepare(nc, c, w, (cos, sin, bias, v_bias), q_stack, k_stack, v, None)
        narrow_attention(nc, c, True, q_stack, k_stack, v, None, raw, w_out, b_out)


def stage_l2_attn(nc, c):
    with ExitStack() as ctx:
        s = Stage(c, ctx, "blk")
        w_out = s.tile("l2a_w_out", [P, P])
        raw = s.tile("l2a_same", [P, P])
        q_stack = c.sbuf(ctx, "blk_q_stack", [P, NARROW, SEQ], BF16)
        k_stack = c.sbuf(ctx, "blk_k_stack", [P, NARROW, SEQ], BF16)
        v = c.sbuf(ctx, "blk_v", [P, NARROW, TPB, 2 * DH + 1])
        diag = c.sbuf(ctx, "blk_diag", [P, NARROW, TPB])
        with ExitStack() as prep:
            s.ctx = prep
            w = s.tile("l2a_w", [P, 3 * P])
            layer_norm(nc, c, "ln_blk", c.x, loads=s.loads, clears=narrow_clears(k_stack, v))
            narrow_prepare(nc, c, w, None, q_stack, k_stack, v, diag)
        narrow_attention(nc, c, False, q_stack, k_stack, v, diag, raw, w_out, None)


def stage_l2_ffn(nc, c):
    with ExitStack() as ctx:
        s = Stage(c, ctx, "mlp2")
        w1 = s.tile("l2f_w1", [P, 512])
        w2 = s.tile("l2f_w2", [P, 4, P])
        b1 = s.tile("l2f_b1", [P, 4])
        b2 = s.tile("l2f_b2", [1, P])
        layer_norm(nc, c, "ln_mlp2", c.x, loads=s.loads)
        ternary_mlp(nc, c, w1, w2, b1, b2)


def packs(i):
    cat, asc = np.concatenate, np.ascontiguousarray
    o = {"x": i["L0_attn_x"].reshape(TOKENS, D), "ident": np.eye(P, dtype=np.float32)}

    q, k, v = np.split(i["L0_attn_w_qkv"], 3, axis=1)
    bq, bk, bv = np.split(i["L0_attn_b_qkv"], 3)
    o["l0a_w"] = cat([i["L0_attn_w_gate"], k, q, v], axis=1)
    o["l0a_bias"] = np.stack([i["L0_attn_b_gate"], bk, bq, bv], axis=1)
    o["l0a_w_out"] = i["L0_attn_w_proj"]
    o["l0a_b_out"] = i["L0_attn_b_proj"][None]
    o["l0a_gain_shift"] = np.stack([i["L0_attn_ln_g"], i["L0_attn_ln_b"]], axis=1)
    o["upper"] = np.triu(np.ones((P, P), np.float32))

    pad = np.zeros((3 * P - 352, D), np.float32)
    o["l0f_w"] = cat([cat([i[n], pad]).reshape(3, P, D).transpose(1, 0, 2).reshape(P, 3 * D)
                      for n in ("L0_ffn_w_gate", "L0_ffn_w_up")] + [i["L0_ffn_w_down"]], axis=1)

    qk = i["L1_attn_W_qk"].reshape(D, 4, 2 * 64, 2)
    bqk = i["L1_attn_b_qk"].reshape(4, 2 * 64, 2)
    wv, bv = i["L1_attn_W_v"].reshape(D, 4, P), i["L1_attn_b_v"].reshape(4, P)
    o["l1a_w"] = np.stack([cat([qk[:, k, :, 0], qk[:, k, :, 1], wv[:, k], bqk[k], bv[k][:, None]], axis=1)
                           for k in range(4)])
    o["l1a_w_out"] = i["L1_attn_W_out"].reshape(4, P, D).transpose(1, 0, 2)
    o["l1a_b_out"] = i["L1_attn_b_out"][None]
    o["l1a_gain"] = np.broadcast_to(i["L1_attn_ln_gamma"], (P, D))
    o["l1a_shift"] = np.broadcast_to(i["L1_attn_ln_beta"], (P, D))

    fc1, fc2, s1, s2 = i["L1_ffn_fc1_w"], i["L1_ffn_fc2_w"], i["L1_ffn_s_fc1_w"], i["L1_ffn_s_fc2_w"]
    packed = [cat([fc1[e, P:].T, fc1[e, :P].T, fc2[e].T], axis=1) for e in range(15)]
    packed += [cat([s1[2 * P + k * P:3 * P + k * P].T, s1[k * P:(k + 1) * P].T, s2[:, k * P:(k + 1) * P].T], axis=1)
               for k in range(2)]
    b, sb_, m, sm = i["L1_ffn_fc1_b"], i["L1_ffn_s_fc1_b"], i["L1_ffn_geglu_mult"], i["L1_ffn_s_geglu_mult"]
    rows = [np.stack([b[e, P:], b[e, :P], m[e]], axis=1) for e in range(15)]
    rows += [np.stack([sb_[2 * P + k * P:3 * P + k * P], sb_[k * P:(k + 1) * P], sm[k * P:(k + 1) * P]], axis=1)
             for k in range(2)]
    o["l1f_weights"] = np.stack([cat([w, r], axis=1) for w, r in zip(packed, rows)])
    o["l1f_gate"] = i["L1_ffn_gate_w"].T
    o["l1f_out_bias"] = cat([i["L1_ffn_fc2_b"], i["L1_ffn_s_fc2_b"][None]], axis=0)

    o["l2a_w"] = cat([i["L2_attn_" + n].T for n in ("wq", "wk", "wv")], axis=1)
    o["l2a_w_out"] = i["L2_attn_wo"].T
    tok, feat = np.arange(SEQ), np.arange(P)
    o["l2a_onehot"] = (np.arange(NBLK)[:, None] == tok // BLK).astype(np.float32)
    o["l2a_headsel"] = (feat[:, None] // DH == np.arange(HEADS)).astype(np.float32)
    o["l2a_same"] = (feat[:, None] // BLK == feat // BLK).astype(np.float32)

    swap = feat ^ 1
    wq, wk, bq, bk = (i["L3_attn_" + n] for n in ("Wq", "Wk", "bq", "bk"))
    o["l3a_w"] = cat([wq.T, wq[swap].T, wk.T, wk[swap].T, i["L3_attn_Wv"].T], axis=1)
    o["l3a_bias"] = np.stack([bq, bq[swap], bk, bk[swap]], axis=1)
    o["l3a_v_bias"] = i["L3_attn_bv"][None]
    o["l3a_w_out"] = i["L3_attn_Wp"].T
    o["l3a_b_out"] = i["L3_attn_bp"][None]
    theta = np.array([10.0 ** k for k in range(DH // 2)], np.float32)
    angle = (theta[feat % DH // 2][:, None] * tok.astype(np.float32)).astype(np.float64)
    o["l3a_cos"] = np.cos(angle).astype(np.float32)
    o["l3a_sin"] = (np.where(feat % 2, 1.0, -1.0)[:, None] * np.sin(angle)).astype(np.float32)
    after = np.where(feat > feat[:, None], FAR, 0.0)
    before = after.T
    o["l3a_masks"] = cat([after, before, 0 * after, 0 * after + FAR, before], axis=1).astype(np.float32)

    w0, w1, wo = i["L3_ffn_w0_kernel"], i["L3_ffn_w1_kernel"], i["L3_ffn_wo_kernel"]
    o["l3f_weights"] = np.stack([cat([w0[e][:, k * P:(k + 1) * P], w1[e][:, k * P:(k + 1) * P],
                                      wo[e][k * P:(k + 1) * P]], axis=1) for e in range(8) for k in range(2)])
    o["l3f_gate"] = i["L3_ffn_gate_kernel"]

    o["l2f_w1"] = i["L2_ffn_W1"].T
    o["l2f_w2"] = i["L2_ffn_W2"].T.reshape(4, P, D).transpose(1, 0, 2)
    o["l2f_b1"] = i["L2_ffn_b1"].reshape(4, P).T
    o["l2f_b2"] = i["L2_ffn_b2"][None]
    return {k: asc(v) for k, v in o.items()}


def layers(nc, ins, out):
    with ExitStack() as ctx:
        c = Chip(nc, ctx, ins, out)
        start(nc, c)
        stage_l0_attn(nc, c)
        stage_l0_ffn(nc, c)
        stage_l1_attn(nc, c)
        stage_l1_ffn(nc, c)
        c.clear_semaphores()
        stage_l2_attn(nc, c)
        stage_l2_ffn(nc, c)
        stage_l3_attn(nc, c)
        stage_l3_ffn(nc, c)
        finish(nc, c)


def kernel(**inputs):
    import concourse.bacc as bacc
    from concourse.bass_utils import run_bass_kernel_spmd as run

    nc = bacc.Bacc("TRN2", target_bir_lowering=False, num_devices=1)
    laid_out = packs({name: np.asarray(a) for name, a in inputs.items()})
    arrays = {f"in_{name}_dram": a for name, a in laid_out.items()}
    ins = {name: nc.dram_tensor(f"in_{name}_dram", a.shape, mybir.dt.from_np(a.dtype), kind="ExternalInput").ap()
           for name, a in laid_out.items()}
    out = nc.dram_tensor("out_dram", (TOKENS, D), F32, kind="ExternalOutput").ap()
    layers(nc, ins, out)
    r = run(nc, [arrays], core_ids=[0])
    return r.results[0]["out_dram"].reshape(BATCH, SEQ, D)
```
